# Optimizing a Trainium2 kernel written in Bass

```python
import numpy as np
import jax
import jax.numpy as jnp

def _softmax(x, axis=-1):
    return jax.nn.softmax(x, axis=axis)

def _gelu(x):
    return jax.nn.gelu(x, approximate=True)

def _silu(x):
    return jax.nn.silu(x)

def _sigmoid(x):
    return jax.nn.sigmoid(x)

def _layernorm(x, axis=-1, eps=1e-05):
    m = jnp.mean(x, axis=axis, keepdims=True)
    v = jnp.var(x, axis=axis, keepdims=True)
    return (x - m) / jnp.sqrt(v + eps)

def _scatter_add(tgt, idx, src, axis=0):
    return tgt.at[idx].add(src)

def _segment_sum(src, seg, n):
    return jax.ops.segment_sum(src, seg, n)
kernel_name = 'mk_gps_d1_gnn_r8_b7d7e5'

def setup_inputs(seed: int=0):
    np.random.seed(seed)
    _w = jnp.asarray

    def _rec_inputs():
        import jax
        import jax.numpy as jnp
        _gk = jax.random.key(seed)
        x = -0.0002117 + 1 * jax.random.normal(jax.random.fold_in(_gk, 1), (6250, 512), jnp.float32)
        src = jax.random.randint(jax.random.fold_in(_gk, 2), (100000,), 0, 6250, jnp.int32)
        dst = jnp.minimum((6250 * jax.random.uniform(jax.random.fold_in(_gk, 3), (100000,)) ** 2.0).astype(jnp.int32), 49999)
        _o = jnp.argsort(dst, stable=True)
        src = src[_o]
        dst = dst[_o]
        return (x, src, dst)
    x, src, dst = _rec_inputs()

    def _L0_gnn_setup():
        import jax, jax.numpy as jnp
        import numpy as np
        N_NODES = 6250
        EMBED_DIM = 512
        N_EDGES = 100000
        NEG_SLOPE = 0.01
        key = jax.random.key(seed)
        k1, k2, k3 = jax.random.split(key, 3)
        X = jax.random.normal(k1, (N_NODES, EMBED_DIM), dtype=jnp.float32)
        W = jax.random.normal(k2, (EMBED_DIM, EMBED_DIM), dtype=jnp.float32) / np.sqrt(EMBED_DIM)
        b = jnp.zeros((EMBED_DIM,), dtype=jnp.float32)
        edge_index = jax.random.randint(k3, (2, N_EDGES), 0, N_NODES, dtype=jnp.int32)
        return {'X': X, 'W': W, 'b': b, 'edge_index': edge_index}
    _L0_gnn_all = _L0_gnn_setup()
    _L0_gnn_in = {k: v for k, v in _L0_gnn_all.items() if k in ('W', 'b')}
    del _L0_gnn_all

    def _L0_mix_setup():
        import jax, jax.numpy as jnp
        import numpy as np
        NUM_HEADS = 16
        EPS = 1e-15
        key = jax.random.key(seed)
        k1, k2, k3, k4 = jax.random.split(key, 4)
        B, N, C = (4, 2048, 512)
        x = jax.random.normal(k1, (B, N, C), dtype=jnp.float32)
        qkv_weight = jax.random.normal(k2, (3 * C, C), dtype=jnp.float32) * 0.02
        proj_weight = jax.random.normal(k3, (C, C), dtype=jnp.float32) * 0.02
        proj_bias = jax.random.normal(k4, (C,), dtype=jnp.float32) * 0.02
        return {'x': x, 'qkv_weight': qkv_weight, 'proj_weight': proj_weight, 'proj_bias': proj_bias}
    _L0_mix_all = _L0_mix_setup()
    _L0_mix_in = {k: v for k, v in _L0_mix_all.items() if k in ('qkv_weight', 'proj_weight', 'proj_bias')}
    del _L0_mix_all

    def _L0_ffn_setup():
        import jax, jax.numpy as jnp
        import numpy as np
        D_MODEL = 512
        D_FF = 256
        NUM_EXPERTS = 8
        TOP_K = 2
        key = jax.random.key(seed)
        k_x, k_g, k_w1, k_w2 = jax.random.split(key, 4)
        x = jax.random.normal(k_x, (8, 512, D_MODEL), dtype=jnp.float32)
        Wg = jax.random.normal(k_g, (D_MODEL, NUM_EXPERTS), dtype=jnp.float32) * (1.0 / np.sqrt(D_MODEL))
        W1 = jax.random.normal(k_w1, (NUM_EXPERTS, D_MODEL, D_FF), dtype=jnp.float32) * (1.0 / np.sqrt(D_MODEL))
        W2 = jax.random.normal(k_w2, (NUM_EXPERTS, D_FF, D_MODEL), dtype=jnp.float32) * (1.0 / np.sqrt(D_FF))
        return {'x': x, 'Wg': Wg, 'W1': W1, 'W2': W2}
    _L0_ffn_all = _L0_ffn_setup()
    _L0_ffn_in = {k: v for k, v in _L0_ffn_all.items() if k in ('Wg', 'W1', 'W2')}
    del _L0_ffn_all
    return {'x': x, 'src': src, 'dst': dst, 'L0_gnn_W': _L0_gnn_in['W'], 'L0_gnn_b': _L0_gnn_in['b'], 'L0_mix_qkv_weight': _L0_mix_in['qkv_weight'], 'L0_mix_proj_weight': _L0_mix_in['proj_weight'], 'L0_mix_proj_bias': _L0_mix_in['proj_bias'], 'L0_ffn_Wg': _L0_ffn_in['Wg'], 'L0_ffn_W1': _L0_ffn_in['W1'], 'L0_ffn_W2': _L0_ffn_in['W2']}

def reference(x, src, dst, L0_gnn_W, L0_gnn_b, L0_mix_qkv_weight, L0_mix_proj_weight, L0_mix_proj_bias, L0_ffn_Wg, L0_ffn_W1, L0_ffn_W2):
    import jax
    import jax.numpy as jnp

    def _L0_gnn_ref(X, W, b, edge_index):
        import jax, jax.numpy as jnp
        import numpy as np
        N_NODES = 6250
        EMBED_DIM = 512
        N_EDGES = 100000
        NEG_SLOPE = 0.01
        N = X.shape[0]
        loop = jnp.arange(N, dtype=edge_index.dtype)
        src = jnp.concatenate([edge_index[0], loop])
        dst = jnp.concatenate([edge_index[1], loop])
        deg = jax.ops.segment_sum(jnp.ones_like(dst, dtype=X.dtype), dst, num_segments=N)
        dinv = jnp.where(deg > 0, jax.lax.rsqrt(deg), 0.0)
        norm = dinv[src] * dinv[dst]
        H = X @ W
        msgs = H[src] * norm[:, None]
        out = jax.ops.segment_sum(msgs, dst, num_segments=N) + b
        return jnp.where(out >= 0, out, NEG_SLOPE * out)

    def _L0_mix_ref(x, qkv_weight, proj_weight, proj_bias):
        import jax, jax.numpy as jnp
        import numpy as np
        NUM_HEADS = 16
        EPS = 1e-15
        B, N, C = x.shape
        H = NUM_HEADS
        D = C // H
        qkv = (x @ qkv_weight.T).reshape(B, N, 3, C)
        q = jax.nn.relu(qkv[:, :, 0]).reshape(B, N, H, D)
        k = jax.nn.relu(qkv[:, :, 1]).reshape(B, N, H, D)
        v = qkv[:, :, 2].reshape(B, N, H, D)
        qf = q.astype(jnp.float32)
        kf = k.astype(jnp.float32)
        vf = v.astype(jnp.float32)
        v_pad = jnp.concatenate([vf, jnp.ones_like(vf[..., :1])], axis=-1)
        vk = jnp.einsum('bnhc,bnhd->bhcd', v_pad, kf)
        vk_q = jnp.einsum('bnhd,bhcd->bnhc', qf, vk)
        proj_input = (vk_q[..., :-1] / (vk_q[..., -1:] + EPS)).astype(x.dtype).reshape(B, N, C)
        return proj_input @ proj_weight.T + proj_bias

    def _L0_ffn_ref(x, Wg, W1, W2):
        import jax, jax.numpy as jnp
        import numpy as np
        D_MODEL = 512
        D_FF = 256
        NUM_EXPERTS = 8
        TOP_K = 2
        B, S, D = x.shape
        E = Wg.shape[-1]
        router_logits = jnp.einsum('bsd,de->bse', x, Wg)
        top_logits, top_idx = jax.lax.top_k(router_logits, TOP_K)
        top_w = jax.nn.softmax(top_logits, axis=-1)
        combine = jnp.sum(jax.nn.one_hot(top_idx, E, dtype=x.dtype) * top_w[..., None], axis=-2)
        xt = x.reshape(B * S, D)
        cw = combine.reshape(B * S, E)
        out = jnp.zeros_like(xt)
        for e in range(E):
            h = jax.nn.silu(xt @ W1[e]) @ W2[e]
            out = out + cw[:, e:e + 1] * h
        return out.reshape(B, S, D)
    edge_index = jnp.stack([src, dst])
    xn = _layernorm(x, axis=-1)
    x = x + _L0_gnn_ref(xn, L0_gnn_W, L0_gnn_b, edge_index) + _L0_mix_ref(xn[None], L0_mix_qkv_weight, L0_mix_proj_weight, L0_mix_proj_bias)[0]
    x = x + _L0_ffn_ref(_layernorm(x, axis=-1)[None], L0_ffn_Wg, L0_ffn_W1, L0_ffn_W2)[0]
    return x

_drawn_inputs = setup_inputs


def setup_inputs(seed=0):
    import zlib

    import numpy as np

    out = dict(_drawn_inputs(seed))
    spreads = {'L0_gnn_b': (0.0, 0.1)}
    factors = {'L0_mix_qkv_weight': 2.813, 'L0_mix_proj_weight': 2.827}
    for name, (base, spread) in spreads.items():
        noise = np.random.default_rng([zlib.crc32(name.encode()), seed]).standard_normal(out[name].shape)
        drawn = base * np.exp(spread * noise) if base else spread * noise
        out[name] = jnp.asarray(drawn.astype(out[name].dtype))
    for name, factor in factors.items():
        out[name] = (out[name] * factor).astype(out[name].dtype)
    return out
```

```python
from contextlib import ExitStack

import concourse.bass as bass
from concourse import mybir

F32 = mybir.dt.float32
F32R = mybir.dt.float32r
F16 = mybir.dt.float16
BF16 = mybir.dt.bfloat16
I32 = mybir.dt.int32
U32 = mybir.dt.uint32
ALU = mybir.AluOpType
ACT = mybir.ActivationFunctionType
AX_X = mybir.AxisListType.X

P = 128
N, D = 6250, 512
E = 100000
H, DH = 16, 32
NEXP, FF = 8, 256
C = D // P
NT = -(-N // P)
LAST = N - (NT - 1) * P
ET = 16 * NT
GE = 4
NG = ET // GE
GPT = NG // NT
ROWT = 8
ER = ET // ROWT
EFULL = E // (ROWT * P)
EREST = E - EFULL * ROWT * P
PAD_DST = 8191
NWB = 3 * D // P
LN_EPS = 1e-5
DIV_EPS = 1e-15
SLOPE = 0.01
TABLE_SCALE = 1024.0
assert ET * P >= E and ER <= P and NT % 2 == 1 and GPT == 4 and EREST > 0


def node_tiles(eng, body):
    with eng.Fori(0, NT // 2) as j:
        body(2 * j, 0, j)
        body(2 * j + 1, 1, j)
    body(NT - 1, 0, NT // 2)


def node_tiles_ahead(eng, start, finish):
    start(0, 0)
    with eng.Fori(0, NT // 2) as j:
        start(2 * j + 1, 1)
        finish(2 * j, 0)
        start(2 * j + 2, 0)
        finish(2 * j + 1, 1)
    finish(NT - 1, 0)


def rows_of(t):
    return LAST if isinstance(t, int) and t == NT - 1 else P


def turn(pe, out, rows, ident):
    for c in range(C):
        last = pe.transpose(out[:, c * P:(c + 1) * P], rows[:, c * P:(c + 1) * P], ident)
    return last


def product(pe, out, left, right, first=True, final=True):
    for c in range(C):
        for a, b in ((1, 0), (0, 1), (0, 0)):
            last = pe.matmul(out, left[a][:, c, :], right[b][:, c, :],
                             start=first and c == 0 and a == 1, stop=final and c == C - 1 and a + b == 0)
    return last


def mix(nc, sb_in, ps_in, sem, turns, settle, acc, k_sum, kv, ident, ones, dinv_down, x, q_rows, x2_rows,
        w_gnn, b_gnn, w_proj, b_proj):
    scope = ExitStack()
    with scope:
        sb, ps = sb_in(scope), ps_in(scope)
        proj_rows = sb("proj_rows", [P, C, D], F32)
        proj_t = sb("proj_t", [P, C, D], F32)
        gnn_raw = sb("gnn_raw", [P, C, D], F32)
        gnn_w = [sb(f"gnn_w_{n}", [P, C, D], F32R) for n in ("hi", "lo")]
        mixer = [sb(f"mixer_{n}", [P, C, D], F32R) for n in ("hi", "lo")]
        kv_heads = sb("kv_heads", [P, C, P], F32)
        k_all = sb("k_all", [P, D], F32)
        b_gnn_rows, b_proj_rows = sb("b_gnn_rows", [P, D], F32), sb("b_proj_rows", [P, D], F32)
        x_rows = [sb(f"x_rows_c{b}", [P, D], F32) for b in (0, 1)]
        q = [sb(f"q_c{b}", [P, D], F32) for b in (0, 1)]
        qk = sb("qk", [P, D], F32)
        den, den_eps, den_inv = (sb(n, [P, H], F32) for n in ("den", "den_eps", "den_inv"))
        a_rows = sb("a_rows", [P, D], F32)
        q_t = [[sb(f"q_t{b}{n}", [P, C, P], F32R) for n in ("hi", "lo")] for b in (0, 1)]
        a_t = [[sb(f"a_t{b}{n}", [P, C, P], F32R) for n in ("hi", "lo")] for b in (0, 1)]
        h, g = sb("h", [P, D], F32), sb("g", [P, D], F32)
        x2 = [sb(f"x2_{b}", [P, D], F32) for b in (0, 1)]
        ps_q, ps_a = ps("ps_q_turned", [P, 512]), ps("ps_a_turned", [P, 512])
        ps_mix = [ps(f"ps_mix{b}", [P, 512]) for b in (0, 1)]
        ps_gnn = [ps(f"ps_gnn{b}", [P, 512]) for b in (0, 1)]

        proj_loaded, gnn_loaded, biases_loaded = sem("proj_loaded"), sem("gnn_loaded"), sem("biases_loaded")
        proj_turned, proj_copied = sem("proj_turned"), sem("proj_copied")
        heads_zeroed, heads_set, k_all_summed, k_all_set = (
            sem(n) for n in ("heads_zeroed", "heads_set", "k_all_summed", "k_all_set"))
        mixer_summed, mixer_hi_set, mixer_lo_set = sem("mixer_summed"), sem("mixer_hi_set"), sem("mixer_lo_set")
        gnn_hi_set, gnn_lo_set = sem("gnn_hi_set"), sem("gnn_lo_set")
        x_loaded = [sem(f"x_loaded_c{b}") for b in (0, 1)]
        q_loaded = [sem(f"q_loaded_c{b}") for b in (0, 1)]
        rows_used = sem("rows_used_c")
        qk_set, x_biased, q_divided, a_set = sem("qk_set"), sem("x_biased"), sem("q_divided"), sem("a_set")
        den_step = sem("den_step")
        turned, hi_set, lo_set = sem("turned_c"), sem("hi_set_c"), sem("lo_set_c")
        mixed, gnn_done, h_step, x2_set = sem("mixed"), sem("gnn_done"), sem("h_step"), sem("x2_set")
        x2_stored = [sem(f"x2_stored{b}") for b in (0, 1)]

        with nc.Block() as block:

            @block.sync
            def _(sp):
                sp.dma_start(proj_rows[:, :, :], w_proj.rearrange("(r p) d -> p r d", p=P)).then_inc(proj_loaded, 16)
                sp.dma_start(gnn_raw[:, :, :], w_gnn.rearrange("(c p) d -> p c d", p=P)).then_inc(gnn_loaded, 16)
                for rows, bias in ((b_gnn_rows, b_gnn), (b_proj_rows, b_proj)):
                    sp.dma_start(rows[:, :], bias.rearrange("(a d) -> a d", a=1).broadcast_to([P, D])
                                 ).then_inc(biases_loaded, 16)

                def load(t, b, j):
                    sp.wait_ge(rows_used, t + 1)
                    r = rows_of(t)
                    sp.dma_start(q[b][:, :], q_rows[bass.ds(t * P, P), :]).then_inc(q_loaded[b], 16)
                    sp.dma_start(x_rows[b][0:r, :], x[bass.ds(t * P, r), :]).then_inc(x_loaded[b], 16)

                node_tiles(sp, load)

            @block.gpsimd
            def _(pool):
                pool.memset(kv_heads[:, :, :], 0.0).then_inc(heads_zeroed, 1)
                pool.wait_ge(k_all_set, 1)
                pool.wait_ge(biases_loaded, 32)

                def tile(t, b, j):
                    pool.wait_ge(q_loaded[b], 16 * j + 16)
                    pool.wait_ge(den_step, 3 * t + 1)
                    settle(pool, "pool")
                    pool.tensor_tensor(qk[:, :], q[b][:, :], k_all[:, :], ALU.mult).then_inc(qk_set, 1)
                    pool.wait_ge(x_loaded[b], 16 * j + 16)
                    settle(pool, "pool")
                    pool.tensor_tensor(x_rows[b][:, :], x_rows[b][:, :], b_proj_rows[:, :], ALU.add
                                       ).then_inc(x_biased, 1)

                node_tiles(pool, tile)

            @block.tensor
            def _(pe):
                pe.matmul(ps_a[:, :], ones[:, :], k_sum[:, :], start=True, stop=True).then_inc(k_all_summed, 1)
                pe.wait_ge(proj_loaded, 16)
                for r in range(C):
                    pe.wait_ge(proj_copied, r) if r else None
                    turn(pe, ps_q, proj_rows[:, r, :], ident[:, :]).then_inc(proj_turned, 1)
                pe.wait_ge(heads_set, 1)
                pe.wait_ge(proj_copied, C)
                for c in range(C):
                    if c >= 2:
                        pe.wait_ge(mixer_lo_set, c - 1)
                    pe.matmul(ps_mix[c % 2][:, :], kv_heads[:, c, :], proj_t[:, c, :], start=True, stop=True
                              ).then_inc(mixer_summed, 1)
                pe.wait_ge(mixer_lo_set, C)
                pe.wait_ge(gnn_lo_set, 1)
                pe.wait_ge(k_all_set, 1)

                def start(t, b):
                    pe.wait_ge(q_divided, t + 1)
                    pe.wait_ge(lo_set, 2 * t + 1)
                    turn(pe, ps_q, q[b], ident[:, :]).then_inc(turned, 1)
                    pe.wait_ge(a_set, t + 1)
                    turn(pe, ps_a, a_rows, ident[:, :]).then_inc(turned, 1)

                def finish(t, b):
                    pe.wait_ge(lo_set, 2 * t + 2)
                    product(pe, ps_mix[b][:, :], q_t[b], mixer).then_inc(mixed, 1)
                    pe.wait_ge(lo_set, 2 * t + 3)
                    product(pe, ps_gnn[b][:, :], a_t[b], gnn_w).then_inc(gnn_done, 1)

                node_tiles_ahead(pe, start, finish)

            @block.scalar
            def _(act):
                act.sem_inc(x2_stored[0], 16)
                act.sem_inc(x2_stored[1], 16)
                act.wait_ge(gnn_loaded, 16)
                act.copy(gnn_w[0][:, :, :], gnn_raw[:, :, :]).then_inc(gnn_hi_set, 1)
                for c in range(C):
                    act.wait_ge(mixer_summed, c + 1)
                    act.copy(mixer[0][:, c, :], ps_mix[c % 2][:, :]).then_inc(mixer_hi_set, 1)

                def start(t, b):
                    if not (isinstance(t, int) and t == 0):
                        act.wait_ge(turned, 2 * t)
                        settle(act, "act")
                    act.activation(a_rows[:, :], acc[:, t, :], ACT.Copy, scale=dinv_down[:, bass.ds(t, 1)]
                                   ).then_inc(a_set, 1)
                    act.wait_ge(turned, 2 * t + 1)
                    act.copy(q_t[b][0][:, :, :].rearrange("p c n -> p (c n)"), ps_q[:, :]).then_inc(hi_set, 1)
                    act.wait_ge(turned, 2 * t + 2)
                    act.copy(a_t[b][0][:, :, :].rearrange("p c n -> p (c n)"), ps_a[:, :]).then_inc(hi_set, 1)

                def finish(t, b):
                    act.wait_ge(x2_set, t + 1)
                    act.dma_start(x2_rows[bass.ds(t * P, P), :], x2[b][:, :]).then_inc(x2_stored[b], 16)

                node_tiles_ahead(act, start, finish)
                act.wait_ge(x2_stored[0], 16 * (NT // 2 + 2))
                act.wait_ge(x2_stored[1], 16 * (NT // 2 + 1))

            @block.vector
            def _(dve):
                dve.sem_inc(rows_used, 2)
                dve.sem_inc(lo_set, 1)
                dve.sem_inc(den_step, 1)
                dve.wait_ge(k_all_summed, 1)
                dve.tensor_copy(k_all[:, :], ps_a[:, :]).then_inc(k_all_set, 1)
                dve.wait_ge(heads_zeroed, 1)
                for c in range(C):
                    for n in range(P // DH):
                        rows, cols = slice(n * DH, (n + 1) * DH), slice(c * P + n * DH, c * P + (n + 1) * DH)
                        last = dve.tensor_copy(kv_heads[rows, c, rows], kv[rows, cols])
                last.then_inc(heads_set, 1)
                for r in range(C):
                    dve.wait_ge(proj_turned, r + 1)
                    dve.tensor_copy(proj_t[:, :, r * P:(r + 1) * P], ps_q[:, :].rearrange("p (c o) -> p c o", c=C)
                                    ).then_inc(proj_copied, 1)
                dve.wait_ge(gnn_hi_set, 1)
                dve.tensor_tensor(gnn_w[1][:, :, :], gnn_raw[:, :, :], gnn_w[0][:, :, :].bitcast(F32), ALU.subtract
                                  ).then_inc(gnn_lo_set, 1)
                for c in range(C):
                    dve.wait_ge(mixer_hi_set, c + 1)
                    dve.tensor_tensor(mixer[1][:, c, :], ps_mix[c % 2][:, :], mixer[0][:, c, :].bitcast(F32),
                                      ALU.subtract).then_inc(mixer_lo_set, 1)
                dve.wait_ge(biases_loaded, 32)

                def start(t, b):
                    dve.wait_ge(qk_set, t + 1)
                    dve.tensor_reduce(den[:, :], qk[:, :].rearrange("p (h d) -> p h d", h=H), AX_X, ALU.add
                                      ).then_inc(den_step, 1)
                    dve.wait_ge(den_step, 3 * t + 2)
                    dve.tensor_scalar(den_eps[:, :], den[:, :], DIV_EPS, None, ALU.add).then_inc(den_step, 1)
                    dve.wait_ge(den_step, 3 * t + 3)
                    dve.reciprocal(den_inv[:, :], den_eps[:, :]).then_inc(den_step, 1)
                    dve.wait_ge(den_step, 3 * t + 4)
                    dve.tensor_tensor(q[b][:, :].rearrange("p (h d) -> p h d", h=H),
                                      q[b][:, :].rearrange("p (h d) -> p h d", h=H),
                                      den_inv[:, :].rearrange("p (h a) -> p h a", a=1).broadcast_to([P, H, DH]),
                                      ALU.mult).then_inc(q_divided, 1)
                    for n, (banked, parts) in enumerate(((ps_q, q_t[b]), (ps_a, a_t[b]))):
                        dve.wait_ge(hi_set, 2 * t + n + 1)
                        dve.tensor_tensor(parts[1][:, :, :].rearrange("p c n -> p (c n)"), banked[:, :],
                                          parts[0][:, :, :].bitcast(F32).rearrange("p c n -> p (c n)"), ALU.subtract
                                          ).then_inc(lo_set, 1)

                def finish(t, b):
                    dve.wait_ge(mixed, t + 1)
                    dve.wait_ge(x_biased, t + 1)
                    dve.tensor_tensor(x_rows[b][:, :], x_rows[b][:, :], ps_mix[b][:, :], ALU.add).then_inc(h_step, 1)
                    dve.wait_ge(gnn_done, t + 1)
                    dve.tensor_tensor(h[:, :], ps_gnn[b][:, :], b_gnn_rows[:, :], ALU.add).then_inc(h_step, 1)
                    dve.wait_ge(h_step, 3 * t + 2)
                    dve.scalar_tensor_tensor(g[:, :], h[:, :], SLOPE, h[:, :], ALU.mult, ALU.max).then_inc(h_step, 1)
                    dve.wait_ge(h_step, 3 * t + 3)
                    dve.wait_ge(x2_stored[b], (t - b) * 8 + 16)
                    dve.tensor_tensor(x2[b][:, :], x_rows[b][:, :], g[:, :], ALU.add).then_inc(x2_set, 1)
                    dve.wait_ge(x2_set, t + 1)
                    dve.sem_inc(rows_used, 1)

                node_tiles_ahead(dve, start, finish)


def experts(nc, sb_in, ps_in, sem, turns, settle, ident, x2_rows, w_gate, w1, w2, out):
    steps, width = NEXP * FF // D, D
    scope = ExitStack()
    with scope:
        sb, ps = sb_in(scope), ps_in(scope)
        w1_t = [sb(f"w1_{n}", [P, C, NEXP * FF], F32R) for n in ("hi", "lo")]
        w2_t = [sb(f"w2_{n}", [P, steps * C, D], F32R) for n in ("hi", "lo")]
        gate_raw = sb("gate_raw", [P, C, NEXP], F32)
        gate = [sb(f"gate_{n}", [P, C, NEXP], F32R) for n in ("hi", "lo")]
        raw = [sb(f"w_raw{b}", [P, 2 * D], F32) for b in (0, 1)]
        expert_no = sb("expert_no", [P, NEXP], F32)
        x2 = [sb(f"x2_d{b}", [P, D], F32) for b in (0, 1)]
        stats, moments = sb("stats_d", [P, 6], F32), sb("moments_d", [P, 2], F32)
        var_eps, rstd, minus_half = (sb(n, [P, 1], F32) for n in ("var_eps_d", "rstd_d", "minus_half_d"))
        xn = sb("xn_d", [P, D], F32)
        xn_t = [sb(f"xn_t_d{n}", [P, C, P], F32R) for n in ("hi", "lo")]
        logits, top, top_no_f = (sb(n, [P, NEXP], F32) for n in ("logits", "top", "top_no_f"))
        top_no = sb("top_no", [P, NEXP], U32)
        gap, squashed = sb("gap", [P, 1], F32), sb("squashed", [P, 1], F32)
        top_w = sb("top_w", [P, 2], F32)
        picked = [sb(f"picked{n}", [P, NEXP], F32) for n in (0, 1)]
        weight = [sb(f"weight{b}", [P, NEXP], F32) for b in (0, 1)]
        s = [sb(f"s{n}", [P, D], F32) for n in (0, 1)]
        s_t = [sb(f"s_t{n}", [P, C, P], F32R) for n in ("hi", "lo")]
        out_rows = [sb(f"out_rows{b}", [P, D], F32) for b in (0, 1)]
        ps_x, ps_s = ps("ps_x_turned", [P, 512]), ps("ps_s_turned", [P, 512])
        ps_h = [ps(f"ps_h{n}", [P, 512]) for n in (0, 1)]
        ps_out = ps("ps_out", [P, 512])
        ps_gate = ps("ps_gate", [P, 512])

        raw_loaded = [sem(f"raw_loaded{b}") for b in (0, 1)]
        gate_loaded, const_set, split_hi, split_lo = (sem(n) for n in ("gate_loaded", "const_set_d", "split_hi", "split_lo"))
        x2_loaded = [sem(f"x2_loaded{b}") for b in (0, 1)]
        x2_used = sem("x2_used")
        ln_step, root_set, xn_set = sem("ln_step_d"), sem("root_set_d"), sem("xn_set_d")
        x_turned, x_hi_set, x_lo_set = sem("x_turned_d"), sem("x_hi_set_d"), sem("x_lo_set_d")
        gated, gate_step, gap_set, squashed_set, weight_set = (
            sem(n) for n in ("gated", "gate_step", "gap_set", "squashed_set", "weight_set"))
        h_ready, silu_set, s_scaled = sem("h_ready"), sem("silu_set"), sem("s_scaled")
        s_turned, s_hi_set, s_lo_set = sem("s_turned"), sem("s_hi_set"), sem("s_lo_set")
        out_ready, out_set = sem("out_ready"), sem("out_set")
        out_stored = [sem(f"out_stored{b}") for b in (0, 1)]

        def body_order(start, up, down, last):
            def body(t, b, j):
                ahead = not (isinstance(t, int) and t == NT - 1)
                down(t, b, 0, before=lambda: up(t, b, 2))
                down(t, b, 1, before=lambda: (up(t, b, 3), ahead and start(t + 1, 1 - b, 0)))
                if ahead:
                    start(t + 1, 1 - b, 1)
                down(t, b, 2, before=lambda: ahead and up(t + 1, 1 - b, 0))
                down(t, b, 3, before=lambda: ahead and up(t + 1, 1 - b, 1))
                last(t, b)
            return body

        def run(eng, start, up, down, last):
            start(0, 0, 0)
            start(0, 0, 1)
            up(0, 0, 0)
            up(0, 0, 1)
            node_tiles(eng, body_order(start, up, down, last))

        with nc.Block() as block:

            @block.sync
            def _(sp):
                sp.dma_start(gate_raw[:, :, :], w_gate.rearrange("(c p) e -> p c e", p=P)).then_inc(gate_loaded, 16)
                n = 0
                for weights in (w1, w2):
                    for e in range(NEXP):
                        if n >= 2:
                            sp.wait_ge(split_lo, n)
                        sp.dma_start(raw[n % 2][:, :].rearrange("p (c f) -> p c f", f=weights.shape[2]),
                                     weights[e].rearrange("(c p) f -> p c f", p=P)).then_inc(raw_loaded[n % 2], 16)
                        n += 1

                def load(t, b, j):
                    sp.wait_ge(x2_used, t + 1)
                    sp.dma_start(x2[b][:, :], x2_rows[bass.ds(t * P, P), :]).then_inc(x2_loaded[b], 16)

                node_tiles(sp, load)

            @block.gpsimd
            def _(pool):
                pool.memset(minus_half[:, :], -0.5).then_inc(const_set, 1)
                pool.iota(expert_no[:, :], [[1, NEXP]], base=0, channel_multiplier=0,
                          allow_small_or_imprecise_dtypes=True).then_inc(const_set, 1)
                pool.wait_ge(const_set, 2)
                with pool.Fori(0, NT) as t:
                    pool.wait_ge(ln_step, 3 * t + 3)
                    settle(pool, "pool")
                    pool.tensor_tensor(rstd[:, :], var_eps[:, :], minus_half[:, :], ALU.pow).then_inc(root_set, 1)

            def split_places():
                for e in range(NEXP):
                    cols = slice(e * FF, (e + 1) * FF)
                    yield e % 2, *[w[:, :, cols] for w in w1_t]
                for e in range(NEXP):
                    rows = slice(e * FF // P, (e + 1) * FF // P)
                    yield e % 2, *[w[:, rows, :] for w in w2_t]

            @block.tensor
            def _(pe):
                pe.wait_ge(split_lo, 2 * NEXP + 1)

                def start(t, b, part):
                    if part == 0:
                        pe.wait_ge(xn_set, t + 1)
                        turn(pe, ps_x, xn, ident[:, :]).then_inc(x_turned, 1)
                    else:
                        pe.wait_ge(x_lo_set, t + 1)
                        product(pe, ps_gate[:, 0:NEXP], xn_t, gate).then_inc(gated, 1)

                def up(t, b, c):
                    if c >= 2 or not isinstance(t, int) or t > 0:
                        pe.wait_ge(silu_set, steps * t + c - 1)
                    product(pe, ps_h[c % 2][:, :], xn_t, [w[:, :, c * width:(c + 1) * width] for w in w1_t]
                            ).then_inc(h_ready, 1)

                def down(t, b, c, before):
                    pe.wait_ge(s_scaled, steps * t + c + 1)
                    turn(pe, ps_s, s[c % 2], ident[:, :]).then_inc(s_turned, 1)
                    before()
                    pe.wait_ge(s_lo_set, steps * t + c + 1)
                    if c == 0 and not (isinstance(t, int) and t == 0):
                        pe.wait_ge(out_set, t + 1)
                    last = product(pe, ps_out[:, :], s_t, [w[:, c * C:(c + 1) * C, :] for w in w2_t],
                                   first=c == 0, final=c == steps - 1)
                    if c == steps - 1:
                        last.then_inc(out_ready, 1)

                run(pe, start, up, down, lambda t, b: None)

            @block.scalar
            def _(act):
                act.sem_inc(out_stored[0], 16)
                act.sem_inc(out_stored[1], 16)
                act.wait_ge(gate_loaded, 16)
                act.copy(gate[0][:, :, :], gate_raw[:, :, :]).then_inc(split_hi, 1)
                for n, (b, hi, lo) in enumerate(split_places()):
                    act.wait_ge(raw_loaded[b], 16 * (n // 2 + 1))
                    act.copy(hi, raw[b][:, :].rearrange("p (c f) -> p c f", f=hi.shape[2])).then_inc(split_hi, 1)

                def start(t, b, part):
                    if part == 0:
                        act.wait_ge(x_turned, t + 1)
                        act.copy(xn_t[0][:, :, :].rearrange("p c n -> p (c n)"), ps_x[:, :]).then_inc(x_hi_set, 1)
                    else:
                        act.wait_ge(gap_set, t + 1)
                        act.activation(squashed[:, :], gap[:, :], ACT.Tanh, scale=0.5).then_inc(squashed_set, 1)

                def up(t, b, c):
                    act.wait_ge(h_ready, steps * t + c + 1)
                    act.activation(s[c % 2][:, :], ps_h[c % 2][:, :], ACT.Silu).then_inc(silu_set, 1)

                def down(t, b, c, before):
                    act.wait_ge(s_turned, steps * t + c + 1)
                    act.copy(s_t[0][:, :, :].rearrange("p c n -> p (c n)"), ps_s[:, :]).then_inc(s_hi_set, 1)
                    before()

                def last(t, b):
                    r = rows_of(t)
                    act.wait_ge(out_set, t + 2)
                    act.dma_start(out[bass.ds(t * P, r), :], out_rows[b][0:r, :]).then_inc(out_stored[b], 16)

                run(act, start, up, down, last)
                act.wait_ge(out_stored[0], 16 * (NT // 2 + 2))
                act.wait_ge(out_stored[1], 16 * (NT // 2 + 1))

            @block.vector
            def _(dve):
                dve.sem_inc(x2_used, 2)
                dve.sem_inc(out_set, 1)
                dve.wait_ge(split_hi, 1)
                dve.tensor_tensor(gate[1][:, :, :], gate_raw[:, :, :], gate[0][:, :, :].bitcast(F32), ALU.subtract
                                  ).then_inc(split_lo, 1)
                for n, (b, hi, lo) in enumerate(split_places()):
                    dve.wait_ge(split_hi, n + 2)
                    dve.tensor_tensor(lo, raw[b][:, :].rearrange("p (c f) -> p c f", f=hi.shape[2]),
                                      hi.bitcast(F32), ALU.subtract).then_inc(split_lo, 1)
                dve.wait_ge(const_set, 2)

                def start(t, b, part):
                    if part == 0:
                        dve.wait_ge(x2_loaded[b], (t - b) * 8 + 16)
                        dve.bn_stats(stats[:, :], x2[b][:, :]).then_inc(ln_step, 1)
                        dve.wait_ge(ln_step, 3 * t + 1)
                        settle(dve, "dve")
                        dve.bn_aggr(moments[:, :], stats[:, :]).then_inc(ln_step, 1)
                        dve.wait_ge(ln_step, 3 * t + 2)
                        dve.tensor_scalar(var_eps[:, :], moments[:, 1:2], LN_EPS, None, ALU.add).then_inc(ln_step, 1)
                        dve.wait_ge(root_set, t + 1)
                        dve.tensor_scalar(xn[:, :], x2[b][:, :], moments[:, 0:1], rstd[:, 0:1], ALU.subtract, ALU.mult
                                          ).then_inc(xn_set, 1)
                        dve.wait_ge(x_hi_set, t + 1)
                        dve.tensor_tensor(xn_t[1][:, :, :].rearrange("p c n -> p (c n)"), ps_x[:, :],
                                          xn_t[0][:, :, :].bitcast(F32).rearrange("p c n -> p (c n)"), ALU.subtract
                                          ).then_inc(x_lo_set, 1)
                        return
                    base = 7 * t
                    dve.wait_ge(gated, t + 1)
                    dve.tensor_copy(logits[:, :], ps_gate[:, 0:NEXP]).then_inc(gate_step, 1)
                    dve.wait_ge(gate_step, base + 1)
                    settle(dve, "dve")
                    dve.max(top[:, :], logits[:, :]).then_inc(gate_step, 1)
                    dve.wait_ge(gate_step, base + 2)
                    dve.tensor_tensor(gap[:, :], top[:, 0:1], top[:, 1:2], ALU.subtract).then_inc(gap_set, 1)
                    settle(dve, "dve")
                    dve.max_index(top_no[:, :], top[:, :], logits[:, :]).then_inc(gate_step, 1)
                    dve.wait_ge(gate_step, base + 3)
                    dve.tensor_copy(top_no_f[:, :], top_no[:, :]).then_inc(gate_step, 1)
                    dve.wait_ge(squashed_set, t + 1)
                    dve.tensor_scalar(top_w[:, 0:1], squashed[:, :], 0.5, 0.5, ALU.mult, ALU.add).then_inc(gate_step, 1)
                    dve.tensor_scalar(top_w[:, 1:2], squashed[:, :], -0.5, 0.5, ALU.mult, ALU.add).then_inc(gate_step, 1)
                    dve.wait_ge(gate_step, base + 6)
                    for n in (0, 1):
                        last = dve.tensor_scalar(picked[n][:, :], expert_no[:, :], top_no_f[:, n:n + 1],
                                                 top_w[:, n:n + 1], ALU.is_equal, ALU.mult)
                    last.then_inc(gate_step, 1)
                    dve.wait_ge(gate_step, base + 7)
                    dve.tensor_tensor(weight[b][:, :], picked[0][:, :], picked[1][:, :], ALU.add).then_inc(weight_set, 1)

                def up(t, b, c):
                    dve.wait_ge(silu_set, steps * t + c + 1)
                    dve.wait_ge(weight_set, t + 1)
                    for n in (0, 1):
                        cols, e = slice(n * FF, (n + 1) * FF), 2 * c + n
                        last = dve.tensor_scalar(s[c % 2][:, cols], s[c % 2][:, cols], weight[b][:, e:e + 1], None,
                                                 ALU.mult)
                    last.then_inc(s_scaled, 1)

                def down(t, b, c, before):
                    dve.wait_ge(s_hi_set, steps * t + c + 1)
                    dve.tensor_tensor(s_t[1][:, :, :].rearrange("p c n -> p (c n)"), ps_s[:, :],
                                      s_t[0][:, :, :].bitcast(F32).rearrange("p c n -> p (c n)"), ALU.subtract
                                      ).then_inc(s_lo_set, 1)
                    before()

                def last(t, b):
                    dve.wait_ge(out_ready, t + 1)
                    dve.wait_ge(out_stored[b], (t - b) * 8 + 16)
                    dve.tensor_tensor(out_rows[b][:, :], x2[b][:, :], ps_out[:, :], ALU.add).then_inc(out_set, 1)
                    dve.wait_ge(out_set, t + 2)
                    dve.sem_inc(x2_used, 1)

                run(dve, start, up, down, last)


def build(nc, x, src, dst, w_gnn, b_gnn, w_qkv, w_proj, b_proj, w_gate, w1, w2, out, stop=4):
    table = nc.dram_tensor("gather_table", [NT * P, 2 * D], F16, kind="Internal").ap()
    q_rows = nc.dram_tensor("q_rows", [NT * P, D], F32, kind="Internal").ap()
    x2_rows = nc.dram_tensor("x2_rows", [NT * P, D], F32, kind="Internal").ap()
    window_rows = nc.dram_tensor("window_rows", [2 * NG], I32, kind="Internal").ap()
    everything = ExitStack()
    with everything:
        def sem(name):
            return everything.enter_context(nc.semaphore(name))

        def sb_in(scope):
            return lambda name, shape, dt: scope.enter_context(nc.sbuf_tensor(name, shape, dt))

        def ps_in(scope):
            return lambda name, shape: scope.enter_context(nc.psum_tensor(name, shape, F32))

        keep = sb_in(everything)
        ident = keep("ident", [P, P], F32)
        ones = keep("ones", [P, P], F32)
        mean = keep("mean", [P, NT], F32)
        rstd = keep("rstd", [P, NT], F32)
        dinv_down = keep("dinv_down", [P, NT], F32)
        real_row = keep("real_row", [P, 1], F32)

        acc_scope = everything.enter_context(ExitStack())
        acc = sb_in(acc_scope)("acc", [P, NT, D], F32)
        k_sum = sb_in(acc_scope)("k_sum", [P, D], F32)
        v = sb_in(acc_scope)("v", [P, D], F32)
        edge_scope = ExitStack()
        sb = sb_in(edge_scope)
        src_col = sb("src_col", [P, ET], I32)
        dst_col = sb("dst_col", [P, ET], F32)
        windows = sb("windows", [1, 2, NG], I32)
        tile_start = sb("tile_start", [P, NT], F32)
        iota = sb("iota", [P, P], BF16)
        w_t = [sb(f"w_qkv_t{n}", [P, C, 3 * D], F32R) for n in ("hi", "lo")]

        scope = ExitStack()
        with scope:
            sb, ps = sb_in(scope), ps_in(scope)
            edge_rows = [sb(f"{n}_rows", [P, ROWT * P], I32) for n in ("src", "dst")]
            edge_rows_f = [sb(f"{n}_rows_f", [P, ROWT * P], F32) for n in ("src", "dst")]
            w_ends = sb("window_ends", [P, 2, 2], F32)
            w_ends_i = sb("window_ends_i", [P, 2, 2], I32)
            w_tile_i = sb("window_tiles_i", [P, 2, 2], I32)
            w_clamped = sb("window_tiles", [P, 2, 2], I32)
            dst_i = sb("dst_i", [P, ET], I32)
            hi_i = sb("dst_tile_i", [P, ET], I32)
            hi_f = sb("dst_tile", [P, ET], F32)
            lo_f = sb("dst_in_tile", [P, ET], F32)
            one_hot_lo = [sb(f"one_hot_lo{b}", [P, ROWT, P], BF16) for b in (0, 1)]
            one_hot_hi = [sb(f"one_hot_hi{b}", [P, ROWT, NT], BF16) for b in (0, 1)]
            zeros = sb("zeros_b", [P, P], BF16)
            degree = sb("degree", [P, NT], F32)
            dinv_up = sb("dinv_up", [P, NT], F32)
            x_rows = [sb(f"x_rows{b}", [P, D], F32) for b in (0, 1)]
            stats = sb("stats", [P, NT, 6], F32)
            dinv, row_scale, var_eps, mean_sum, mean_gap, square_sum, gap_square, square_mean, minus_half = (
                sb(n, [P, NT], F32) for n in ("dinv", "row_scale", "var_eps", "mean_sum", "mean_gap",
                                              "square_sum", "gap_square", "square_mean", "minus_half"))
            parts = [sb(f"table_parts{b}", [P, 2, D], F16) for b in (0, 1)]
            w_rows = [p[:, :, :].rearrange("p a d -> p (a d)").bitcast(F32) for p in parts]
            turned = [ps(f"turned{b}", [P, 512]) for b in (0, 1)]
            ps_deg = ps("ps_deg", [P, 512])

            edges_loaded = [sem("src_loaded"), sem("dst_loaded")]
            windows_stored, windows_loaded = sem("windows_stored"), sem("windows_loaded")
            w_loaded = [sem(f"w_loaded{b}") for b in (0, 1)]
            x_loaded = [sem(f"x_loaded{b}") for b in (0, 1)]
            edges_padded, consts_set = sem("edges_padded"), sem("consts_set")
            edge_step = sem("edge_step")
            edges_turned = sem("edges_turned")
            edges_copied = sem("edges_copied")
            w_turned, w_hi_set, w_lo_set = sem("w_turned"), sem("w_hi_set"), sem("w_lo_set")
            one_hots_built = [sem(f"one_hots_built{b}") for b in (0, 1)]
            one_hots_used = sem("one_hots_used")
            degrees_summed, degree_set, roots_set = sem("degrees_summed"), sem("degree_set"), sem("roots_set")
            x_used = sem("x_used")
            stats_set, moment_step, var_set = sem("stats_set"), sem("moment_step"), sem("var_set")
            acc_set, hi_part_set, lo_part_set = sem("acc_set"), sem("hi_part_set"), sem("lo_part_set")
            parts_stored = [sem(f"parts_stored{b}") for b in (0, 1)]
            turns = {e: sem(f"{e}_turns") for e in ("pe", "act", "dve", "pool")}

            def settle(eng, name):
                eng.sem_inc(turns[name], 1)

            with nc.Block() as block:

                @block.sync
                def _(sp):
                    sp.wait_ge(edges_padded, 2)
                    for rows, col, loaded in zip(edge_rows, (src, dst), edges_loaded):
                        full = EFULL * ROWT * P
                        sp.dma_start(rows[0:EFULL, :], col[0:full].rearrange("(r e) -> r e", e=ROWT * P)
                                     ).then_inc(loaded, 16)
                        sp.dma_start(rows[EFULL:EFULL + 1, 0:EREST],
                                     col[full:E].rearrange("(r e) -> r e", r=1)).then_inc(loaded, 16)
                    def load_x(t, b, j, before=0):
                        sp.wait_ge(x_used, t + before + 1)
                        r = rows_of(t)
                        sp.dma_start(x_rows[b][0:r, :], x[bass.ds(t * P, r), :]).then_inc(x_loaded[b], 16)

                    node_tiles(sp, load_x)
                    with sp.Fori(0, NWB // 2) as j:
                        for b in (0, 1):
                            sp.wait_ge(w_turned, 2 * j + b + 1)
                            sp.dma_start(w_rows[b], w_qkv[bass.ds((2 * j + b) * P, P), :]
                                         ).then_inc(w_loaded[b], 16)
                    sp.wait_ge(edge_step, 8)
                    for side in (0, 1):
                        sp.dma_start(window_rows[side * NG:(side + 1) * NG].rearrange("(r g) -> r g", g=2),
                                     w_clamped[0:ER, side, :]).then_inc(windows_stored, 16)
                    sp.wait_ge(windows_stored, 32)
                    sp.dma_start(windows[:, :, :], window_rows.rearrange("(a s g) -> a s g", a=1, s=2)
                                 ).then_inc(windows_loaded, 16)


                    def reload_x(t, b):
                        load_x(t, 1 - b, None, NT)

                    def store_parts(t, b):
                        sp.wait_ge(lo_part_set, t + 1)
                        sp.dma_start(table[bass.ds(t * P, P), :], parts[b][:, :, :].rearrange("p a d -> p (a d)")
                                     ).then_inc(parts_stored[b], 16)

                    reload_x(0, 0)
                    reload_x(1, 1)
                    with sp.Fori(0, NT // 2 - 1) as j:
                        for b in (0, 1):
                            store_parts(2 * j + b, b)
                            reload_x(2 * j + 2 + b, b)
                    store_parts(NT - 3, 0)
                    reload_x(NT - 1, 0)
                    store_parts(NT - 2, 1)
                    store_parts(NT - 1, 0)
                    sp.wait_ge(parts_stored[0], 16 * (NT // 2 + 2))
                    sp.wait_ge(parts_stored[1], 16 * (NT // 2 + 1))
                    sp.wait_ge(windows_loaded, 16)

                @block.gpsimd
                def _(pool):
                    pool.memset(edge_rows[0][:, :], 0).then_inc(edges_padded, 1)
                    pool.memset(edge_rows[1][:, :], PAD_DST).then_inc(edges_padded, 1)
                    pool.memset(ones[:, :], 1.0).then_inc(consts_set, 1)
                    pool.memset(zeros[:, :], 0.0).then_inc(consts_set, 1)
                    pool.iota(iota[:, :], [[1, P]], base=0, channel_multiplier=0,
                              allow_small_or_imprecise_dtypes=True).then_inc(consts_set, 1)
                    pool.iota(tile_start[:, :], [[P, NT]], base=0, channel_multiplier=0,
                              allow_small_or_imprecise_dtypes=True).then_inc(consts_set, 1)
                    pool.wait_ge(consts_set, 4)
                    pool.affine_select(out=ident[:, :], in_=ones[:, :], compare_op=ALU.is_equal, fill=0.0,
                                       base=0, pattern=[[-1, P]], channel_multiplier=1).then_inc(consts_set, 1)
                    pool.affine_select(out=real_row[:, :], in_=ones[:, 0:1], compare_op=ALU.is_gt, fill=0.0,
                                       base=LAST, pattern=[[0, 1]], channel_multiplier=-1).then_inc(consts_set, 1)
                    pool.memset(minus_half[:, :], -0.5).then_inc(consts_set, 1)
                    pool.wait_ge(consts_set, 7)
                    pool.wait_ge(var_set, 1)
                    pool.tensor_tensor(rstd[:, :], var_eps[:, :], minus_half[:, :], ALU.pow).then_inc(roots_set, 1)
                    pool.wait_ge(degree_set, 1)
                    pool.tensor_tensor(dinv[:, :], degree[:, :], minus_half[:, :], ALU.pow).then_inc(roots_set, 1)

                    def low_part(t, b, j):
                        pool.wait_ge(hi_part_set, t + 1)
                        settle(pool, "pool")
                        pool.tensor_tensor(parts[b][:, 1, :], acc[:, t, :], parts[b][:, 0, :],
                                           ALU.subtract).then_inc(lo_part_set, 1)

                    node_tiles(pool, low_part)

                @block.tensor
                def _(pe):
                    pe.sem_inc(w_turned, 2)
                    pe.sem_inc(one_hots_used, 2)
                    pe.wait_ge(consts_set, 6)
                    n = 0
                    for k in (0, 1):
                        pe.wait_ge(edge_step, k + 1)
                        for b in range(ROWT):
                            pe.wait_ge(edges_copied, n + 1)
                            pe.transpose(turned[n % 2][:, 0:ER], edge_rows_f[k][0:ER, b * P:(b + 1) * P],
                                         ident[0:ER, 0:ER]).then_inc(edges_turned, 1)
                            n += 1
                    pe.wait_ge(edges_copied, n + 2)
                    with pe.Fori(0, NWB // 2) as j:
                        for b in (0, 1):
                            pe.wait_ge(w_loaded[b], 16 * j + 16)
                            pe.wait_ge(w_lo_set, 2 * j + b + 1)
                            turn(pe, turned[b], w_rows[b], ident[:, :]).then_inc(w_turned, 1)
                    pe.matmul(ps_deg[:, 0:NT], zeros[:, :], zeros[:, 0:NT], start=True, stop=False,
                              skip_group_check=True)
                    with pe.Fori(0, NT) as j:
                        for b in (0, 1):
                            pe.wait_ge(one_hots_built[b], j + 1)
                            for e in range(ROWT):
                                last = pe.matmul(ps_deg[:, 0:NT], one_hot_lo[b][:, e, :], one_hot_hi[b][:, e, :],
                                                 start=False, stop=False, skip_group_check=True)
                            last.then_inc(one_hots_used, 1)
                    pe.matmul(ps_deg[:, 0:NT], zeros[:, :], zeros[:, 0:NT], start=False, stop=True,
                              skip_group_check=True).then_inc(degrees_summed, 1)

                @block.scalar
                def _(act):
                    act.sem_inc(parts_stored[0], 16)
                    act.sem_inc(parts_stored[1], 16)
                    with act.Fori(0, NWB // 2) as j:
                        for b in (0, 1):
                            act.wait_ge(w_turned, 2 * j + b + 3)
                            settle(act, "act")
                            act.copy(w_t[0][:, :, bass.ds((2 * j + b) * P, P)],
                                     turned[b][:, :].rearrange("p (c o) -> p c o", c=C)).then_inc(w_hi_set, 1)

                    def high_part(t, b, j):
                        act.wait_ge(acc_set, t + 1)
                        act.wait_ge(parts_stored[b], 16 * j + 16)
                        settle(act, "act")
                        act.copy(parts[b][:, 0, :], acc[:, t, :]).then_inc(hi_part_set, 1)

                    node_tiles(act, high_part)

                @block.vector
                def _(dve):
                    dve.sem_inc(x_used, 2)
                    dve.sem_inc(w_lo_set, 2)
                    dve.sem_inc(edges_copied, 2)
                    steps = 0

                    def step(ins):
                        nonlocal steps
                        ins.then_inc(edge_step, 1)
                        steps += 1

                    def after_steps():
                        dve.wait_ge(edge_step, steps)

                    for k in (0, 1):
                        dve.wait_ge(edges_loaded[k], 32)
                        step(dve.tensor_copy(edge_rows_f[k][0:ER, :], edge_rows[k][0:ER, :]))
                    after_steps()
                    dst_groups = edge_rows_f[1][0:ER, :].rearrange("r (g e) -> r g e", g=2)
                    step(dve.tensor_reduce(w_ends[0:ER, 0, :], dst_groups, AX_X, ALU.min))
                    step(dve.tensor_reduce(w_ends[0:ER, 1, :], dst_groups, AX_X, ALU.max))
                    after_steps()
                    step(dve.tensor_copy(w_ends_i[0:ER], w_ends[0:ER]))
                    after_steps()
                    step(dve.tensor_single_scalar(w_tile_i[0:ER], w_ends_i[0:ER], 7, ALU.arith_shift_right))
                    after_steps()
                    step(dve.tensor_scalar(w_clamped[0:ER, 0, :], w_tile_i[0:ER, 0, :], NT - 1, None, ALU.min))
                    step(dve.tensor_scalar(w_clamped[0:ER, 1, :], w_tile_i[0:ER, 1, :], NT - 1, 1,
                                           ALU.min, ALU.add))
                    assert steps == 8
                    n = 0
                    for k in (0, 1):
                        col = (src_col, dst_col)[k]
                        for b in range(ROWT):
                            dve.wait_ge(edges_turned, n + 1)
                            dve.tensor_copy(col[:, b:ET:ROWT], turned[n % 2][:, 0:ER]).then_inc(edges_copied, 1)
                            n += 1
                    dve.wait_ge(edges_copied, n + 2)
                    step(dve.tensor_copy(dst_i[:, :], dst_col[:, :]))
                    after_steps()
                    step(dve.tensor_single_scalar(hi_i[:, :], dst_i[:, :], 7, ALU.arith_shift_right))
                    after_steps()
                    step(dve.tensor_copy(hi_f[:, :], hi_i[:, :]))
                    after_steps()
                    step(dve.scalar_tensor_tensor(lo_f[:, :], hi_f[:, :], -float(P), dst_col[:, :],
                                                  ALU.mult, ALU.add))
                    after_steps()

                    def row_stats(t, b, j):
                        dve.wait_ge(x_loaded[b], 16 * j + 16)
                        dve.bn_stats(stats[:, t, :], x_rows[b][:, :]).then_inc(stats_set, 1)
                        dve.wait_ge(stats_set, t + 1)
                        dve.sem_inc(x_used, 1)

                    node_tiles(dve, row_stats)
                    moments = 0

                    def moment(ins):
                        nonlocal moments
                        ins.then_inc(moment_step, 1)
                        moments += 1

                    def after():
                        dve.wait_ge(moment_step, moments)

                    even, odd = stats[:, :, 1], stats[:, :, 4]
                    moment(dve.tensor_tensor(mean_sum[:, :], even, odd, ALU.add))
                    moment(dve.tensor_tensor(mean_gap[:, :], even, odd, ALU.subtract))
                    moment(dve.tensor_tensor(square_sum[:, :], stats[:, :, 2], stats[:, :, 5], ALU.add))
                    after()
                    moment(dve.tensor_scalar(mean[:, :], mean_sum[:, :], 0.5, None, ALU.mult))
                    moment(dve.scalar_tensor_tensor(gap_square[:, :], mean_gap[:, :], 0.25, mean_gap[:, :],
                                                    ALU.mult, ALU.mult))
                    moment(dve.tensor_scalar(square_mean[:, :], square_sum[:, :], 1.0 / D, LN_EPS, ALU.mult, ALU.add))
                    after()
                    dve.tensor_tensor(var_eps[:, :], square_mean[:, :], gap_square[:, :], ALU.add).then_inc(var_set, 1)

                    with dve.Fori(0, NWB // 2) as j:
                        for b in (0, 1):
                            dve.wait_ge(w_hi_set, 2 * j + b + 1)
                            cols = bass.ds((2 * j + b) * P, P)
                            dve.tensor_tensor(w_t[1][:, :, cols],
                                              turned[b][:, :].rearrange("p (c o) -> p c o", c=C),
                                              w_t[0][:, :, cols].bitcast(F32), ALU.subtract).then_inc(w_lo_set, 1)

                    dve.wait_ge(consts_set, 6)
                    with dve.Fori(0, NT) as j:
                        for b in (0, 1):
                            dve.wait_ge(one_hots_used, 2 * j + b + 1)
                            for e in range(ROWT):
                                t = (2 * j + b) * ROWT + e
                                dve.tensor_scalar(one_hot_lo[b][:, e, :], iota[:, :],
                                                  lo_f[:, bass.ds(t, 1)], None, ALU.is_equal)
                            tiles = hi_f[:, bass.ds((2 * j + b) * ROWT, ROWT)]
                            dve.tensor_tensor(
                                one_hot_hi[b][:, :, :],
                                iota[:, 0:NT].rearrange("p (a n) -> p a n", a=1).broadcast_to([P, ROWT, NT]),
                                tiles.rearrange("p (t a) -> p t a", a=1).broadcast_to([P, ROWT, NT]),
                                ALU.is_equal).then_inc(one_hots_built[b], 1)

                    dve.wait_ge(degrees_summed, 1)
                    dve.tensor_scalar(degree[:, :], ps_deg[:, 0:NT], 1.0, None, ALU.add).then_inc(degree_set, 1)
                    dve.wait_ge(roots_set, 2)
                    moment(dve.tensor_scalar(dinv_up[:, :], dinv[:, :], TABLE_SCALE, None, ALU.mult))
                    moment(dve.tensor_scalar(dinv_down[:, :], dinv[:, :], 1.0 / TABLE_SCALE, None, ALU.mult))
                    moment(dve.tensor_tensor(rstd[:, NT - 1:NT], rstd[:, NT - 1:NT], real_row[:, :], ALU.mult))
                    after()
                    moment(dve.tensor_tensor(row_scale[:, :], rstd[:, :], dinv_up[:, :], ALU.mult))
                    after()

                    def scaled_rows(t, b, j):
                        o = 1 - b
                        dve.wait_ge(x_loaded[o], 16 * (j + NT // 2 + 1 - o) + 16)
                        dve.tensor_scalar(acc[:, t, :], x_rows[o][:, :], mean[:, bass.ds(t, 1)],
                                          row_scale[:, bass.ds(t, 1)], ALU.subtract, ALU.mult).then_inc(acc_set, 1)
                        dve.wait_ge(acc_set, t + 1)
                        dve.sem_inc(x_used, 1)

                    node_tiles(dve, scaled_rows)

        if stop < 2:
            return

        scope = ExitStack()
        with scope:
            sb, ps = sb_in(scope), ps_in(scope)
            ring = sb("gathered", [P, GPT, GE, 2, D], F16)
            src_now = sb("src_now", [P, GPT, GE], I32)
            one_hot = sb("one_hot", [P, 2, GE, P], F16)
            x_rows = [sb(f"x_rows_b{b}", [P, D], F32) for b in (0, 1)]
            xn_t = [sb(f"xn_t{n}", [P, C, P], F32R) for n in ("hi", "lo")]
            q = sb("q", [P, D], F32)
            k = sb("k", [P, D], F32)
            zeros = sb("zeros_b2", [P, P], BF16)
            ps_turn = ps("ps_turn", [P, 512])
            ps_qv, ps_k, ps_kv = ps("ps_qv", [P, 512]), ps("ps_k", [P, 512]), ps("ps_kv", [P, 512])
            ps_sum = ps("ps_sum", [P, 2, 512])
            ps_mark = ps("ps_mark", [P, 512])

            landed = [sem(f"group_landed{g}") for g in range(GPT)]
            src_copied, group_summed = sem("src_copied"), sem("group_summed")
            one_hot_built, pair_summed, pair_added = sem("one_hot_built"), sem("pair_summed"), sem("pair_added")
            x_loaded = [sem(f"x_loaded_b{b}") for b in (0, 1)]
            xn_set, xn_turned, xn_hi_set, xn_lo_set = sem("xn_set"), sem("xn_turned"), sem("xn_hi_set"), sem("xn_lo_set")
            q_ready, k_ready, v_ready = sem("q_ready"), sem("k_ready"), sem("v_ready")
            q_set, k_set, v_set, q_stored = sem("q_set"), sem("k_set"), sem("v_set"), sem("q_stored")
            k_added, kv_summed, zeros_set = sem("k_added"), sem("kv_summed"), sem("zeros_set")

            with nc.Block() as block:

                @block.sync
                def _(sp):
                    def load_x(t, b, j):
                        sp.wait_ge(xn_turned, t + 1)
                        r = rows_of(t)
                        sp.dma_start(x_rows[b][0:r, :], x[bass.ds(t * P, r), :]).then_inc(x_loaded[b], 16)

                    node_tiles(sp, load_x)

                @block.gpsimd
                def _(pool):
                    with pool.Fori(0, NT) as t:
                        for g in range(GPT):
                            pool.wait_ge(group_summed, GPT * t + g + 1)
                            settle(pool, "pool")
                            pool.tensor_copy(src_now[:, g, :], src_col[:, bass.ds((GPT * t + g) * GE, GE)]
                                             ).then_inc(src_copied, 1)
                            pool.wait_ge(src_copied, GPT * t + g + 1)
                            settle(pool, "pool")
                            for e in range(GE):
                                pool.indirect_dma_start(
                                    ring[:, g, e, :, :].rearrange("p a d -> p (a d)"), None, table,
                                    bass.IndirectOffsetOnAxis(src_now[:, g, e:e + 1], 0)).then_inc(landed[g], 16)

                @block.tensor
                def _(pe):
                    pe.sem_inc(group_summed, GPT)
                    pe.sem_inc(xn_turned, 2)
                    pe.wait_ge(zeros_set, 2)
                    pe.matmul(ps_kv[:, :], zeros[:, :], one_hot[:, 0, :, :].bitcast(BF16).rearrange("p e n -> p (e n)"),
                              start=True, stop=False, skip_group_check=True)
                    pe.matmul(ps_sum[:, 0, :], zeros[:, :], one_hot[:, 0, :, :].bitcast(BF16).rearrange("p e n -> p (e n)"),
                              start=True, stop=True).then_inc(pair_summed, 1)
                    pair = pe.alloc_register("pair")
                    pe.reg_mov(pair, 1)

                    def sum_group(t, g):
                        at = GPT * t + g
                        first = pe.value_load(windows[0:1, 0, bass.ds(at, 1)], min_val=0, max_val=NT - 1)
                        end = pe.value_load(windows[0:1, 1, bass.ds(at, 1)], min_val=1, max_val=NT)
                        pe.wait_ge(landed[g], 16 * GE * t + 16 * GE)
                        settle(pe, "pe")
                        with pe.Fori(first, end):
                            now = pe.snap(pair, min_val=1, max_val=NG * NT)
                            half = pe.snap(now % 2)
                            pe.wait_ge(one_hot_built, now)
                            settle(pe, "pe")
                            for e in range(GE):
                                for part in (0, 1):
                                    last = pe.matmul(ps_sum[:, half, :], one_hot[:, half, e, :], ring[:, g, e, part, :],
                                                     start=e == 0 and part == 0, stop=e == GE - 1 and part == 1)
                            last.then_inc(pair_summed, 1)
                            pe.reg_add(pair, now, 1)
                        pe.matmul(ps_mark[0:2, 0:2], zeros[:, 0:2], zeros[:, 0:2], start=True, stop=True
                                  ).then_inc(group_summed, 1)

                    def tile(t, b, j):
                        pe.wait_ge(xn_set, t + 1)
                        turn(pe, ps_turn, x_rows[b], ident[:, :]).then_inc(xn_turned, 1)
                        sum_group(t, 0)
                        pe.wait_ge(xn_lo_set, t + 1)
                        product(pe, ps_qv[:, :], xn_t, [w[:, :, 0:D] for w in w_t]).then_inc(q_ready, 1)
                        sum_group(t, 1)
                        product(pe, ps_k[:, :], xn_t, [w[:, :, D:2 * D] for w in w_t]).then_inc(k_ready, 1)
                        sum_group(t, 2)
                        pe.wait_ge(q_set, t + 1)
                        product(pe, ps_qv[:, :], xn_t, [w[:, :, 2 * D:3 * D] for w in w_t]).then_inc(v_ready, 1)
                        sum_group(t, 3)
                        pe.wait_ge(k_set, t + 1)
                        pe.wait_ge(v_set, t + 1)
                        for c in range(C):
                            cols = slice(c * P, (c + 1) * P)
                            last = pe.matmul(ps_kv[:, cols], v[:, cols], k[:, cols], start=False, stop=False,
                                             skip_group_check=True)
                        last.then_inc(kv_summed, 1)

                    node_tiles(pe, tile)
                    pe.matmul(ps_kv[:, :], zeros[:, :], one_hot[:, 0, :, :].bitcast(BF16).rearrange("p e n -> p (e n)"),
                              start=False, stop=True, skip_group_check=True).then_inc(kv_summed, 1)

                @block.scalar
                def _(act):
                    act.sem_inc(q_stored, 16)

                    def tile(t, b, j):
                        act.wait_ge(xn_turned, t + 3)
                        act.copy(xn_t[0][:, :, :].rearrange("p c n -> p (c n)"), ps_turn[:, :]).then_inc(xn_hi_set, 1)
                        act.wait_ge(q_ready, t + 1)
                        act.wait_ge(q_stored, 16 * t + 16)
                        act.activation(q[:, :], ps_qv[:, :], ACT.Relu).then_inc(q_set, 1)
                        act.wait_ge(q_set, t + 1)
                        act.dma_start(q_rows[bass.ds(t * P, P), :], q[:, :]).then_inc(q_stored, 16)
                        act.wait_ge(k_ready, t + 1)
                        act.wait_ge(k_added, t + 1)
                        act.activation(k[:, :], ps_k[:, :], ACT.Relu).then_inc(k_set, 1)

                    node_tiles(act, tile)
                    act.wait_ge(q_stored, 16 * NT + 16)

                @block.vector
                def _(dve):
                    dve.memset(zeros[:, :], 0.0).then_inc(zeros_set, 1)
                    dve.memset(one_hot[:, 0, :, :], 0.0).then_inc(zeros_set, 1)
                    dve.memset(k_sum[:, :], 0.0).then_inc(k_added, 1)
                    dve.sem_inc(pair_added, 1)
                    pair, window_before = dve.alloc_register("pair"), dve.alloc_register("window_before")
                    dve.reg_mov(pair, 1)
                    dve.reg_mov(window_before, 0)

                    def add_pair(before, window):
                        dve.wait_ge(pair_summed, before + 1)
                        dve.wait_ge(pair_added, before + 1)
                        dve.tensor_tensor(acc[:, window, :], acc[:, window, :], ps_sum[:, before % 2, :], ALU.add
                                          ).then_inc(pair_added, 1)

                    def sum_group(t, g):
                        at = GPT * t + g
                        first = dve.value_load(windows[0:1, 0, bass.ds(at, 1)], min_val=0, max_val=NT - 1)
                        end = dve.value_load(windows[0:1, 1, bass.ds(at, 1)], min_val=1, max_val=NT)
                        with dve.Fori(first, end) as window:
                            now = dve.snap(pair, min_val=1, max_val=NG * NT)
                            half = dve.snap(now % 2)
                            start = tile_start[:, bass.ds(window, 1)]
                            for e in range(GE):
                                last = dve.tensor_scalar(one_hot[:, half, e, :], iota[:, :], start,
                                                         dst_col[:, bass.ds(at * GE + e, 1)], ALU.add, ALU.is_equal)
                            last.then_inc(one_hot_built, 1)
                            add_pair(now - 1, dve.snap(window_before, min_val=0, max_val=NT - 1))
                            dve.reg_add(pair, now, 1)
                            dve.reg_mov(window_before, window)

                    def tile(t, b, j):
                        dve.wait_ge(x_loaded[b], 16 * j + 16)
                        dve.tensor_scalar(x_rows[b][:, :], x_rows[b][:, :], mean[:, bass.ds(t, 1)], rstd[:, bass.ds(t, 1)],
                                          ALU.subtract, ALU.mult).then_inc(xn_set, 1)
                        dve.wait_ge(xn_hi_set, t + 1)
                        dve.tensor_tensor(xn_t[1][:, :, :], ps_turn[:, :].rearrange("p (c n) -> p c n", c=C),
                                          xn_t[0][:, :, :].bitcast(F32), ALU.subtract).then_inc(xn_lo_set, 1)
                        sum_group(t, 0)
                        sum_group(t, 1)
                        sum_group(t, 2)
                        dve.wait_ge(k_set, t + 1)
                        dve.wait_ge(k_added, t + 1)
                        dve.tensor_tensor(k_sum[:, :], k_sum[:, :], k[:, :], ALU.add).then_inc(k_added, 1)
                        dve.wait_ge(v_ready, t + 1)
                        dve.tensor_scalar(v[:, :], ps_qv[:, :], 1.0, None, ALU.mult).then_inc(v_set, 1)
                        sum_group(t, 3)

                    node_tiles(dve, tile)
                    dve.drain()
                    now = dve.snap(pair, min_val=1, max_val=NG * NT + 1)
                    add_pair(now - 1, dve.snap(window_before, min_val=0, max_val=NT - 1))
                    dve.wait_ge(kv_summed, NT + 1)
                    dve.tensor_copy(v[:, :], ps_kv[:, :])

        edge_scope.close()
        if stop < 3:
            return
        mix(nc, sb_in, ps_in, sem, turns, settle, acc, k_sum, v, ident, ones, dinv_down, x, q_rows, x2_rows,
            w_gnn, b_gnn, w_proj, b_proj)
        acc_scope.close()
        if stop < 4:
            return
        experts(nc, sb_in, ps_in, sem, turns, settle, ident, x2_rows, w_gate, w1, w2, out)


_INS = ['x', 'src', 'dst', 'L0_gnn_W', 'L0_gnn_b', 'L0_mix_qkv_weight', 'L0_mix_proj_weight',
        'L0_mix_proj_bias', 'L0_ffn_Wg', 'L0_ffn_W1', 'L0_ffn_W2']


def kernel(**inputs):
    import numpy as _np
    import concourse.bacc as _bacc
    from concourse import mybir as _mybir
    from concourse.bass_utils import run_bass_kernel_spmd as _run

    nc = _bacc.Bacc("TRN2", target_bir_lowering=False, num_devices=1)
    arrays, args = {}, []
    for name in _INS:
        a = _np.ascontiguousarray(inputs[name])
        arrays[f"in_{name}"] = a
        args.append(nc.dram_tensor(f"in_{name}", a.shape, _mybir.dt.from_np(a.dtype), kind="ExternalInput").ap())
    args.append(nc.dram_tensor("out_0", (N, D), _mybir.dt.float32, kind="ExternalOutput").ap())
    build(nc, *args, stop=4)
    r = _run(nc, [arrays], core_ids=[0])
    return r.results[0]["out_0"]
```

```python
from contextlib import ExitStack

import concourse.bass as bass
from concourse import mybir

F32 = mybir.dt.float32
F32R = mybir.dt.float32r
F16 = mybir.dt.float16
BF16 = mybir.dt.bfloat16
I32 = mybir.dt.int32
U32 = mybir.dt.uint32
ALU = mybir.AluOpType
ACT = mybir.ActivationFunctionType
AX_X = mybir.AxisListType.X

P = 128
N, D = 6250, 512
E = 100000
H, DH = 16, 32
NEXP, FF = 8, 256
C = D // P
NT = -(-N // P)
LAST = N - (NT - 1) * P
ET = 16 * NT
GE = 4
NG = ET // GE
GPT = NG // NT
BATCH = ET // NT
ROWT = 8
ER = ET // ROWT
EFULL = E // (ROWT * P)
EREST = E - EFULL * ROWT * P
PAD_DST = 8191
XPARTS = 7
NWB = 3 * D // P
PAIRS = 2 * NT * P // (2 * P) + NEXP
LOWEST = -3.0e38
LN_EPS = 1e-5
DIV_EPS = 1e-15
SLOPE = 0.01
TABLE_SCALE = 1024.0
assert ET * P >= E and ER <= P and NT % 2 == 1 and GPT == 4 and EREST > 0 and NT % XPARTS == 0


def node_tiles(eng, body):
    with eng.Fori(0, NT // 2) as j:
        body(2 * j, 0, j)
        body(2 * j + 1, 1, j)
    body(NT - 1, 0, NT // 2)


def tile_pairs(eng, body):
    assert NT % 4 == 1
    with eng.Fori(0, NT // 4) as j:
        body(2 * j, 2, 0)
        body(2 * j + 1, 2, 1)
    body(NT // 2, 1, 0)


def node_tiles_ahead(eng, start, finish):
    start(0, 0)
    with eng.Fori(0, NT // 2) as j:
        start(2 * j + 1, 1)
        finish(2 * j, 0)
        start(2 * j + 2, 0)
        finish(2 * j + 1, 1)
    finish(NT - 1, 0)


def staggered(eng, *stages):
    most = max(ahead for ahead, _ in stages)
    turns = NT // 4 * 4 - 4

    def run(t, b):
        for ahead, body in stages:
            if not isinstance(t, int) or 0 <= t + ahead < NT:
                body(t + ahead, (b + ahead) % 4)

    assert NT % 4 == 1 and most <= 4
    for t in range(-most, 0):
        run(t, t % 4)
    with eng.Fori(0, turns // 4) as j:
        for b in range(4):
            run(4 * j + b, b)
    for t in range(turns, NT):
        run(t, t % 4)


def rows_of(t):
    return LAST if isinstance(t, int) and t == NT - 1 else P


def turn(pe, out, rows, ident, chunks=C):
    for c in range(chunks):
        last = pe.transpose(out[:, c * P:(c + 1) * P], rows[:, c * P:(c + 1) * P], ident)
    return last


def product(pe, out, left, right, chunks=C):
    for c in range(chunks):
        for a, b in ((1, 0), (0, 1), (0, 0)):
            last = pe.matmul(out, left[a][:, c, :], right[b][:, c, :],
                             start=c == 0 and a == 1, stop=c == chunks - 1 and a + b == 0)
    return last


def mix(nc, sb_in, ps_in, sem, turns, settle, acc, k_sum, kv, ident, ones, dinv_down, x, q_rows, x2_rows,
        w_gnn, b_gnn, w_proj, b_proj):
    scope = ExitStack()
    with scope:
        sb, ps = sb_in(scope), ps_in(scope)
        proj_rows = sb("proj_rows", [P, C, D], F32)
        proj_t = sb("proj_t", [P, C, D], F32)
        gnn_raw = sb("gnn_raw", [P, C, D], F32)
        gnn_w = [sb(f"gnn_w_{n}", [P, C, D], F32R) for n in ("hi", "lo")]
        mixer = [sb(f"mixer_{n}", [P, C, D], F32R) for n in ("hi", "lo")]
        kv_heads = sb("kv_heads", [P, C, P], F32)
        k_all = sb("k_all", [P, D], F32)
        b_gnn_rows, b_proj_rows = sb("b_gnn_rows", [P, D], F32), sb("b_proj_rows", [P, D], F32)
        q, x_rows = [proj_rows[:, b, :] for b in range(4)], [proj_t[:, b, :] for b in range(4)]
        qk = [sb(f"qk{b}", [P, D], F32) for b in (0, 1)]
        den, den_eps, den_inv = (sb(n, [P, H], F32) for n in ("den", "den_eps", "den_inv"))
        a_rows = sb("a_rows", [P, D], F32)
        q_t = [[sb(f"q_t{b}{n}", [P, C, P], F32R) for n in ("hi", "lo")] for b in (0, 1)]
        a_t = [[sb(f"a_t{b}{n}", [P, C, P], F32R) for n in ("hi", "lo")] for b in (0, 1)]
        h = sb("h", [P, D], F32)
        g = [sb(f"g{b}", [P, D], F32) for b in (0, 1)]
        ps_q, ps_a = ps("ps_q_turned", [P, 512]), ps("ps_a_turned", [P, 512])
        ps_mix = [ps(f"ps_mix{b}", [P, 512]) for b in (0, 1)]
        ps_gnn = [ps(f"ps_gnn{b}", [P, 512]) for b in (0, 1)]

        proj_loaded, gnn_loaded, biases_loaded = sem("proj_loaded"), sem("gnn_loaded"), sem("biases_loaded")
        proj_turned, proj_copied = sem("proj_turned"), sem("proj_copied")
        heads_zeroed, heads_set, k_all_summed, k_all_set = (
            sem(n) for n in ("heads_zeroed", "heads_set", "k_all_summed", "k_all_set"))
        mixer_summed, mixer_hi_set, mixer_lo_set = sem("mixer_summed"), sem("mixer_hi_set"), sem("mixer_lo_set")
        gnn_hi_set, gnn_lo_set = sem("gnn_hi_set"), sem("gnn_lo_set")
        x_loaded = [sem(f"x_loaded_c{b}") for b in range(4)]
        q_loaded = [sem(f"q_loaded_c{b}") for b in range(4)]
        qk_set, x_biased, q_divided, a_set = sem("qk_set"), sem("x_biased"), sem("q_divided"), sem("a_set")
        den_step = sem("den_step")
        turned, hi_set, lo_set = sem("turned_c"), sem("hi_set_c"), sem("lo_set_c")
        mixed, gnn_done, h_step, x2_set = sem("mixed"), sem("gnn_done"), sem("h_step"), sem("x2_set")
        g_set, x2_stored = sem("g_set"), sem("x2_stored")

        with nc.Block() as block:

            @block.sync
            def _(sp):
                sp.dma_start(proj_rows[:, :, :], w_proj.rearrange("(r p) d -> p r d", p=P)).then_inc(proj_loaded, 16)
                sp.dma_start(gnn_raw[:, :, :], w_gnn.rearrange("(c p) d -> p c d", p=P)).then_inc(gnn_loaded, 16)
                for rows, bias in ((b_gnn_rows, b_gnn), (b_proj_rows, b_proj)):
                    sp.dma_start(rows[:, :], bias.rearrange("(a d) -> a d", a=1).broadcast_to([P, D])
                                 ).then_inc(biases_loaded, 16)

                sp.wait_ge(proj_turned, C)
                sp.wait_ge(mixer_summed, C)

                def load_q(t, b):
                    sp.wait_ge(turned, 2 * t + 1)
                    sp.dma_start(q[b][:, :], q_rows[bass.ds(t * P, P), :]).then_inc(q_loaded[b], 16)

                def load_x(t, b):
                    sp.wait_ge(x2_set, t + 1)
                    r = rows_of(t)
                    sp.dma_start(x_rows[b][0:r, :], x[bass.ds(t * P, r), :]).then_inc(x_loaded[b], 16)

                def store(t, b):
                    sp.wait_ge(x2_set, t + 5)
                    sp.dma_start(x2_rows[bass.ds(t * P, P), :], acc[:, t, :]).then_inc(x2_stored, 16)

                staggered(sp, (4, load_q), (3, load_x), (0, store))
                sp.wait_ge(x2_stored, 16 * NT)

            @block.gpsimd
            def _(pool):
                pool.sem_inc(x2_set, 4)
                pool.memset(kv_heads[:, :, :], 0.0).then_inc(heads_zeroed, 1)
                pool.wait_ge(k_all_set, 1)
                pool.wait_ge(biases_loaded, 32)

                def times_k(t, b):
                    pool.wait_ge(q_loaded[b], (t - b) * 4 + 16)
                    pool.wait_ge(den_step, 3 * t + 1)
                    settle(pool, "pool")
                    pool.tensor_tensor(qk[b % 2][:, :], q[b][:, :], k_all[:, :], ALU.mult).then_inc(qk_set, 1)

                def add_bias(t, b):
                    pool.wait_ge(x_loaded[b], (t - b) * 4 + 16)
                    pool.tensor_tensor(x_rows[b][:, :], x_rows[b][:, :], b_proj_rows[:, :], ALU.add
                                       ).then_inc(x_biased, 1)

                def add_up(t, b):
                    pool.wait_ge(g_set, t + 2)
                    settle(pool, "pool")
                    pool.tensor_tensor(acc[:, t, :], x_rows[b][:, :], g[b % 2][:, :], ALU.add).then_inc(x2_set, 1)

                staggered(pool, (3, times_k), (2, add_bias), (0, add_up))

            @block.tensor
            def _(pe):
                pe.matmul(ps_a[:, :], ones[:, :], k_sum[:, :], start=True, stop=True).then_inc(k_all_summed, 1)
                pe.wait_ge(proj_loaded, 16)
                for r in range(C):
                    pe.wait_ge(proj_copied, r) if r else None
                    turn(pe, ps_q, proj_rows[:, r, :], ident[:, :]).then_inc(proj_turned, 1)
                pe.wait_ge(heads_set, 1)
                pe.wait_ge(proj_copied, C)
                for c in range(C):
                    if c >= 2:
                        pe.wait_ge(mixer_lo_set, c - 1)
                    pe.matmul(ps_mix[c % 2][:, :], kv_heads[:, c, :], proj_t[:, c, :], start=True, stop=True
                              ).then_inc(mixer_summed, 1)
                pe.wait_ge(mixer_lo_set, C)
                pe.wait_ge(gnn_lo_set, 1)
                pe.wait_ge(k_all_set, 1)

                pe.sem_inc(turned, 8)

                def turn_both(t, b):
                    pe.wait_ge(q_divided, t + 1)
                    pe.wait_ge(lo_set, 2 * t + 1)
                    turn(pe, ps_q, q[b], ident[:, :]).then_inc(turned, 1)
                    pe.wait_ge(a_set, t + 1)
                    turn(pe, ps_a, a_rows, ident[:, :]).then_inc(turned, 1)

                def multiply(t, b):
                    pe.wait_ge(lo_set, 2 * t + 2)
                    product(pe, ps_mix[b % 2][:, :], q_t[b % 2], mixer).then_inc(mixed, 1)
                    pe.wait_ge(lo_set, 2 * t + 3)
                    product(pe, ps_gnn[b % 2][:, :], a_t[b % 2], gnn_w).then_inc(gnn_done, 1)

                staggered(pe, (1, turn_both), (0, multiply))

            @block.scalar
            def _(act):
                act.wait_ge(gnn_loaded, 16)
                act.copy(gnn_w[0][:, :, :], gnn_raw[:, :, :]).then_inc(gnn_hi_set, 1)
                for c in range(C):
                    act.wait_ge(mixer_summed, c + 1)
                    act.copy(mixer[0][:, c, :], ps_mix[c % 2][:, :]).then_inc(mixer_hi_set, 1)

                def high_parts(t, b):
                    for n, (banked, parts) in enumerate(((ps_q, q_t[b % 2]), (ps_a, a_t[b % 2]))):
                        act.wait_ge(turned, 2 * t + n + 9)
                        act.copy(parts[0][:, :, :].rearrange("p c n -> p (c n)"), banked[:, :]).then_inc(hi_set, 1)

                def scale_sum(t, b):
                    act.activation(a_rows[:, :], acc[:, t, :], ACT.Copy, scale=dinv_down[:, bass.ds(t, 1)]
                                   ).then_inc(a_set, 1)

                staggered(act, (1, high_parts), (2, scale_sum))

            @block.vector
            def _(dve):
                dve.sem_inc(lo_set, 1)
                dve.sem_inc(den_step, 4)
                dve.sem_inc(g_set, 1)
                dve.wait_ge(k_all_summed, 1)
                dve.tensor_copy(k_all[:, :], ps_a[:, :]).then_inc(k_all_set, 1)
                dve.wait_ge(heads_zeroed, 1)
                for c in range(C):
                    for n in range(P // DH):
                        rows, cols = slice(n * DH, (n + 1) * DH), slice(c * P + n * DH, c * P + (n + 1) * DH)
                        last = dve.tensor_copy(kv_heads[rows, c, rows], kv[rows, cols])
                last.then_inc(heads_set, 1)
                for r in range(C):
                    dve.wait_ge(proj_turned, r + 1)
                    dve.tensor_copy(proj_t[:, :, r * P:(r + 1) * P], ps_q[:, :].rearrange("p (c o) -> p c o", c=C)
                                    ).then_inc(proj_copied, 1)
                dve.wait_ge(gnn_hi_set, 1)
                dve.tensor_tensor(gnn_w[1][:, :, :], gnn_raw[:, :, :], gnn_w[0][:, :, :].bitcast(F32), ALU.subtract
                                  ).then_inc(gnn_lo_set, 1)
                for c in range(C):
                    dve.wait_ge(mixer_hi_set, c + 1)
                    dve.tensor_tensor(mixer[1][:, c, :], ps_mix[c % 2][:, :], mixer[0][:, c, :].bitcast(F32),
                                      ALU.subtract).then_inc(mixer_lo_set, 1)
                dve.wait_ge(biases_loaded, 32)

                def low_parts(t, b):
                    for n, (banked, parts) in enumerate(((ps_q, q_t[b % 2]), (ps_a, a_t[b % 2]))):
                        dve.wait_ge(hi_set, 2 * t + n + 1)
                        dve.tensor_tensor(parts[1][:, :, :].rearrange("p c n -> p (c n)"), banked[:, :],
                                          parts[0][:, :, :].bitcast(F32).rearrange("p c n -> p (c n)"), ALU.subtract
                                          ).then_inc(lo_set, 1)

                def divide(t, b):
                    dve.wait_ge(qk_set, t + 1)
                    dve.tensor_reduce(den[:, :], qk[b % 2][:, :].rearrange("p (h d) -> p h d", h=H), AX_X, ALU.add
                                      ).then_inc(den_step, 1)
                    dve.wait_ge(den_step, 3 * t + 5)
                    dve.tensor_scalar(den_eps[:, :], den[:, :], DIV_EPS, None, ALU.add).then_inc(den_step, 1)
                    dve.wait_ge(den_step, 3 * t + 6)
                    dve.reciprocal(den_inv[:, :], den_eps[:, :]).then_inc(den_step, 1)
                    dve.wait_ge(den_step, 3 * t + 7)
                    dve.tensor_tensor(q[b][:, :].rearrange("p (h d) -> p h d", h=H),
                                      q[b][:, :].rearrange("p (h d) -> p h d", h=H),
                                      den_inv[:, :].rearrange("p (h a) -> p h a", a=1).broadcast_to([P, H, DH]),
                                      ALU.mult).then_inc(q_divided, 1)

                def add_products(t, b):
                    dve.wait_ge(mixed, t + 1)
                    dve.wait_ge(x_biased, t + 1)
                    dve.tensor_tensor(x_rows[b][:, :], x_rows[b][:, :], ps_mix[b % 2][:, :], ALU.add).then_inc(h_step, 1)
                    dve.wait_ge(gnn_done, t + 1)
                    dve.wait_ge(g_set, t + 1)
                    dve.tensor_tensor(h[:, :], ps_gnn[b % 2][:, :], b_gnn_rows[:, :], ALU.add).then_inc(h_step, 1)
                    dve.wait_ge(h_step, 2 * t + 2)
                    dve.wait_ge(x2_set, t + 3)
                    dve.scalar_tensor_tensor(g[b % 2][:, :], h[:, :], SLOPE, h[:, :], ALU.mult, ALU.max).then_inc(g_set, 1)

                staggered(dve, (1, low_parts), (2, divide), (0, add_products))


def route(nc, sb_in, right_in, ps_in, sem, turns, settle, acc, ident, w_gate, w1, sorted_rows,
          expert_rows):
    keep = right_in
    w1_t = [keep(f"w1_{n}", [P, C, NEXP * FF], F32R) for n in ("hi", "lo")]
    place = keep("place", [P, NT, 2], I32)
    top_w = keep("top_w", [P, 2, NT], F32)
    pair_expert = keep("pair_expert", [1, PAIRS + 1], I32)
    pair_count = keep("pair_count", [1, 1], I32)
    scope = ExitStack()
    with scope:
        sb, ps = sb_in(scope), ps_in(scope)
        gate = sb("gate", [P, C, NEXP], F32)
        raw = sb("w1_raw", [P, 2 * D], F32)
        zeros = sb("zero_rows", [P, D], F32)
        stats = sb("stats_d", [P, NT, 6], F32)
        mean, rstd, var_eps, half_a, half_b, half_c, minus_half = (
            sb(f"{n}_d", [P, NT], F32) for n in ("mean", "rstd", "var_eps", "half_a", "half_b", "half_c", "minus_half"))
        xn = [sb(f"xn_d{b}", [P, D], F32) for b in (0, 1)]
        xn_t = [sb(f"xn_t_d{b}", [P, C, P], F32) for b in (0, 1)]
        table8 = [P, NT, NEXP]
        logits, rest, mark, first, second = (sb(n, table8, F32) for n in ("logits", "rest", "mark", "first", "second"))
        picked = sb("picked", table8, BF16)
        total, sum_a, sum_b, rank = (sb(n, table8, F32) for n in ("total", "sum_a", "sum_b", "rank"))
        best, best_no, next_best, next_no, gap, squashed = (
            sb(n, [P, NT], F32) for n in ("best", "best_no", "next_best", "next_no", "gap", "squashed"))
        falling = sb("falling", [P, NEXP], F32)
        pair_no = sb("pair_no", [1, PAIRS + 1], F32)
        reached = sb("reached", [1, PAIRS + 1, NEXP], F32)
        expert_f = sb("expert_f", [1, PAIRS + 1], F32)
        place_f = sb("place_f", [P, NT, 2], F32)
        e8 = [P, NEXP]
        pairs_i, pairs_j = sb("pairs_i", e8, I32), sb("pairs_j", e8, I32)
        pairs, ends_a, ends_b, starts = (sb(n, e8, F32) for n in ("pairs", "ends_a", "ends_b", "starts"))
        zero_from_f, zero_from = sb("zero_from_f", [1, NEXP + 1], F32), sb("zero_from", [1, NEXP + 1], I32)
        rest_count = sb("rest_count", [1, 1], I32)
        before_b = sb("before_b", [P, P], BF16)
        ones_b = sb("ones_b", [P, P], BF16)
        ps_x = [ps(f"ps_x{b}", [P, 512]) for b in (0, 1)]
        ps_gate, ps_rank, ps_total = ps("ps_gate", [P, 512]), ps("ps_rank", [P, 512]), ps("ps_total", [P, 512])

        (gate_loaded, raw_loaded, zeroed, const_set, w1_hi_set, w1_lo_set, stats_set, moment_step, var_set, root_set,
         xn_set, x_turned, x_copied, acc_set, gated, route_step, gap_set, squashed_set, picked_set, ranked,
         zero_from_set, place_set, scattered, rest_zeroed) = (sem(n) for n in (
             "gate_loaded", "w1_raw_loaded", "zeroed", "const_set_d", "w1_hi_set", "w1_lo_set", "stats_set_d",
             "moment_step_d", "var_set_d", "root_set_d", "xn_set_d", "x_turned_d", "x_copied_d", "acc_set_d", "gated",
             "route_step", "gap_set", "squashed_set", "picked_set", "ranked", "zero_from_set", "place_set", "scattered",
             "rest_zeroed"))

        with nc.Block() as block:

            @block.sync
            def _(sp):
                sp.dma_start(gate[:, :, :], w_gate.rearrange("(c p) e -> p c e", p=P)).then_inc(gate_loaded, 16)
                with sp.Fori(0, NEXP) as e:
                    sp.wait_ge(w1_lo_set, e + 1)
                    sp.dma_start(raw[:, :].rearrange("p (c f) -> p c f", c=C),
                                 w1[bass.ds(e, 1)].rearrange("e (c p) f -> p (e c) f", p=P)).then_inc(raw_loaded, 16)
                sp.wait_ge(zero_from_set, 1)
                sp.wait_ge(const_set, 1)
                settle(sp, "sp")
                zero_pair = zeros[:, :].rearrange("p (a d) -> p a d", a=1).broadcast_to([P, 2, D])
                for e in range(NEXP + 1):
                    row = sp.value_load(zero_from[0:1, e:e + 1], min_val=0, max_val=PAIRS * 2 * P)
                    sp.dma_start(sorted_rows[bass.ds(row, 2 * P), :].rearrange("(t p) d -> p t d", p=P), zero_pair
                                 ).then_inc(zeroed, 16)
                sp.wait_ge(zeroed, 16 * (NEXP + 1))
                count = sp.value_load(pair_count[0:1, 0:1], min_val=1, max_val=PAIRS)
                with sp.Fori(count, PAIRS + 1) as pair:
                    sp.dma_start(expert_rows[bass.ds(pair * 2 * P, 2 * P), :].rearrange("(t p) d -> p t d", p=P),
                                 zero_pair).then_inc(rest_zeroed, 16)
                sp.wait_ge(rest_zeroed, sp.value_load(rest_count[0:1, 0:1], min_val=16, max_val=16 * PAIRS))
                settle(sp, "sp")

            @block.gpsimd
            def _(pool):
                pool.sem_inc(w1_lo_set, 1)
                pool.memset(zeros[:, :], 0.0).then_inc(const_set, 1)
                pool.memset(minus_half[:, :], -0.5).then_inc(const_set, 1)
                pool.memset(ones_b[:, :], 1.0).then_inc(const_set, 1)
                pool.iota(falling[:, :], [[-1, NEXP]], base=NEXP, channel_multiplier=0,
                          allow_small_or_imprecise_dtypes=True).then_inc(const_set, 1)
                pool.iota(pair_no[:, :], [[1, PAIRS + 1]], base=0, channel_multiplier=0,
                          allow_small_or_imprecise_dtypes=True).then_inc(const_set, 1)
                pool.wait_ge(const_set, 5)
                pool.affine_select(out=before_b[:, :], in_=ones_b[:, :], compare_op=ALU.is_gt, fill=0.0,
                                   base=0, pattern=[[1, P]], channel_multiplier=-1).then_inc(const_set, 1)
                pool.wait_ge(var_set, 1)
                pool.tensor_tensor(rstd[:, :], var_eps[:, :], minus_half[:, :], ALU.pow).then_inc(root_set, 1)
                with pool.Fori(0, NEXP) as e:
                    pool.wait_ge(w1_hi_set, e + 1)
                    settle(pool, "pool")
                    cols = bass.ds(e * FF, FF)
                    pool.tensor_tensor(w1_t[1][:, :, cols], raw[:, :].rearrange("p (c f) -> p c f", c=C),
                                       w1_t[0][:, :, cols].bitcast(F32), ALU.subtract).then_inc(w1_lo_set, 1)
                pool.wait_ge(zeroed, 16 * (NEXP + 1))
                pool.wait_ge(place_set, 1)
                pool.wait_ge(acc_set, NT + 2)
                for t in range(NT):
                    for n in (0, 1):
                        pool.indirect_dma_start(sorted_rows, bass.IndirectOffsetOnAxis(place[:, t, n:n + 1], 0),
                                                acc[:, t, :], None).then_inc(scattered, 16)
                pool.wait_ge(scattered, 16 * 2 * NT)

            @block.tensor
            def _(pe):
                pe.wait_ge(gate_loaded, 16)

                def start(t, b):
                    pe.wait_ge(xn_set, t + 1)
                    pe.wait_ge(x_copied, t + 1)
                    turn(pe, ps_x[b], xn[b], ident[:, :]).then_inc(x_turned, 1)

                def finish(t, b):
                    pe.wait_ge(x_copied, t + 3)
                    settle(pe, "pe")
                    for c in range(C):
                        last = pe.matmul(ps_gate[:, bass.ds(t * NEXP, NEXP)], xn_t[b][:, c, :], gate[:, c, :],
                                         start=c == 0, stop=c == C - 1)
                    last.then_inc(gated, 1)

                node_tiles_ahead(pe, start, finish)
                pe.wait_ge(picked_set, 1)
                pe.wait_ge(const_set, 6)
                these = picked[:, :, :].rearrange("p t e -> p (t e)")
                pe.matmul(ps_total[:, 0:NT * NEXP], ones_b[:, :], these, start=True, stop=True).then_inc(ranked, 1)
                pe.matmul(ps_rank[:, 0:NT * NEXP], before_b[:, :], these, start=True, stop=True).then_inc(ranked, 1)

            @block.scalar
            def _(act):
                act.sem_inc(x_copied, 2)
                act.sem_inc(acc_set, 2)
                with act.Fori(0, NEXP) as e:
                    act.wait_ge(raw_loaded, 16 * e + 16)
                    settle(act, "act")
                    act.copy(w1_t[0][:, :, bass.ds(e * FF, FF)], raw[:, :].rearrange("p (c f) -> p c f", c=C)
                             ).then_inc(w1_hi_set, 1)

                def start(t, b):
                    act.wait_ge(x_turned, t + 1)
                    act.wait_ge(gated, t + 1)
                    act.copy(xn_t[b][:, :, :].rearrange("p c n -> p (c n)"), ps_x[b][:, :]).then_inc(x_copied, 1)
                    act.copy(acc[:, t, :], xn[b][:, :]).then_inc(acc_set, 1)

                node_tiles(act, lambda t, b, j: start(t, b))
                act.wait_ge(gap_set, 1)
                act.activation(squashed[:, :], gap[:, :], ACT.Tanh, scale=0.5).then_inc(squashed_set, 1)

            @block.vector
            def _(dve):
                dve.sem_inc(gated, 2)
                with dve.Fori(0, NT) as t:
                    dve.bn_stats(stats[:, t, :], acc[:, t, :]).then_inc(stats_set, 1)
                dve.wait_ge(stats_set, NT)
                count = {"moment": 0, "route": 0}

                def moment(ins):
                    ins.then_inc(moment_step, 1)
                    count["moment"] += 1

                even, odd = stats[:, :, 1], stats[:, :, 4]
                moment(dve.tensor_tensor(half_a[:, :], even, odd, ALU.add))
                moment(dve.tensor_tensor(half_b[:, :], even, odd, ALU.subtract))
                moment(dve.tensor_tensor(half_c[:, :], stats[:, :, 2], stats[:, :, 5], ALU.add))
                dve.wait_ge(moment_step, count["moment"])
                moment(dve.tensor_scalar(mean[:, :], half_a[:, :], 0.5, None, ALU.mult))
                moment(dve.scalar_tensor_tensor(rest[:, :, 0], half_b[:, :], 0.25, half_b[:, :], ALU.mult, ALU.mult))
                moment(dve.tensor_scalar(rest[:, :, 1], half_c[:, :], 1.0 / D, LN_EPS, ALU.mult, ALU.add))
                dve.wait_ge(moment_step, count["moment"])
                dve.tensor_tensor(var_eps[:, :], rest[:, :, 0], rest[:, :, 1], ALU.add).then_inc(var_set, 1)
                dve.wait_ge(root_set, 1)

                def normalise(t, b, j):
                    dve.wait_ge(acc_set, t + 1)
                    dve.tensor_scalar(xn[b][:, :], acc[:, t, :], mean[:, bass.ds(t, 1)], rstd[:, bass.ds(t, 1)],
                                      ALU.subtract, ALU.mult).then_inc(xn_set, 1)

                node_tiles(dve, normalise)

                def step(ins):
                    ins.then_inc(route_step, 1)
                    count["route"] += 1
                    dve.wait_ge(route_step, count["route"])

                def wide(x):
                    if x.shape[1] == NT:
                        return x.rearrange("p (t a) -> p t a", a=1).broadcast_to(table8)
                    return x.rearrange("p (a e) -> p a e", a=1).broadcast_to(table8)

                def pick(values, top, number, one_hot):
                    step(dve.tensor_reduce(top[:, :], values[:, :, :], AX_X, ALU.max))
                    step(dve.tensor_tensor(mark[:, :, :], values[:, :, :], wide(top[:, :]), ALU.is_equal))
                    step(dve.tensor_tensor(mark[:, :, :], mark[:, :, :], wide(falling[:, :]), ALU.mult))
                    step(dve.tensor_reduce(number[:, :], mark[:, :, :], AX_X, ALU.max))
                    step(dve.tensor_tensor(one_hot[:, :, :], wide(falling[:, :]), wide(number[:, :]), ALU.is_equal))

                dve.wait_ge(gated, NT + 2)
                dve.wait_ge(const_set, 6)
                step(dve.tensor_copy(logits[:, :, :], ps_gate[:, 0:NT * NEXP].rearrange("p (t e) -> p t e", e=NEXP)))
                pick(logits, best, best_no, first)
                step(dve.scalar_tensor_tensor(rest[:, :, :], first[:, :, :], LOWEST, logits[:, :, :], ALU.mult, ALU.add))
                pick(rest, next_best, next_no, second)
                dve.tensor_tensor(picked[:, :, :], first[:, :, :], second[:, :, :], ALU.add).then_inc(picked_set, 1)
                dve.tensor_tensor(gap[:, :], best[:, :], next_best[:, :], ALU.subtract).then_inc(gap_set, 1)
                dve.wait_ge(ranked, 2)
                step(dve.tensor_copy(total[:, :, :], ps_total[:, 0:NT * NEXP].rearrange("p (t e) -> p t e", e=NEXP)))

                def running_sum(source, buffers, n):
                    reach, k = 1, 0
                    while reach < n:
                        to = buffers[k % 2]
                        step(dve.tensor_copy(to[:, 0:reach], source[:, 0:reach]))
                        step(dve.tensor_tensor(to[:, reach:n], source[:, reach:n], source[:, 0:n - reach], ALU.add))
                        source, reach, k = to, 2 * reach, k + 1
                    return source

                sums = running_sum(total, (sum_a, sum_b), NT)
                step(dve.tensor_scalar(pairs_i[:, :], sums[:, NT - 1, :], 2.0 * P - 1, None, ALU.add))
                step(dve.tensor_single_scalar(pairs_j[:, :], pairs_i[:, :], 8, ALU.arith_shift_right))
                step(dve.tensor_copy(pairs[:, :], pairs_j[:, :]))
                step(dve.tensor_scalar(pairs[:, :], pairs[:, :], 1.0, None, ALU.max))
                ends = running_sum(pairs, (ends_a, ends_b), NEXP)
                step(dve.tensor_scalar(zero_from_f[:, 0:NEXP], ends[0:1, :], -1.0, 2.0 * P, ALU.add, ALU.mult))
                step(dve.tensor_scalar(zero_from_f[:, NEXP:], ends[0:1, NEXP - 1:], 2.0 * P, None, ALU.mult))
                step(dve.tensor_copy(pair_count[:, :], ends[0:1, NEXP - 1:]))
                step(dve.tensor_scalar(rest_count[:, :], ends[0:1, NEXP - 1:], -16.0, 16.0 * (PAIRS + 1), ALU.mult, ALU.add))
                dve.tensor_copy(zero_from[:, :], zero_from_f[:, :]).then_inc(zero_from_set, 1)
                step(dve.tensor_tensor(starts[:, :], ends[:, :], pairs[:, :], ALU.subtract))
                step(dve.tensor_scalar(starts[:, :], starts[:, :], 2.0 * P, None, ALU.mult))
                step(dve.tensor_tensor(rank[:, :, :], sums[:, :, :], total[:, :, :], ALU.subtract))
                step(dve.tensor_tensor(rank[:, :, :], rank[:, :, :], wide(starts[:, :]), ALU.add))
                step(dve.tensor_tensor(rank[:, :, :], rank[:, :, :],
                                       ps_rank[:, 0:NT * NEXP].rearrange("p (t e) -> p t e", e=NEXP), ALU.add))
                for n, one_hot in enumerate((first, second)):
                    step(dve.tensor_tensor(mark[:, :, :], one_hot[:, :, :], rank[:, :, :], ALU.mult))
                    step(dve.tensor_reduce(place_f[:, :, n], mark[:, :, :], AX_X, ALU.add))
                dve.tensor_copy(place[:, :, :], place_f[:, :, :]).then_inc(place_set, 1)
                dve.wait_ge(squashed_set, 1)
                dve.tensor_scalar(top_w[:, 0, :], squashed[:, :], 0.5, 0.5, ALU.mult, ALU.add)
                dve.tensor_scalar(top_w[:, 1, :], squashed[:, :], -0.5, 0.5, ALU.mult, ALU.add)
                wide_pairs = [1, PAIRS + 1, NEXP]
                step(dve.tensor_tensor(reached[:, :, :], pair_no[:, :].rearrange("p (g a) -> p g a", a=1).broadcast_to(wide_pairs),
                                       ends[0:1, :].rearrange("p (a e) -> p a e", a=1).broadcast_to(wide_pairs), ALU.is_ge))
                step(dve.tensor_reduce(expert_f[:, :], reached[:, :, :], AX_X, ALU.add))
                step(dve.tensor_scalar(pair_expert[:, :], expert_f[:, :], NEXP - 1.0, None, ALU.min))
    return w1_t, place, top_w, pair_expert, pair_count


def experts(nc, sb_in, ps_in, sem, turns, settle, ident, x2_rows, sorted_rows, expert_rows, w1_t, place, top_w,
            pair_expert, pair_count, w2, out):
    scope = ExitStack()
    with scope:
        sb, ps = sb_in(scope), ps_in(scope)
        FC = FF // P
        w2_t = [sb(f"w2_{n}", [P, NEXP * FC, D], F32R) for n in ("hi", "lo")]
        raw = [sb(f"w2_raw{b}", [P, FC * D], F32) for b in (0, 1)]
        rows = sb("rows", [P, 2, D], F32)
        x_t = [[sb(f"x_t{n}{m}", [P, C, P], F32R) for m in ("hi", "lo")] for n in (0, 1)]
        s = [sb(f"s{n}", [P, FF], F32) for n in (0, 1)]
        s_t = [[sb(f"s_t{n}{m}", [P, FC, P], F32R) for m in ("hi", "lo")] for n in (0, 1)]
        y = sb("y", [P, 2, D], F32)
        place_now = [sb(f"place_now{b}", [P, 4], I32) for b in (0, 1)]
        chosen = [sb(f"chosen{b}", [P, 2, 2, D], F32) for b in (0, 1)]
        x2 = [sb(f"x2_e{b}", [P, 2, D], F32) for b in (0, 1)]
        out_rows = [sb(f"out_rows{b}", [P, 2, D], F32) for b in (0, 1)]
        ps_x = [ps(f"ps_x_e{n}", [P, 512]) for n in (0, 1)]
        ps_h = [ps(f"ps_h{n}", [P, 512]) for n in (0, 1)]
        ps_s = [ps(f"ps_s{n}", [P, 512]) for n in (0, 1)]
        ps_y = [ps(f"ps_y{n}", [P, 512]) for n in (0, 1)]

        raw_loaded = [sem(f"w2_raw_loaded{b}") for b in (0, 1)]
        w2_hi_set, w2_lo_set, rows_loaded = sem("w2_hi_set"), sem("w2_lo_set"), sem("rows_loaded")
        x_turned, x_hi_set, x_lo_set = sem("x_turned_e"), sem("x_hi_set_e"), sem("x_lo_set_e")
        h_ready, s_set, s_turned, s_hi_set, s_lo_set = (
            sem(n) for n in ("h_ready", "s_set", "s_turned", "s_hi_set", "s_lo_set"))
        y_ready, y_stored = sem("y_ready"), sem("y_stored")
        y_set = [sem(f"y_set{n}") for n in (0, 1)]
        place_copied, combined = sem("place_copied"), sem("combined")
        chosen_loaded = [sem(f"chosen_loaded{b}") for b in (0, 1)]
        x2_loaded = [sem(f"x2_loaded_e{b}") for b in (0, 1)]
        part_set, out_stored = sem("part_set"), [sem(f"out_stored{b}") for b in (0, 1)]

        def pairs_of(eng):
            return eng.value_load(pair_count[0:1, 0:1], min_val=1, max_val=PAIRS)

        with nc.Block() as block:

            @block.sync
            def _(sp):
                def load(pair):
                    sp.dma_start(rows[:, :, :], sorted_rows[bass.ds(pair * 2 * P, 2 * P), :]
                                 .rearrange("(t p) d -> p t d", p=P)).then_inc(rows_loaded, 16)

                load(0)
                for e in range(NEXP):
                    if e >= 2:
                        sp.wait_ge(w2_lo_set, e - 1)
                    sp.dma_start(raw[e % 2][:, :].rearrange("p (c d) -> p c d", c=FC),
                                 w2[e].rearrange("(c p) d -> p c d", p=P)).then_inc(raw_loaded[e % 2], 16)
                with sp.Fori(0, pairs_of(sp)) as g:
                    sp.wait_ge(x_turned, 2 * g + 2)
                    load(g + 1)

                def load_x2(u, tiles, b):
                    sp.wait_ge(combined, u + 1)
                    sp.dma_start(x2[b][:, 0:tiles, :], x2_rows[bass.ds(2 * u * P, tiles * P), :]
                                 .rearrange("(t p) d -> p t d", p=P)).then_inc(x2_loaded[b], 16)

                tile_pairs(sp, load_x2)

            @block.gpsimd
            def _(pool):
                pool.wait_ge(y_stored, 16 * pairs_of(pool) + 16)
                settle(pool, "pool")

                def choose(u, tiles, b):
                    pool.wait_ge(combined, u + 1)
                    settle(pool, "pool")
                    pool.tensor_copy(place_now[b][:, 0:2 * tiles].rearrange("p (t n) -> p t n", n=2),
                                     place[:, bass.ds(2 * u, tiles), :]).then_inc(place_copied, 1)
                    pool.wait_ge(place_copied, u + 1)
                    settle(pool, "pool")
                    for n in range(2 * tiles):
                        pool.indirect_dma_start(chosen[b][:, n // 2, n % 2, :], None, expert_rows,
                                                bass.IndirectOffsetOnAxis(place_now[b][:, n:n + 1], 0)
                                                ).then_inc(chosen_loaded[b], 16)

                tile_pairs(pool, choose)

            @block.tensor
            def _(pe):
                def turn_rows(g, n):
                    pe.wait_ge(rows_loaded, 16 * g + 16)
                    turn(pe, ps_x[n], rows[:, n, :], ident[:, :]).then_inc(x_turned, 1)

                turn_rows(0, 0)
                turn_rows(0, 1)
                pe.wait_ge(w2_lo_set, NEXP)
                with pe.Fori(0, pairs_of(pe)) as g:
                    e = pe.value_load(pair_expert[0:1, bass.ds(g, 1)], min_val=0, max_val=NEXP - 1)
                    w1_e = [w[:, :, bass.ds(e * FF, FF)] for w in w1_t]
                    w2_e = [w[:, bass.ds(e * FC, FC), :] for w in w2_t]
                    for n in (0, 1):
                        pe.wait_ge(x_lo_set, 2 * g + n + 1)
                        settle(pe, "pe")
                        product(pe, ps_h[n][:, 0:FF], x_t[n], w1_e).then_inc(h_ready, 1)
                    for n in (0, 1):
                        pe.wait_ge(s_set, 2 * g + n + 1)
                        turn(pe, ps_s[n], s[n], ident[:, :], FC).then_inc(s_turned, 1)
                        turn_rows(g + 1, n)
                    for n in (0, 1):
                        pe.wait_ge(s_lo_set, 2 * g + n + 1)
                        pe.wait_ge(y_set[n], g + 1)
                        settle(pe, "pe")
                        product(pe, ps_y[n][:, :], s_t[n], w2_e, chunks=FC).then_inc(y_ready, 1)

            @block.scalar
            def _(act):
                act.sem_inc(y_stored, 16)
                act.sem_inc(out_stored[0], 16)
                act.sem_inc(out_stored[1], 16)

                def high_x(g, n):
                    act.wait_ge(x_turned, 2 * g + n + 1)
                    act.copy(x_t[n][0][:, :, :].rearrange("p c r -> p (c r)"), ps_x[n][:, :]).then_inc(x_hi_set, 1)

                high_x(0, 0)
                high_x(0, 1)
                for e in range(NEXP):
                    act.wait_ge(raw_loaded[e % 2], 16 * (e // 2) + 16)
                    act.copy(w2_t[0][:, e * FC:(e + 1) * FC, :].rearrange("p c d -> p (c d)"), raw[e % 2][:, :]
                             ).then_inc(w2_hi_set, 1)
                with act.Fori(0, pairs_of(act)) as g:
                    for n in (0, 1):
                        act.wait_ge(h_ready, 2 * g + n + 1)
                        act.activation(s[n][:, :], ps_h[n][:, 0:FF], ACT.Silu).then_inc(s_set, 1)
                    for n in (0, 1):
                        act.wait_ge(s_turned, 2 * g + n + 1)
                        act.copy(s_t[n][0][:, :, :].rearrange("p c r -> p (c r)"), ps_s[n][:, 0:FF]).then_inc(s_hi_set, 1)
                        high_x(g + 1, n)
                    act.wait_ge(y_ready, 2 * g + 1)
                    act.wait_ge(y_stored, 16 * g + 16)
                    act.copy(y[:, 0, :], ps_y[0][:, :]).then_inc(y_set[0], 1)
                    act.wait_ge(y_set[0], g + 2)
                    act.wait_ge(y_set[1], g + 2)
                    act.dma_start(expert_rows[bass.ds(g * 2 * P, 2 * P), :].rearrange("(t p) d -> p t d", p=P),
                                  y[:, :, :]).then_inc(y_stored, 16)

                def store(u, tiles, b):
                    act.wait_ge(combined, u + 3)
                    r = LAST if tiles == 1 else P
                    act.dma_start(out[bass.ds(2 * u * P, (tiles - 1) * P + r), :].rearrange("(t p) d -> p t d", p=r),
                                  out_rows[b][0:r, 0:tiles, :]).then_inc(out_stored[b], 16)

                tile_pairs(act, store)
                act.wait_ge(out_stored[0], 16 * (NT // 4 + 2))
                act.wait_ge(out_stored[1], 16 * (NT // 4 + 1))

            @block.vector
            def _(dve):
                dve.sem_inc(combined, 2)
                dve.sem_inc(y_set[0], 1)
                dve.sem_inc(y_set[1], 1)

                def low_x(g, n):
                    dve.wait_ge(x_hi_set, 2 * g + n + 1)
                    dve.tensor_tensor(x_t[n][1][:, :, :].rearrange("p c r -> p (c r)"), ps_x[n][:, :],
                                      x_t[n][0][:, :, :].bitcast(F32).rearrange("p c r -> p (c r)"), ALU.subtract
                                      ).then_inc(x_lo_set, 1)

                low_x(0, 0)
                low_x(0, 1)
                for e in range(NEXP):
                    dve.wait_ge(w2_hi_set, e + 1)
                    these = slice(e * FC, (e + 1) * FC)
                    dve.tensor_tensor(w2_t[1][:, these, :], raw[e % 2][:, :].rearrange("p (c d) -> p c d", c=FC),
                                      w2_t[0][:, these, :].bitcast(F32), ALU.subtract).then_inc(w2_lo_set, 1)
                with dve.Fori(0, pairs_of(dve)) as g:
                    for n in (0, 1):
                        dve.wait_ge(s_hi_set, 2 * g + n + 1)
                        dve.tensor_tensor(s_t[n][1][:, :, :].rearrange("p c r -> p (c r)"), ps_s[n][:, 0:FF],
                                          s_t[n][0][:, :, :].bitcast(F32).rearrange("p c r -> p (c r)"), ALU.subtract
                                          ).then_inc(s_lo_set, 1)
                        low_x(g + 1, n)
                    dve.wait_ge(y_ready, 2 * g + 2)
                    dve.wait_ge(y_stored, 16 * g + 16)
                    dve.tensor_scalar(y[:, 1, :], ps_y[1][:, :], 1.0, None, ALU.mult).then_inc(y_set[1], 1)

                def combine(u, tiles, b):
                    dve.wait_ge(x2_loaded[b], (u - b) * 8 + 16)
                    uses = (u - b) * 32
                    dve.wait_ge(chosen_loaded[b], uses + 32 * tiles)
                    for n in range(tiles):
                        for to, k, base in ((x2[b], 0, x2[b]), (out_rows[b], 1, x2[b])):
                            if k == 1 and n == 0:
                                dve.wait_ge(out_stored[b], (u - b) * 8 + 16)
                            if k == 1:
                                dve.wait_ge(part_set, 2 * u + n + 1)
                            ins = dve.scalar_tensor_tensor(to[:, n, :], chosen[b][:, n, k, :],
                                                           top_w[:, k, bass.ds(2 * u + n, 1)], base[:, n, :],
                                                           ALU.mult, ALU.add)
                            if k == 0:
                                ins.then_inc(part_set, 1)
                    ins.then_inc(combined, 1)

                tile_pairs(dve, combine)


def build(nc, x, src, dst, w_gnn, b_gnn, w_qkv, w_proj, b_proj, w_gate, w1, w2, out):
    table = nc.dram_tensor("gather_table", [NT * P, 2 * D], F16, kind="Internal").ap()
    q_rows = nc.dram_tensor("q_rows", [NT * P, D], F32, kind="Internal").ap()
    x2_rows = nc.dram_tensor("x2_rows", [NT * P, D], F32, kind="Internal").ap()
    sorted_rows = nc.dram_tensor("sorted_rows", [(PAIRS + 1) * 2 * P, D], F32, kind="Internal").ap()
    expert_rows = nc.dram_tensor("expert_rows", [(PAIRS + 1) * 2 * P, D], F32, kind="Internal").ap()
    window_rows = nc.dram_tensor("window_rows", [2 * NG], I32, kind="Internal").ap()
    everything = ExitStack()
    with everything:
        def sem(name):
            return everything.enter_context(nc.semaphore(name))

        def sb_in(scope):
            return lambda name, shape, dt: scope.enter_context(nc.sbuf_tensor(name, shape, dt))

        def ps_in(scope):
            return lambda name, shape: scope.enter_context(nc.psum_tensor(name, shape, F32))

        keep = sb_in(everything)
        ident = keep("ident", [P, P], F32)
        ones = keep("ones", [P, P], F32)
        mean = keep("mean", [P, NT], F32)
        rstd = keep("rstd", [P, NT], F32)
        dinv_down = keep("dinv_down", [P, NT], F32)
        real_row = keep("real_row", [P, 1], F32)

        acc_scope = everything.enter_context(ExitStack())
        acc = sb_in(acc_scope)("acc", [P, NT, D], F32)
        kv_scope = ExitStack()
        k_sum = sb_in(kv_scope)("k_sum", [P, D], F32)
        v = sb_in(kv_scope)("v", [P, D], F32)
        edge_scope = ExitStack()
        sb = sb_in(edge_scope)
        src_col = sb("src_col", [P, ET], I32)
        dst_col = sb("dst_col", [P, ET], F32)
        windows = sb("windows", [1, 2, NG], I32)
        tile_start = sb("tile_start", [P, NT], F32)
        iota = sb("iota", [P, P], BF16)
        w_t = [sb(f"w_qkv_t{n}", [P, C, 3 * D], F32R) for n in ("hi", "lo")]

        scope = ExitStack()
        with scope:
            sb, ps = sb_in(scope), ps_in(scope)
            edge_rows = [sb(f"{n}_rows", [P, ROWT * P], I32) for n in ("src", "dst")]
            edge_rows_f = [sb(f"{n}_rows_f", [P, ROWT * P], F32) for n in ("src", "dst")]
            w_ends = sb("window_ends", [P, 2, 2], F32)
            w_ends_i = sb("window_ends_i", [P, 2, 2], I32)
            w_tile_i = sb("window_tiles_i", [P, 2, 2], I32)
            w_clamped = sb("window_tiles", [P, 2, 2], I32)
            dst_i = sb("dst_i", [P, ET], I32)
            hi_i = sb("dst_tile_i", [P, ET], I32)
            dst_tile = sb("dst_tile", [P, ET], BF16)
            dst_in_tile = sb("dst_in_tile", [P, ET], BF16)
            number = sb("number", [P, P, BATCH], BF16)
            one_hot_lo = [r[:, :].bitcast(BF16).rearrange("p (n e) -> p n e", e=BATCH) for r in edge_rows]
            one_hot_hi = [sb(f"one_hot_hi{b}", [P, NT, BATCH], BF16) for b in (0, 1)]
            zeros = sb("zeros_b", [P, P], BF16)
            degree = sb("degree", [P, NT], F32)
            dinv_up = sb("dinv_up", [P, NT], F32)
            w_plain = [sb(f"w_plain{b}", [P, C, P], F32) for b in (0, 1)]
            stats = sb("stats", [P, NT, 6], F32)
            dinv, row_scale, var_eps, mean_sum, mean_gap, square_sum, gap_square, square_mean, minus_half = (
                sb(n, [P, NT], F32) for n in ("dinv", "row_scale", "var_eps", "mean_sum", "mean_gap",
                                              "square_sum", "gap_square", "square_mean", "minus_half"))
            parts = [r[:, :].bitcast(F16).rearrange("p (t a d) -> p t a d", t=2, a=2) for r in edge_rows_f]
            w_rows = [sb(f"w_rows{b}", [P, D], F32) for b in (0, 1)]
            turned = [ps(f"turned{b}", [P, 512]) for b in (0, 1)]
            ps_deg = ps("ps_deg", [P, 512])
            per = NT // XPARTS

            edges_loaded = [sem("src_loaded"), sem("dst_loaded")]
            windows_stored, windows_loaded = sem("windows_stored"), sem("windows_loaded")
            w_loaded = [sem(f"w_loaded{b}") for b in (0, 1)]
            x_loaded = [sem(f"x_loaded{n}") for n in range(XPARTS)]
            tail_zeroed, number_set = sem("tail_zeroed"), sem("number_set")
            edges_padded, consts_set = sem("edges_padded"), sem("consts_set")
            edge_step = sem("edge_step")
            edges_turned = sem("edges_turned")
            edges_copied = sem("edges_copied")
            w_turned, w_copied, w_hi_set, w_lo_set = (sem(n) for n in ("w_turned", "w_copied", "w_hi_set", "w_lo_set"))
            one_hots_built = [sem(f"one_hots_built{b}") for b in (0, 1)]
            one_hots_used = sem("one_hots_used")
            degrees_summed, degree_set, roots_set = sem("degrees_summed"), sem("degree_set"), sem("roots_set")
            stats_set, moment_step, var_set = sem("stats_set"), sem("moment_step"), sem("var_set")
            acc_set, hi_part_set, lo_part_set = sem("acc_set"), sem("hi_part_set"), sem("lo_part_set")
            parts_stored = [sem(f"parts_stored{b}") for b in (0, 1)]
            turns = {e: sem(f"{e}_turns") for e in ("pe", "act", "dve", "pool", "sp")}

            def settle(eng, name):
                eng.sem_inc(turns[name], 1)

            with nc.Block() as block:

                @block.sync
                def _(sp):
                    sp.wait_ge(edges_padded, 2)
                    for rows, col, loaded in zip(edge_rows, (src, dst), edges_loaded):
                        full = EFULL * ROWT * P
                        sp.dma_start(rows[0:EFULL, :], col[0:full].rearrange("(r e) -> r e", e=ROWT * P)
                                     ).then_inc(loaded, 16)
                        sp.dma_start(rows[EFULL:EFULL + 1, 0:EREST],
                                     col[full:E].rearrange("(r e) -> r e", r=1)).then_inc(loaded, 16)
                    sp.wait_ge(tail_zeroed, 1)
                    for n in range(XPARTS):
                        full = per - (n == XPARTS - 1)
                        sp.dma_start(acc[:, n * per:n * per + full, :],
                                     x[n * per * P:(n * per + full) * P, :].rearrange("(t p) d -> p t d", p=P)
                                     ).then_inc(x_loaded[n], 16)
                    sp.dma_start(acc[0:LAST, NT - 1, :], x[(NT - 1) * P:N, :]).then_inc(x_loaded[XPARTS - 1], 16)
                    with sp.Fori(0, NWB // 2) as j:
                        for b in (0, 1):
                            sp.wait_ge(w_turned, 2 * j + b + 1)
                            sp.dma_start(w_rows[b][:, :], w_qkv[bass.ds((2 * j + b) * P, P), :]
                                         ).then_inc(w_loaded[b], 16)
                    sp.wait_ge(edge_step, 8)
                    for side in (0, 1):
                        sp.dma_start(window_rows[side * NG:(side + 1) * NG].rearrange("(r g) -> r g", g=2),
                                     w_clamped[0:ER, side, :]).then_inc(windows_stored, 16)
                    sp.wait_ge(windows_stored, 32)
                    sp.dma_start(windows[:, :, :], window_rows.rearrange("(a s g) -> a s g", a=1, s=2)
                                 ).then_inc(windows_loaded, 16)


                    def store_parts(u, tiles, b):
                        sp.wait_ge(lo_part_set, u + 1)
                        sp.dma_start(table[bass.ds(2 * u * P, tiles * P), :].rearrange("(t p) d -> p t d", p=P),
                                     parts[b][:, 0:tiles, :, :].rearrange("p t a d -> p t (a d)")
                                     ).then_inc(parts_stored[b], 16)

                    tile_pairs(sp, store_parts)
                    sp.wait_ge(windows_loaded, 16)
                    sp.wait_ge(parts_stored[0], 16 * (NT // 4 + 2))
                    sp.wait_ge(parts_stored[1], 16 * (NT // 4 + 1))

                @block.gpsimd
                def _(pool):
                    pool.sem_inc(w_lo_set, 2)
                    pool.memset(edge_rows[0][:, :], 0).then_inc(edges_padded, 1)
                    pool.memset(edge_rows[1][:, :], PAD_DST).then_inc(edges_padded, 1)
                    pool.memset(ones[:, :], 1.0).then_inc(consts_set, 1)
                    pool.memset(zeros[:, :], 0.0).then_inc(consts_set, 1)
                    pool.iota(iota[:, :], [[1, P]], base=0, channel_multiplier=0,
                              allow_small_or_imprecise_dtypes=True).then_inc(consts_set, 1)
                    pool.iota(number[:, :, :], [[1, P], [0, BATCH]], base=0, channel_multiplier=0,
                              allow_small_or_imprecise_dtypes=True).then_inc(number_set, 1)
                    pool.iota(tile_start[:, :], [[P, NT]], base=0, channel_multiplier=0,
                              allow_small_or_imprecise_dtypes=True).then_inc(consts_set, 1)
                    pool.wait_ge(consts_set, 4)
                    pool.affine_select(out=ident[:, :], in_=ones[:, :], compare_op=ALU.is_equal, fill=0.0,
                                       base=0, pattern=[[-1, P]], channel_multiplier=1).then_inc(consts_set, 1)
                    pool.affine_select(out=real_row[:, :], in_=ones[:, 0:1], compare_op=ALU.is_gt, fill=0.0,
                                       base=LAST, pattern=[[0, 1]], channel_multiplier=-1).then_inc(consts_set, 1)
                    pool.memset(minus_half[:, :], -0.5).then_inc(consts_set, 1)
                    pool.wait_ge(consts_set, 7)
                    with pool.Fori(0, NWB // 2) as j:
                        for b in (0, 1):
                            cols = bass.ds((2 * j + b) * P, P)
                            pool.wait_ge(w_hi_set, 2 * j + b + 1)
                            settle(pool, "pool")
                            pool.tensor_tensor(w_t[1][:, :, cols], w_plain[b][:, :, :],
                                               w_t[0][:, :, cols].bitcast(F32), ALU.subtract).then_inc(w_lo_set, 1)
                    pool.wait_ge(var_set, 1)
                    pool.tensor_tensor(rstd[:, :], var_eps[:, :], minus_half[:, :], ALU.pow).then_inc(roots_set, 1)
                    pool.wait_ge(degree_set, 1)
                    pool.tensor_tensor(dinv[:, :], degree[:, :], minus_half[:, :], ALU.pow).then_inc(roots_set, 1)


                @block.tensor
                def _(pe):
                    pe.sem_inc(w_turned, 2)
                    pe.sem_inc(one_hots_used, 2)
                    pe.wait_ge(consts_set, 6)
                    n = 0
                    for k in (0, 1):
                        pe.wait_ge(edge_step, k + 1)
                        for b in range(ROWT):
                            pe.wait_ge(edges_copied, n + 1)
                            pe.transpose(turned[n % 2][:, 0:ER], edge_rows_f[k][0:ER, b * P:(b + 1) * P],
                                         ident[0:ER, 0:ER]).then_inc(edges_turned, 1)
                            n += 1
                    pe.wait_ge(edges_copied, n + 2)
                    with pe.Fori(0, NWB // 2) as j:
                        for b in (0, 1):
                            pe.wait_ge(w_loaded[b], 16 * j + 16)
                            pe.wait_ge(w_copied, 2 * j + b + 1)
                            turn(pe, turned[b], w_rows[b], ident[:, :]).then_inc(w_turned, 1)
                    pe.matmul(ps_deg[:, 0:NT], zeros[:, :], zeros[:, 0:NT], start=True, stop=False,
                              skip_group_check=True)

                    def count(t, b, j):
                        pe.wait_ge(one_hots_built[b], j + 1)
                        for e in range(BATCH):
                            last = pe.matmul(ps_deg[:, 0:NT], one_hot_lo[b][:, :, e], one_hot_hi[b][:, :, e],
                                             start=False, stop=False, skip_group_check=True)
                        last.then_inc(one_hots_used, 1)

                    node_tiles(pe, count)
                    pe.matmul(ps_deg[:, 0:NT], zeros[:, :], zeros[:, 0:NT], start=False, stop=True,
                              skip_group_check=True).then_inc(degrees_summed, 1)

                @block.scalar
                def _(act):
                    act.sem_inc(parts_stored[0], 16)
                    act.sem_inc(parts_stored[1], 16)
                    act.sem_inc(w_copied, 2)
                    with act.Fori(0, NWB // 2) as j:
                        for b in (0, 1):
                            act.wait_ge(w_turned, 2 * j + b + 3)
                            act.wait_ge(w_lo_set, 2 * j + b + 1)
                            act.copy(w_plain[b][:, :, :].rearrange("p c o -> p (c o)"), turned[b][:, :]
                                     ).then_inc(w_copied, 1)
                            act.wait_ge(w_copied, 2 * j + b + 3)
                            settle(act, "act")
                            act.copy(w_t[0][:, :, bass.ds((2 * j + b) * P, P)], w_plain[b][:, :, :]).then_inc(w_hi_set, 1)

                    def high_part(u, tiles, b):
                        act.wait_ge(acc_set, 2 * u + tiles)
                        act.wait_ge(parts_stored[b], (u - b) * 8 + 16)
                        settle(act, "act")
                        act.copy(parts[b][:, 0:tiles, 0, :], acc[:, bass.ds(2 * u, tiles), :]).then_inc(hi_part_set, 1)

                    tile_pairs(act, high_part)

                @block.vector
                def _(dve):
                    dve.memset(acc[P - DH:P, NT - 1, :], 0.0).then_inc(tail_zeroed, 1)
                    dve.sem_inc(edges_copied, 2)
                    steps = 0

                    def step(ins):
                        nonlocal steps
                        ins.then_inc(edge_step, 1)
                        steps += 1

                    def after_steps():
                        dve.wait_ge(edge_step, steps)

                    for k in (0, 1):
                        dve.wait_ge(edges_loaded[k], 32)
                        step(dve.tensor_copy(edge_rows_f[k][0:ER, :], edge_rows[k][0:ER, :]))
                    after_steps()
                    dst_groups = edge_rows_f[1][0:ER, :].rearrange("r (g e) -> r g e", g=2)
                    step(dve.tensor_reduce(w_ends[0:ER, 0, :], dst_groups, AX_X, ALU.min))
                    step(dve.tensor_reduce(w_ends[0:ER, 1, :], dst_groups, AX_X, ALU.max))
                    after_steps()
                    step(dve.tensor_copy(w_ends_i[0:ER], w_ends[0:ER]))
                    after_steps()
                    step(dve.tensor_single_scalar(w_tile_i[0:ER], w_ends_i[0:ER], 7, ALU.arith_shift_right))
                    after_steps()
                    step(dve.tensor_scalar(w_clamped[0:ER, 0, :], w_tile_i[0:ER, 0, :], NT - 1, None, ALU.min))
                    step(dve.tensor_scalar(w_clamped[0:ER, 1, :], w_tile_i[0:ER, 1, :], NT - 1, 1,
                                           ALU.min, ALU.add))
                    assert steps == 8
                    n = 0
                    for k in (0, 1):
                        col = (src_col, dst_col)[k]
                        for b in range(ROWT):
                            dve.wait_ge(edges_turned, n + 1)
                            dve.tensor_copy(col[:, b:ET:ROWT], turned[n % 2][:, 0:ER]).then_inc(edges_copied, 1)
                            n += 1
                    dve.wait_ge(edges_copied, n + 2)
                    step(dve.tensor_copy(dst_i[:, :], dst_col[:, :]))
                    after_steps()
                    step(dve.tensor_single_scalar(hi_i[:, :], dst_i[:, :], 7, ALU.arith_shift_right))
                    after_steps()
                    step(dve.tensor_copy(dst_tile[:, :], hi_i[:, :]))
                    after_steps()
                    step(dve.scalar_tensor_tensor(dst_in_tile[:, :], dst_tile[:, :], -float(P), dst_col[:, :],
                                                  ALU.mult, ALU.add))
                    after_steps()

                    for n in range(XPARTS):
                        dve.wait_ge(x_loaded[n], 16 + 16 * (n == XPARTS - 1))
                        settle(dve, "dve")
                        with dve.Fori(n * per, (n + 1) * per) as t:
                            dve.bn_stats(stats[:, t, :], acc[:, t, :]).then_inc(stats_set, 1)
                    dve.wait_ge(stats_set, NT)
                    moments = 0

                    def moment(ins):
                        nonlocal moments
                        ins.then_inc(moment_step, 1)
                        moments += 1

                    def after():
                        dve.wait_ge(moment_step, moments)

                    even, odd = stats[:, :, 1], stats[:, :, 4]
                    moment(dve.tensor_tensor(mean_sum[:, :], even, odd, ALU.add))
                    moment(dve.tensor_tensor(mean_gap[:, :], even, odd, ALU.subtract))
                    moment(dve.tensor_tensor(square_sum[:, :], stats[:, :, 2], stats[:, :, 5], ALU.add))
                    after()
                    moment(dve.tensor_scalar(mean[:, :], mean_sum[:, :], 0.5, None, ALU.mult))
                    moment(dve.scalar_tensor_tensor(gap_square[:, :], mean_gap[:, :], 0.25, mean_gap[:, :],
                                                    ALU.mult, ALU.mult))
                    moment(dve.tensor_scalar(square_mean[:, :], square_sum[:, :], 1.0 / D, LN_EPS, ALU.mult, ALU.add))
                    after()
                    dve.tensor_tensor(var_eps[:, :], square_mean[:, :], gap_square[:, :], ALU.add).then_inc(var_set, 1)

                    dve.wait_ge(number_set, 1)

                    def one_hots(t, b, j):
                        dve.wait_ge(one_hots_used, t + 1)
                        for to, table_, n in ((one_hot_lo[b], dst_in_tile, P), (one_hot_hi[b][:, :, :], dst_tile, NT)):
                            these = table_[:, bass.ds(t * BATCH, BATCH)].rearrange("p (a e) -> p a e", a=1)
                            last = dve.tensor_tensor(to, number[:, 0:n, :], these.broadcast_to([P, n, BATCH]),
                                                     ALU.is_equal)
                        last.then_inc(one_hots_built[b], 1)

                    node_tiles(dve, one_hots)

                    dve.wait_ge(degrees_summed, 1)
                    dve.tensor_scalar(degree[:, :], ps_deg[:, 0:NT], 1.0, None, ALU.add).then_inc(degree_set, 1)
                    dve.wait_ge(roots_set, 2)
                    moment(dve.tensor_scalar(dinv_up[:, :], dinv[:, :], TABLE_SCALE, None, ALU.mult))
                    moment(dve.tensor_scalar(dinv_down[:, :], dinv[:, :], 1.0 / TABLE_SCALE, None, ALU.mult))
                    moment(dve.tensor_tensor(rstd[:, NT - 1:NT], rstd[:, NT - 1:NT], real_row[:, :], ALU.mult))
                    after()
                    moment(dve.tensor_tensor(row_scale[:, :], rstd[:, :], dinv_up[:, :], ALU.mult))
                    after()

                    def scaled_rows(u, tiles, b):
                        for n in range(tiles):
                            t = 2 * u + n
                            dve.tensor_scalar(acc[:, t, :], acc[:, t, :], mean[:, bass.ds(t, 1)],
                                              row_scale[:, bass.ds(t, 1)], ALU.subtract, ALU.mult).then_inc(acc_set, 1)

                    def low_part(u, tiles, b):
                        dve.wait_ge(hi_part_set, u + 1)
                        dve.tensor_tensor(parts[b][:, 0:tiles, 1, :], acc[:, bass.ds(2 * u, tiles), :],
                                          parts[b][:, 0:tiles, 0, :], ALU.subtract).then_inc(lo_part_set, 1)

                    scaled_rows(0, 2, 0)
                    with dve.Fori(0, NT // 4 - 1) as j:
                        for b in (0, 1):
                            scaled_rows(2 * j + b + 1, 2, 1 - b)
                            low_part(2 * j + b, 2, b)
                    scaled_rows(NT // 2 - 1, 2, 1)
                    low_part(NT // 2 - 2, 2, 0)
                    scaled_rows(NT // 2, 1, 0)
                    low_part(NT // 2 - 1, 2, 1)
                    low_part(NT // 2, 1, 0)

        scope = ExitStack()
        with scope:
            sb, ps = sb_in(scope), ps_in(scope)
            ring = sb("gathered", [P, GPT, GE, 2, D], F16)
            src_now = [sb(f"src_now{b}", [P, GPT * GE], I32) for b in (0, 1)]
            one_hot = sb("one_hot", [P, 2, GE, P], F16)
            x_rows = [sb(f"x_rows_b{b}", [P, D], F32) for b in (0, 1)]
            xn_t = [sb(f"xn_t{n}", [P, C, P], F32R) for n in ("hi", "lo")]
            q = sb("q", [P, D], F32)
            k = sb("k", [P, D], F32)
            zeros = sb("zeros_b2", [P, P], BF16)
            ps_turn = ps("ps_turn", [P, 512])
            ps_qv, ps_k, ps_kv = ps("ps_qv", [P, 512]), ps("ps_k", [P, 512]), ps("ps_kv", [P, 512])
            ps_sum = ps("ps_sum", [P, 2, 512])
            ps_mark = ps("ps_mark", [P, 512])

            landed = [sem(f"group_landed{g}") for g in range(GPT)]
            src_copied, group_summed = sem("src_copied"), sem("group_summed")
            one_hot_built, pair_summed, pair_added = sem("one_hot_built"), sem("pair_summed"), sem("pair_added")
            x_loaded = [sem(f"x_loaded_b{b}") for b in (0, 1)]
            xn_set, xn_turned, xn_hi_set, xn_lo_set = sem("xn_set"), sem("xn_turned"), sem("xn_hi_set"), sem("xn_lo_set")
            q_ready, k_ready, v_ready = sem("q_ready"), sem("k_ready"), sem("v_ready")
            q_set, k_set, v_set, q_stored = sem("q_set"), sem("k_set"), sem("v_set"), sem("q_stored")
            k_added, kv_summed, zeros_set = sem("k_added"), sem("kv_summed"), sem("zeros_set")

            with nc.Block() as block:

                @block.sync
                def _(sp):
                    def load_x(t, b, j):
                        sp.wait_ge(xn_turned, t + 1)
                        r = rows_of(t)
                        sp.dma_start(x_rows[b][0:r, :], x[bass.ds(t * P, r), :]).then_inc(x_loaded[b], 16)

                    node_tiles(sp, load_x)

                @block.gpsimd
                def _(pool):
                    def gather(t, b, j):
                        pool.wait_ge(group_summed, GPT * t + 1)
                        settle(pool, "pool")
                        pool.tensor_copy(src_now[b][:, :], src_col[:, bass.ds(GPT * GE * t, GPT * GE)]
                                         ).then_inc(src_copied, 1)
                        pool.wait_ge(src_copied, t + 1)
                        for g in range(GPT):
                            pool.wait_ge(group_summed, GPT * t + g + 1)
                            settle(pool, "pool")
                            for e in range(GE):
                                pool.indirect_dma_start(
                                    ring[:, g, e, :, :].rearrange("p a d -> p (a d)"), None, table,
                                    bass.IndirectOffsetOnAxis(src_now[b][:, g * GE + e:g * GE + e + 1], 0)
                                ).then_inc(landed[g], 16)

                    node_tiles(pool, gather)

                @block.tensor
                def _(pe):
                    pe.sem_inc(group_summed, GPT)
                    pe.sem_inc(xn_turned, 2)
                    pe.wait_ge(zeros_set, 2)
                    pe.matmul(ps_kv[:, :], zeros[:, :], one_hot[:, 0, :, :].bitcast(BF16).rearrange("p e n -> p (e n)"),
                              start=True, stop=False, skip_group_check=True)
                    pe.matmul(ps_sum[:, 0, :], zeros[:, :], one_hot[:, 0, :, :].bitcast(BF16).rearrange("p e n -> p (e n)"),
                              start=True, stop=True).then_inc(pair_summed, 1)
                    pair = pe.alloc_register("pair")
                    pe.reg_mov(pair, 1)

                    def sum_group(t, g):
                        at = GPT * t + g
                        first = pe.value_load(windows[0:1, 0, bass.ds(at, 1)], min_val=0, max_val=NT - 1)
                        end = pe.value_load(windows[0:1, 1, bass.ds(at, 1)], min_val=1, max_val=NT)
                        pe.wait_ge(landed[g], 16 * GE * t + 16 * GE)
                        settle(pe, "pe")
                        with pe.Fori(first, end):
                            now = pe.snap(pair, min_val=1, max_val=NG * NT)
                            half = pe.snap(now % 2)
                            pe.wait_ge(one_hot_built, now)
                            settle(pe, "pe")
                            for e in range(GE):
                                for part in (0, 1):
                                    last = pe.matmul(ps_sum[:, half, :], one_hot[:, half, e, :], ring[:, g, e, part, :],
                                                     start=e == 0 and part == 0, stop=e == GE - 1 and part == 1)
                            last.then_inc(pair_summed, 1)
                            pe.reg_add(pair, now, 1)
                        pe.matmul(ps_mark[0:2, 0:2], zeros[:, 0:2], zeros[:, 0:2], start=True, stop=True
                                  ).then_inc(group_summed, 1)

                    def tile(t, b, j):
                        pe.wait_ge(xn_set, t + 1)
                        turn(pe, ps_turn, x_rows[b], ident[:, :]).then_inc(xn_turned, 1)
                        sum_group(t, 0)
                        pe.wait_ge(xn_lo_set, t + 1)
                        product(pe, ps_qv[:, :], xn_t, [w[:, :, 0:D] for w in w_t]).then_inc(q_ready, 1)
                        sum_group(t, 1)
                        product(pe, ps_k[:, :], xn_t, [w[:, :, D:2 * D] for w in w_t]).then_inc(k_ready, 1)
                        sum_group(t, 2)
                        pe.wait_ge(q_set, t + 1)
                        product(pe, ps_qv[:, :], xn_t, [w[:, :, 2 * D:3 * D] for w in w_t]).then_inc(v_ready, 1)
                        sum_group(t, 3)
                        pe.wait_ge(k_set, t + 1)
                        pe.wait_ge(v_set, t + 1)
                        for c in range(C):
                            cols = slice(c * P, (c + 1) * P)
                            last = pe.matmul(ps_kv[:, cols], v[:, cols], k[:, cols], start=False, stop=False,
                                             skip_group_check=True)
                        last.then_inc(kv_summed, 1)

                    node_tiles(pe, tile)
                    pe.matmul(ps_kv[:, :], zeros[:, :], one_hot[:, 0, :, :].bitcast(BF16).rearrange("p e n -> p (e n)"),
                              start=False, stop=True, skip_group_check=True).then_inc(kv_summed, 1)

                @block.scalar
                def _(act):
                    act.sem_inc(q_stored, 16)

                    def tile(t, b, j):
                        act.wait_ge(xn_turned, t + 3)
                        act.copy(xn_t[0][:, :, :].rearrange("p c n -> p (c n)"), ps_turn[:, :]).then_inc(xn_hi_set, 1)
                        act.wait_ge(q_ready, t + 1)
                        act.wait_ge(q_stored, 16 * t + 16)
                        act.activation(q[:, :], ps_qv[:, :], ACT.Relu).then_inc(q_set, 1)
                        act.wait_ge(q_set, t + 1)
                        act.dma_start(q_rows[bass.ds(t * P, P), :], q[:, :]).then_inc(q_stored, 16)
                        act.wait_ge(k_ready, t + 1)
                        act.wait_ge(k_added, t + 1)
                        act.activation(k[:, :], ps_k[:, :], ACT.Relu).then_inc(k_set, 1)
                        act.wait_ge(v_ready, t + 1)
                        act.copy(v[:, :], ps_qv[:, :]).then_inc(v_set, 1)

                    node_tiles(act, tile)
                    act.wait_ge(q_stored, 16 * NT + 16)

                @block.vector
                def _(dve):
                    dve.memset(zeros[:, :], 0.0).then_inc(zeros_set, 1)
                    dve.memset(one_hot[:, 0, :, :], 0.0).then_inc(zeros_set, 1)
                    dve.memset(k_sum[:, :], 0.0).then_inc(k_added, 1)
                    dve.sem_inc(pair_added, 1)
                    pair, window_before = dve.alloc_register("pair"), dve.alloc_register("window_before")
                    dve.reg_mov(pair, 1)
                    dve.reg_mov(window_before, 0)

                    def add_pair(before, window):
                        dve.wait_ge(pair_summed, before + 1)
                        dve.wait_ge(pair_added, before + 1)
                        dve.tensor_tensor(acc[:, window, :], acc[:, window, :], ps_sum[:, before % 2, :], ALU.add
                                          ).then_inc(pair_added, 1)

                    def sum_group(t, g):
                        at = GPT * t + g
                        first = dve.value_load(windows[0:1, 0, bass.ds(at, 1)], min_val=0, max_val=NT - 1)
                        end = dve.value_load(windows[0:1, 1, bass.ds(at, 1)], min_val=1, max_val=NT)
                        with dve.Fori(first, end) as window:
                            now = dve.snap(pair, min_val=1, max_val=NG * NT)
                            half = dve.snap(now % 2)
                            start = tile_start[:, bass.ds(window, 1)]
                            for e in range(GE):
                                last = dve.tensor_scalar(one_hot[:, half, e, :], iota[:, :], start,
                                                         dst_col[:, bass.ds(at * GE + e, 1)], ALU.add, ALU.is_equal)
                            last.then_inc(one_hot_built, 1)
                            add_pair(now - 1, dve.snap(window_before, min_val=0, max_val=NT - 1))
                            dve.reg_add(pair, now, 1)
                            dve.reg_mov(window_before, window)

                    def normalise(t, b):
                        dve.wait_ge(x_loaded[b], (t - b) * 8 + 16)
                        dve.tensor_scalar(x_rows[b][:, :], x_rows[b][:, :], mean[:, bass.ds(t, 1)],
                                          rstd[:, bass.ds(t, 1)], ALU.subtract, ALU.mult).then_inc(xn_set, 1)

                    def tile(t, b, j):
                        sum_group(t, 0)
                        dve.wait_ge(xn_hi_set, t + 1)
                        dve.tensor_tensor(xn_t[1][:, :, :], ps_turn[:, :].rearrange("p (c n) -> p c n", c=C),
                                          xn_t[0][:, :, :].bitcast(F32), ALU.subtract).then_inc(xn_lo_set, 1)
                        for g in range(1, GPT):
                            sum_group(t, g)
                        dve.wait_ge(k_set, t + 1)
                        dve.wait_ge(k_added, t + 1)
                        dve.tensor_tensor(k_sum[:, :], k_sum[:, :], k[:, :], ALU.add).then_inc(k_added, 1)
                        if rows_of(t) == P:
                            normalise(t + 1, 1 - b)

                    normalise(0, 0)
                    node_tiles(dve, tile)
                    dve.drain()
                    now = dve.snap(pair, min_val=1, max_val=NG * NT + 1)
                    add_pair(now - 1, dve.snap(window_before, min_val=0, max_val=NT - 1))
                    dve.wait_ge(kv_summed, NT + 1)
                    dve.tensor_copy(v[:, :], ps_kv[:, :])

        edge_scope.close()
        mix(nc, sb_in, ps_in, sem, turns, settle, acc, k_sum, v, ident, ones, dinv_down, x, q_rows, x2_rows,
            w_gnn, b_gnn, w_proj, b_proj)
        kv_scope.close()
        def right(name, shape, dt):
            return everything.enter_context(nc.sbuf_tensor(name, shape, dt, side="right"))

        routing = route(nc, sb_in, right, ps_in, sem, turns, settle, acc, ident, w_gate, w1, sorted_rows,
                        expert_rows)
        acc_scope.close()
        experts(nc, sb_in, ps_in, sem, turns, settle, ident, x2_rows, sorted_rows, expert_rows, *routing, w2, out)


_INS = ['x', 'src', 'dst', 'L0_gnn_W', 'L0_gnn_b', 'L0_mix_qkv_weight', 'L0_mix_proj_weight',
        'L0_mix_proj_bias', 'L0_ffn_Wg', 'L0_ffn_W1', 'L0_ffn_W2']


def kernel(**inputs):
    import numpy as _np
    import concourse.bacc as _bacc
    from concourse import mybir as _mybir
    from concourse.bass_utils import run_bass_kernel_spmd as _run

    nc = _bacc.Bacc("TRN2", target_bir_lowering=False, num_devices=1)
    arrays, args = {}, []
    for name in _INS:
        a = _np.ascontiguousarray(inputs[name])
        arrays[f"in_{name}"] = a
        args.append(nc.dram_tensor(f"in_{name}", a.shape, _mybir.dt.from_np(a.dtype), kind="ExternalInput").ap())
    args.append(nc.dram_tensor("out_0", (N, D), _mybir.dt.float32, kind="ExternalOutput").ap())
    build(nc, *args)
    r = _run(nc, [arrays], core_ids=[0])
    return r.results[0]["out_0"]
```

```python
from contextlib import ExitStack

import concourse.bass as bass
from concourse import mybir

F32 = mybir.dt.float32
F32R = mybir.dt.float32r
F16 = mybir.dt.float16
BF16 = mybir.dt.bfloat16
I32 = mybir.dt.int32
ALU = mybir.AluOpType
ACT = mybir.ActivationFunctionType
AX_X = mybir.AxisListType.X

P = 128
N, D = 6250, 512
E = 100000
H, DH = 16, 32
NEXP, FF = 8, 256
C = D // P
NT = -(-N // P)
LAST = N - (NT - 1) * P
ET = 16 * NT
GE = 4
NG = ET // GE
GPT = NG // NT
BATCH = ET // NT
ROWT = 8
ER = ET // ROWT
EFULL = E // (ROWT * P)
EREST = E - EFULL * ROWT * P
PAD_DST = 8191
XPARTS = 7
ACT_PARTS = 5
BEFORE = 2
FIRST = 8
ALONE = 7
EARLY = NT // 2 - 1
NWB = 3 * D // P
PAIRS = 2 * NT * P // (2 * P) + NEXP
CHUNK = 7
AHEAD = 4
REGION = 2 ** 13
LOWEST = -3.0e38
LN_EPS = 1e-5
DIV_EPS = 1e-15
SLOPE = 0.01
TABLE_SCALE = 1024.0
assert ET * P >= E and ER <= P and NT % 2 == 1 and GPT == 4 and EREST > 0 and NT % XPARTS == 0
assert NT % CHUNK == 0 and CHUNK % 2 == 1 and REGION >= NT * P + 2 * P


def node_tiles(eng, body):
    with eng.Fori(0, NT // 2) as j:
        body(2 * j, 0, j)
        body(2 * j + 1, 1, j)
    body(NT - 1, 0, NT // 2)


def some_node_tiles(eng, body, first, end):
    with eng.Fori(first, end) as j:
        body(2 * j, 0, j)
        body(2 * j + 1, 1, j)


def tile_pairs(eng, body):
    assert NT % 8 == 1
    with eng.Fori(0, NT // 8) as j:
        for b in range(4):
            body(4 * j + b, 2, b)
    body(NT // 2, 1, 0)


def staggered(eng, *stages):
    most = max(ahead for ahead, _ in stages)
    turns = NT // 4 * 4 - 4

    def run(t, b):
        for ahead, body in stages:
            if not isinstance(t, int) or 0 <= t + ahead < NT:
                body(t + ahead, (b + ahead) % 4)

    assert NT % 4 == 1 and most <= 4
    for t in range(-most, 0):
        run(t, t % 4)
    with eng.Fori(0, turns // 4) as j:
        for b in range(4):
            run(4 * j + b, b)
    for t in range(turns, NT):
        run(t, t % 4)


def rows_of(t):
    return LAST if isinstance(t, int) and t == NT - 1 else P


def turn(pe, out, rows, ident, chunks=C):
    for c in range(chunks):
        last = pe.transpose(out[:, c * P:(c + 1) * P], rows[:, c * P:(c + 1) * P], ident)
    return last


def product(pe, out, left, right, chunks=C, ready=None):
    for c in range(chunks):
        if ready:
            ready(c)
        for a, b in ((1, 0), (0, 1), (0, 0)):
            last = pe.matmul(out, left[a][:, c, :], right[b][:, c, :],
                             start=c == 0 and a == 1, stop=c == chunks - 1 and a + b == 0)
    return last


def mix(nc, sb_in, ps_in, sem, turns, settle, acc, stats, k_sum, kv, ident, ones, dinv_down, x, q_rows, x2_rows,
        w_gnn, b_gnn, w_proj, b_proj):
    scope = ExitStack()
    with scope:
        sb, ps = sb_in(scope), ps_in(scope)
        proj_rows = sb("proj_rows", [P, C, D], F32)
        proj_t = sb("proj_t", [P, C, D], F32)
        gnn_raw = sb("gnn_raw", [P, C, D], F32)
        gnn_w = [sb(f"gnn_w_{n}", [P, C, D], F32R) for n in ("hi", "lo")]
        mixer = [sb(f"mixer_{n}", [P, C, D], F32R) for n in ("hi", "lo")]
        kv_heads = sb("kv_heads", [P, C, P], F32)
        k_all = sb("k_all", [P, D], F32)
        b_gnn_rows, b_proj_rows = sb("b_gnn_rows", [P, D], F32), sb("b_proj_rows", [P, D], F32)
        q, x_rows = [proj_rows[:, b, :] for b in range(4)], [proj_t[:, b, :] for b in range(4)]
        qk = [sb(f"qk{b}", [P, D], F32) for b in (0, 1)]
        den, den_eps, den_inv = (sb(n, [P, H], F32) for n in ("den", "den_eps", "den_inv"))
        a_rows = sb("a_rows", [P, D], F32)
        q_t = [[sb(f"q_t{b}{n}", [P, C, P], F32R) for n in ("hi", "lo")] for b in (0, 1)]
        a_t = [[sb(f"a_t{b}{n}", [P, C, P], F32R) for n in ("hi", "lo")] for b in (0, 1)]
        h = sb("h", [P, D], F32)
        g = [sb(f"g{b}", [P, D], F32) for b in (0, 1)]
        ps_q, ps_a = ps("ps_q_turned", [P, 512]), ps("ps_a_turned", [P, 512])
        ps_mix = [ps(f"ps_mix{b}", [P, 512]) for b in (0, 1)]
        ps_gnn = [ps(f"ps_gnn{b}", [P, 512]) for b in (0, 1)]
        mixer_banks = ps_mix + ps_gnn
        assert len(mixer_banks) == C

        proj_loaded, gnn_loaded, biases_loaded = sem("proj_loaded"), sem("gnn_loaded"), sem("biases_loaded")
        proj_turned, proj_copied = sem("proj_turned"), sem("proj_copied")
        heads_zeroed, heads_set, k_all_summed, k_all_set = (
            sem(n) for n in ("heads_zeroed", "heads_set", "k_all_summed", "k_all_set"))
        mixer_summed, mixer_hi_set, mixer_lo_set = sem("mixer_summed"), sem("mixer_hi_set"), sem("mixer_lo_set")
        gnn_hi_set, gnn_lo_set = sem("gnn_hi_set"), sem("gnn_lo_set")
        x_loaded = [sem(f"x_loaded_c{b}") for b in range(4)]
        q_loaded = [sem(f"q_loaded_c{b}") for b in range(4)]
        qk_set, x_biased, q_divided, a_set = sem("qk_set"), sem("x_biased"), sem("q_divided"), sem("a_set")
        den_step = sem("den_step")
        turned, hi_set, lo_set = sem("turned_c"), sem("hi_set_c"), sem("lo_set_c")
        mixed, gnn_done, h_step, x2_set = sem("mixed"), sem("gnn_done"), sem("h_step"), sem("x2_set")
        g_set, x2_stored, stats_set = sem("g_set"), sem("x2_stored"), sem("stats_set_c")

        with nc.Block() as block:

            @block.sync
            def _(sp):
                sp.dma_start(proj_rows[:, :, :], w_proj.rearrange("(r p) d -> p r d", p=P)).then_inc(proj_loaded, 16)
                sp.dma_start(gnn_raw[:, :, :], w_gnn.rearrange("(c p) d -> p c d", p=P)).then_inc(gnn_loaded, 16)
                for rows, bias in ((b_gnn_rows, b_gnn), (b_proj_rows, b_proj)):
                    sp.dma_start(rows[:, :], bias.rearrange("(a d) -> a d", a=1).broadcast_to([P, D])
                                 ).then_inc(biases_loaded, 16)

                sp.wait_ge(proj_turned, C)

                def load_q(t, b):
                    sp.wait_ge(turned, 2 * t + 1)
                    sp.dma_start(q[b][:, :], q_rows[bass.ds(t * P, P), :]).then_inc(q_loaded[b], 16)

                def load_x(t, b):
                    if isinstance(t, int) and t == 0:
                        sp.wait_ge(mixer_summed, C)
                    sp.wait_ge(x2_set, t + 1)
                    r = rows_of(t)
                    sp.dma_start(x_rows[b][0:r, :], x[bass.ds(t * P, r), :]).then_inc(x_loaded[b], 16)

                def store(t, b):
                    sp.wait_ge(x2_set, t + 5)
                    sp.dma_start(x2_rows[bass.ds(t * P, P), :], acc[:, t, :]).then_inc(x2_stored, 16)

                staggered(sp, (4, load_q), (3, load_x), (0, store))
                sp.wait_ge(x2_stored, 16 * NT)

            @block.gpsimd
            def _(pool):
                pool.sem_inc(x2_set, 4)
                pool.memset(kv_heads[:, :, :], 0.0).then_inc(heads_zeroed, 1)
                pool.wait_ge(k_all_set, 1)
                pool.wait_ge(biases_loaded, 32)

                def times_k(t, b):
                    pool.wait_ge(q_loaded[b], (t - b) * 4 + 16)
                    pool.wait_ge(den_step, 3 * t + 1)
                    settle(pool)
                    pool.tensor_tensor(qk[b % 2][:, :], q[b][:, :], k_all[:, :], ALU.mult).then_inc(qk_set, 1)

                def add_bias(t, b):
                    pool.wait_ge(x_loaded[b], (t - b) * 4 + 16)
                    pool.tensor_tensor(x_rows[b][:, :], x_rows[b][:, :], b_proj_rows[:, :], ALU.add
                                       ).then_inc(x_biased, 1)

                def add_up(t, b):
                    pool.wait_ge(g_set, t + 2)
                    settle(pool)
                    pool.tensor_tensor(acc[:, t, :], x_rows[b][:, :], g[b % 2][:, :], ALU.add).then_inc(x2_set, 1)

                staggered(pool, (3, times_k), (2, add_bias), (0, add_up))

            @block.tensor
            def _(pe):
                pe.matmul(ps_a[:, :], ones[:, :], k_sum[:, :], start=True, stop=True).then_inc(k_all_summed, 1)
                pe.wait_ge(proj_loaded, 16)
                for r in range(C):
                    if r == 1:
                        pe.wait_ge(k_all_set, 1)
                    if r >= 2:
                        pe.wait_ge(proj_copied, r - 1)
                    turn(pe, (ps_q, ps_a)[r % 2], proj_rows[:, r, :], ident[:, :]).then_inc(proj_turned, 1)
                pe.wait_ge(heads_set, 1)
                pe.wait_ge(proj_copied, C)
                for c in range(C):
                    pe.matmul(mixer_banks[c][:, :], kv_heads[:, c, :], proj_t[:, c, :], start=True, stop=True
                              ).then_inc(mixer_summed, 1)
                pe.sem_inc(turned, 8)

                def turn_both(t, b):
                    pe.wait_ge(q_divided, t + 1)
                    pe.wait_ge(lo_set, 2 * t + 1)
                    turn(pe, ps_q, q[b], ident[:, :]).then_inc(turned, 1)
                    pe.wait_ge(a_set, t + 1)
                    turn(pe, ps_a, a_rows, ident[:, :]).then_inc(turned, 1)

                def multiply(t, b):
                    if isinstance(t, int) and t == 0:
                        pe.wait_ge(mixer_lo_set, C)
                        pe.wait_ge(gnn_lo_set, 1)
                    pe.wait_ge(lo_set, 2 * t + 2)
                    product(pe, ps_mix[b % 2][:, :], q_t[b % 2], mixer).then_inc(mixed, 1)
                    pe.wait_ge(lo_set, 2 * t + 3)
                    product(pe, ps_gnn[b % 2][:, :], a_t[b % 2], gnn_w).then_inc(gnn_done, 1)

                staggered(pe, (1, turn_both), (0, multiply))

            @block.scalar
            def _(act):
                act.wait_ge(gnn_loaded, 16)
                act.copy(gnn_w[0][:, :, :], gnn_raw[:, :, :]).then_inc(gnn_hi_set, 1)
                for c in range(C):
                    act.wait_ge(mixer_summed, c + 1)
                    act.copy(mixer[0][:, c, :], mixer_banks[c][:, :]).then_inc(mixer_hi_set, 1)

                def high_parts(t, b):
                    for n, (banked, parts) in enumerate(((ps_q, q_t[b % 2]), (ps_a, a_t[b % 2]))):
                        act.wait_ge(turned, 2 * t + n + 9)
                        act.copy(parts[0][:, :, :].rearrange("p c n -> p (c n)"), banked[:, :]).then_inc(hi_set, 1)

                def scale_sum(t, b):
                    act.activation(a_rows[:, :], acc[:, t, :], ACT.Copy, scale=dinv_down[:, bass.ds(t, 1)]
                                   ).then_inc(a_set, 1)

                staggered(act, (1, high_parts), (2, scale_sum))

            @block.vector
            def _(dve):
                dve.sem_inc(lo_set, 1)
                dve.sem_inc(den_step, 4)
                dve.sem_inc(g_set, 1)
                dve.wait_ge(k_all_summed, 1)
                dve.tensor_copy(k_all[:, :], ps_a[:, :]).then_inc(k_all_set, 1)
                dve.wait_ge(heads_zeroed, 1)
                for c in range(C):
                    for n in range(P // DH):
                        rows, cols = slice(n * DH, (n + 1) * DH), slice(c * P + n * DH, c * P + (n + 1) * DH)
                        last = dve.tensor_copy(kv_heads[rows, c, rows], kv[rows, cols])
                last.then_inc(heads_set, 1)
                for r in range(C):
                    dve.wait_ge(proj_turned, r + 1)
                    dve.tensor_copy(proj_t[:, :, r * P:(r + 1) * P], (ps_q, ps_a)[r % 2][:, :].rearrange("p (c o) -> p c o", c=C)
                                    ).then_inc(proj_copied, 1)
                for c in range(C):
                    dve.wait_ge(mixer_hi_set, c + 1)
                    dve.tensor_tensor(mixer[1][:, c, :], mixer_banks[c][:, :], mixer[0][:, c, :].bitcast(F32),
                                      ALU.subtract).then_inc(mixer_lo_set, 1)
                dve.wait_ge(gnn_hi_set, 1)
                dve.tensor_tensor(gnn_w[1][:, :, :], gnn_raw[:, :, :], gnn_w[0][:, :, :].bitcast(F32), ALU.subtract
                                  ).then_inc(gnn_lo_set, 1)
                dve.wait_ge(biases_loaded, 32)

                def low_parts(t, b):
                    for n, (banked, parts) in enumerate(((ps_q, q_t[b % 2]), (ps_a, a_t[b % 2]))):
                        dve.wait_ge(hi_set, 2 * t + n + 1)
                        dve.tensor_tensor(parts[1][:, :, :].rearrange("p c n -> p (c n)"), banked[:, :],
                                          parts[0][:, :, :].bitcast(F32).rearrange("p c n -> p (c n)"), ALU.subtract
                                          ).then_inc(lo_set, 1)

                def divide(t, b):
                    dve.wait_ge(qk_set, t + 1)
                    dve.tensor_reduce(den[:, :], qk[b % 2][:, :].rearrange("p (h d) -> p h d", h=H), AX_X, ALU.add
                                      ).then_inc(den_step, 1)
                    dve.wait_ge(den_step, 3 * t + 5)
                    dve.tensor_scalar(den_eps[:, :], den[:, :], DIV_EPS, None, ALU.add).then_inc(den_step, 1)
                    dve.wait_ge(den_step, 3 * t + 6)
                    dve.reciprocal(den_inv[:, :], den_eps[:, :]).then_inc(den_step, 1)
                    dve.wait_ge(den_step, 3 * t + 7)
                    dve.tensor_tensor(q[b][:, :].rearrange("p (h d) -> p h d", h=H),
                                      q[b][:, :].rearrange("p (h d) -> p h d", h=H),
                                      den_inv[:, :].rearrange("p (h a) -> p h a", a=1).broadcast_to([P, H, DH]),
                                      ALU.mult).then_inc(q_divided, 1)

                def add_products(t, b):
                    dve.wait_ge(mixed, t + 1)
                    dve.wait_ge(x_biased, t + 1)
                    dve.tensor_tensor(x_rows[b][:, :], x_rows[b][:, :], ps_mix[b % 2][:, :], ALU.add).then_inc(h_step, 1)
                    dve.wait_ge(gnn_done, t + 1)
                    dve.wait_ge(g_set, t + 1)
                    dve.tensor_tensor(h[:, :], ps_gnn[b % 2][:, :], b_gnn_rows[:, :], ALU.add).then_inc(h_step, 1)
                    dve.wait_ge(h_step, 2 * t + 2)
                    dve.wait_ge(x2_set, t + 3)
                    dve.scalar_tensor_tensor(g[b % 2][:, :], h[:, :], SLOPE, h[:, :], ALU.mult, ALU.max).then_inc(g_set, 1)

                def moments(t, b):
                    dve.wait_ge(x2_set, t + 5)
                    settle(dve)
                    dve.bn_stats(stats[:, t, :], acc[:, t, :]).then_inc(stats_set, 1)

                staggered(dve, (2, low_parts), (3, divide), (0, moments), (1, add_products))
                dve.wait_ge(stats_set, NT)


def route(nc, sb_in, keep, ps_in, sem, turns, settle, acc, stats, ident, w_gate, w1, w2, sorted_rows):
    place = keep("place", [P, NT, 2], I32)
    top_w = keep("top_w", [P, 2, NT], F32)
    bounds = keep("bounds", [1, NEXP + 1], I32)
    pair_row = keep("pair_row", [1, PAIRS + 2], I32)
    rest_count = keep("rest_count", [1, 1], I32)
    zeros = keep("zero_rows", [P, D], F32)
    raw = [[keep(f"w{m}_raw{b}", [P, k, n], F32) for b in (0, 1)] for m, k, n in ((1, C, FF), (2, FF // P, D))]
    scope = ExitStack()
    with scope:
        sb, ps = sb_in(scope), ps_in(scope)
        gate = sb("gate", [P, C, NEXP], F32)
        mean, rstd, var_eps, half_a, half_b, half_c, part_a, part_b, minus_half = (
            sb(f"{n}_d", [P, NT], F32) for n in ("mean", "rstd", "var_eps", "half_a", "half_b", "half_c", "part_a",
                                                "part_b", "minus_half"))
        xn = [sb(f"xn_d{n}", [P, D], F32) for n in range(CHUNK)]
        xn_t = [sb(f"xn_t_d{n}", [P, C, P], F32) for n in range(CHUNK)]
        logits_t = sb("logits_t", [NEXP, 2 * D], F32)
        chunk = [P, CHUNK, NEXP]
        logits, rest, mark, first, second, rank = (
            sb(n, chunk, F32) for n in ("logits", "rest", "mark", "first", "second", "rank"))
        picked = sb("picked", chunk, BF16)
        best, best_no, next_best, next_no = (sb(n, [P, CHUNK], F32) for n in ("best", "best_no", "next_best", "next_no"))
        place_f = sb("place_f", [P, CHUNK, 2], F32)
        picked_sum = sb("picked_sum", [P, NEXP], F32)
        picked_before = sb("picked_before", [P, NEXP], BF16)
        all_picks = [sb(f"all_picks{n}", [P, NT, NEXP], F32) for n in (0, 1)]
        all_mark = sb("all_mark", [P, NT, NEXP], F32)
        gap, squashed = sb("gap", [P, NT], F32), sb("squashed", [P, NT], F32)
        old_place, moved, new_place = (sb(n, [P, NT, 2], F32) for n in ("old_place", "moved", "new_place"))
        falling = sb("falling", [P, NEXP], F32)
        region = sb("region", [P, NEXP], F32)
        e8 = [P, NEXP]
        pairs_i, pairs_j = sb("pairs_i", e8, I32), sb("pairs_j", e8, I32)
        total, pairs, ends_a, ends_b, starts, shift = (
            sb(n, e8, F32) for n in ("total", "pairs", "ends_a", "ends_b", "starts", "shift"))
        shift_steps = sb("shift_steps", [1, NEXP - 1], F32)
        last_pair = sb("last_pair", [1, 1], F32)
        pair_start, shifts, pair_no, real_pair = (
            sb(n, [1, PAIRS + 2], F32) for n in ("pair_start", "shifts", "pair_no", "real_pair"))
        reached, reached_steps = (sb(n, [1, PAIRS + 2, NEXP - 1], F32) for n in ("reached", "reached_steps"))
        zero_from = sb("zero_from", [1, NEXP], I32)
        before_b = sb("before_b", [P, P], BF16)
        ones_b = sb("ones_b", [P, P], BF16)
        ps_x = [ps(f"ps_x{b}", [P, 512]) for b in range(3)]
        ps_logits = [ps(f"ps_logits{n}", [P, 512]) for n in (0, 1)]
        ps_gate, ps_rank, ps_total = ps("ps_gate", [P, 512]), ps("ps_rank", [P, 512]), ps("ps_total", [P, 512])

        (gate_loaded, zeroed, const_set, moment_step, var_set, root_set, xn_set, x_turned, x_copied, acc_set, gated,
         route_step, end_step, gap_set, squashed_set, picked_set, ranked, counted, zero_from_set, place_set, scattered,
         sum_set, logits_copied, raw_loaded, logits_turned, logits_t_set) = (sem(n) for n in (
             "gate_loaded", "zeroed", "const_set_d", "moment_step_d", "var_set_d", "root_set_d", "xn_set_d",
             "x_turned_d", "x_copied_d", "acc_set_d", "gated", "route_step", "end_step", "gap_set", "squashed_set",
             "picked_set", "ranked", "counted", "zero_from_set", "place_set", "scattered", "sum_set",
             "logits_copied", "first_raw_loaded", "logits_turned", "logits_t_set"))
        bank_of = [n % 2 for n in range(CHUNK - 1)] + [2]

        with nc.Block() as block:

            @block.sync
            def _(sp):
                sp.dma_start(gate[:, :, :], w_gate.rearrange("(c p) e -> p c e", p=P)).then_inc(gate_loaded, 16)
                for e in (0, 1):
                    for to, w in zip(raw, (w1, w2)):
                        sp.dma_start(to[e][:, :, :], w[e].rearrange("(c p) d -> p c d", p=P)).then_inc(raw_loaded, 16)
                sp.wait_ge(raw_loaded, 64)
                sp.wait_ge(zero_from_set, 1)
                sp.wait_ge(const_set, 1)
                settle(sp)
                for e in range(NEXP):
                    row = sp.value_load(zero_from[0:1, e:e + 1], min_val=0, max_val=NEXP * REGION - 2 * P)
                    sp.dma_start(sorted_rows[bass.ds(row, 2 * P), :].rearrange("(t p) d -> p t d", p=P),
                                 zeros[:, :].rearrange("p (a d) -> p a d", a=1).broadcast_to([P, 2, D])
                                 ).then_inc(zeroed, 16)
                sp.wait_ge(zeroed, 16 * NEXP)

            @block.gpsimd
            def _(pool):
                pool.memset(zeros[:, :], 0.0).then_inc(const_set, 1)
                pool.memset(minus_half[:, :], -0.5).then_inc(const_set, 1)
                pool.memset(ones_b[:, :], 1.0).then_inc(const_set, 1)
                pool.memset(picked_before[:, :], 0.0).then_inc(const_set, 1)
                for to, step, base in ((falling, -1, NEXP), (region, REGION, 0)):
                    pool.iota(to[:, :], [[step, NEXP]], base=base, channel_multiplier=0,
                              allow_small_or_imprecise_dtypes=True).then_inc(const_set, 1)
                pool.iota(pair_no[:, :], [[1, PAIRS + 2]], base=0, channel_multiplier=0,
                          allow_small_or_imprecise_dtypes=True).then_inc(const_set, 1)
                pool.wait_ge(const_set, 7)
                pool.affine_select(out=before_b[:, :], in_=ones_b[:, :], compare_op=ALU.is_gt, fill=0.0,
                                   base=0, pattern=[[1, P]], channel_multiplier=-1).then_inc(const_set, 1)
                pool.wait_ge(var_set, 1)
                for these in (slice(0, CHUNK), slice(CHUNK, NT)):
                    pool.tensor_tensor(rstd[:, these], var_eps[:, these], minus_half[:, these], ALU.pow
                                       ).then_inc(root_set, 1)
                for t in range(NT):
                    if t % CHUNK == 0:
                        pool.wait_ge(place_set, t // CHUNK + 1)
                        pool.wait_ge(acc_set, t + CHUNK + CHUNK)
                    for n in (0, 1):
                        pool.indirect_dma_start(sorted_rows, bass.IndirectOffsetOnAxis(place[:, t, n:n + 1], 0),
                                                acc[:, t, :], None).then_inc(scattered, 16)
                pool.wait_ge(scattered, 16 * 2 * NT)

            @block.tensor
            def _(pe):
                pe.wait_ge(gate_loaded, 16)
                pe.wait_ge(const_set, 8)

                def start(t, n):
                    pe.wait_ge(xn_set, t + 1)
                    pe.wait_ge(x_copied, t + 1)
                    turn(pe, ps_x[bank_of[n]], xn[n], ident[:, :]).then_inc(x_turned, 1)

                def finish(t, n):
                    pe.wait_ge(x_copied, t + 3)
                    for c in range(C):
                        last = pe.matmul(ps_logits[n // 4][0:NEXP, n % 4 * P:(n % 4 + 1) * P], gate[:, c, :],
                                         xn_t[n][:, c, :], start=c == 0, stop=c == C - 1)
                    last.then_inc(gated, 1)

                def tiles(k, between):
                    start(k * CHUNK, 0)
                    for n in range(CHUNK):
                        if n + 1 < CHUNK:
                            start(k * CHUNK + n + 1, n + 1)
                        if n == 0:
                            pe.wait_ge(logits_t_set, 2 * k + 2)
                        finish(k * CHUNK + n, n)
                        between(n)

                def turn_logits(k):
                    pe.wait_ge(logits_t_set, 2 * k + 4)
                    pe.wait_ge(logits_copied, k + 1)
                    settle(pe)
                    for n in range(CHUNK):
                        last = pe.transpose(ps_gate[:, n * NEXP:(n + 1) * NEXP], logits_t[:, n * P:(n + 1) * P],
                                            ident[0:NEXP, 0:NEXP])
                    last.then_inc(logits_turned, 1)

                def count_picks(k):
                    pe.wait_ge(picked_set, k + 1)
                    pe.wait_ge(counted, k + 1)
                    for n in range(CHUNK):
                        left = picked_before[:, :] if n == 0 else picked[:, n - 1, :]
                        pe.matmul(ps_rank[:, n * NEXP:CHUNK * NEXP], ones_b[:, :],
                                  left.rearrange("p (a e) -> p a e", a=1).broadcast_to([P, CHUNK - n, NEXP]),
                                  start=n == 0, stop=False, skip_group_check=True)
                    pe.matmul(ps_rank[:, 0:CHUNK * NEXP], before_b[:, :], picked[:, :, :].rearrange("p t e -> p (t e)"),
                              start=False, stop=True, skip_group_check=True).then_inc(ranked, 1)

                tiles(0, lambda n: None)
                with pe.Fori(1, NT // CHUNK) as k:
                    tiles(k, lambda n: turn_logits(k - 1) if n == 1 else count_picks(k - 1) if n == 4 else None)
                turn_logits(NT // CHUNK - 1)
                count_picks(NT // CHUNK - 1)
                pe.wait_ge(counted, NT // CHUNK + 1)
                pe.matmul(ps_total[:, 0:NEXP], ones_b[:, :], picked_before[:, :], start=True, stop=True
                          ).then_inc(ranked, 1)

            @block.scalar
            def _(act):
                act.sem_inc(x_copied, 2)
                act.sem_inc(acc_set, CHUNK)
                with act.Fori(0, NT // CHUNK) as k:
                    for n, b in enumerate(bank_of):
                        t = k * CHUNK + n
                        act.wait_ge(x_turned, t + 1)
                        act.wait_ge(gated, t + 1)
                        act.copy(xn_t[n][:, :, :].rearrange("p c n -> p (c n)"), ps_x[b][:, :]).then_inc(x_copied, 1)
                        act.copy(acc[:, t, :], xn[n][:, :]).then_inc(acc_set, 1)
                        if n in (3, CHUNK - 1):
                            act.wait_ge(gated, t + CHUNK + 1)
                            act.wait_ge(logits_turned, k + 1)
                            settle(act)
                            half, tiles = n // 4, n % 4 + 1
                            act.copy(logits_t[:, half * D:half * D + tiles * P], ps_logits[half][0:NEXP, 0:tiles * P]
                                     ).then_inc(logits_t_set, 1)
                act.wait_ge(gap_set, NT // CHUNK)
                act.activation(squashed[:, :], gap[:, :], ACT.Tanh, scale=0.5).then_inc(squashed_set, 1)

            @block.vector
            def _(dve):
                dve.sem_inc(gated, CHUNK)
                dve.sem_inc(counted, 1)
                dve.sem_inc(logits_copied, 1)
                dve.sem_inc(logits_turned, 1)
                dve.sem_inc(logits_t_set, 2)
                count = {"moment": 0, "end": 0}

                def moment(ins):
                    ins.then_inc(moment_step, 1)
                    count["moment"] += 1

                even, odd = stats[:, :, 1], stats[:, :, 4]
                moment(dve.tensor_tensor(half_a[:, :], even, odd, ALU.add))
                moment(dve.tensor_tensor(half_b[:, :], even, odd, ALU.subtract))
                moment(dve.tensor_tensor(half_c[:, :], stats[:, :, 2], stats[:, :, 5], ALU.add))
                dve.wait_ge(moment_step, count["moment"])
                moment(dve.tensor_scalar(mean[:, :], half_a[:, :], 0.5, None, ALU.mult))
                moment(dve.scalar_tensor_tensor(part_a[:, :], half_b[:, :], 0.25, half_b[:, :], ALU.mult, ALU.mult))
                moment(dve.tensor_scalar(part_b[:, :], half_c[:, :], 1.0 / D, LN_EPS, ALU.mult, ALU.add))
                dve.wait_ge(moment_step, count["moment"])
                dve.tensor_tensor(var_eps[:, :], part_a[:, :], part_b[:, :], ALU.add).then_inc(var_set, 1)
                dve.wait_ge(root_set, 1)
                dve.wait_ge(const_set, 8)

                def normalise(k, n):
                    t = k * CHUNK + n
                    dve.wait_ge(acc_set, t + 1)
                    dve.tensor_scalar(xn[n][:, :], acc[:, t, :], mean[:, bass.ds(t, 1)], rstd[:, bass.ds(t, 1)],
                                      ALU.subtract, ALU.mult).then_inc(xn_set, 1)

                def wide(x, n=CHUNK):
                    if x.shape[1] == n:
                        return x.rearrange("p (t a) -> p t a", a=1).broadcast_to([P, n, NEXP])
                    return x.rearrange("p (a e) -> p a e", a=1).broadcast_to([P, n, NEXP])

                def run(k, steps, before, in_chunk):
                    for n, make in enumerate(steps):
                        make().then_inc(route_step, 1)
                        dve.wait_ge(route_step, k * in_chunk + before + n + 1)
                    settle(dve)

                def pick(values, top, number, one_hot):
                    return [
                        lambda: dve.tensor_reduce(top[:, :], values[:, :, :], AX_X, ALU.max),
                        lambda: dve.tensor_tensor(mark[:, :, :], values[:, :, :], wide(top[:, :]), ALU.is_equal),
                        lambda: dve.tensor_tensor(mark[:, :, :], mark[:, :, :], wide(falling[:, :]), ALU.mult),
                        lambda: dve.tensor_reduce(number[:, :], mark[:, :, :], AX_X, ALU.max),
                        lambda: dve.tensor_tensor(one_hot[:, :, :], wide(falling[:, :]), wide(number[:, :]), ALU.is_equal)]

                pick_steps = pick(logits, best, best_no, first) + [
                    lambda: dve.scalar_tensor_tensor(rest[:, :, :], first[:, :, :], LOWEST, logits[:, :, :],
                                                     ALU.mult, ALU.add)] + pick(rest, next_best, next_no, second)
                place_steps = [
                    lambda: dve.tensor_tensor(rank[:, :, :], ps_rank[:, 0:CHUNK * NEXP].rearrange(
                        "p (t e) -> p t e", e=NEXP), wide(region[:, :]), ALU.add),
                    lambda: dve.tensor_tensor(mark[:, :, :], first[:, :, :], rank[:, :, :], ALU.mult),
                    lambda: dve.tensor_reduce(place_f[:, :, 0], mark[:, :, :], AX_X, ALU.add),
                    lambda: dve.tensor_tensor(mark[:, :, :], second[:, :, :], rank[:, :, :], ALU.mult),
                    lambda: dve.tensor_reduce(place_f[:, :, 1], mark[:, :, :], AX_X, ALU.add)]
                in_chunk = len(pick_steps) + len(place_steps)

                def picks(k):
                    dve.wait_ge(logits_turned, k + 2)
                    dve.tensor_copy(logits[:, :, :], ps_gate[:, 0:CHUNK * NEXP].rearrange("p (t e) -> p t e", e=NEXP)
                                    ).then_inc(logits_copied, 1)
                    dve.wait_ge(logits_copied, k + 2)
                    run(k, pick_steps, 0, in_chunk)
                    dve.tensor_tensor(picked[:, :, :], first[:, :, :], second[:, :, :], ALU.add).then_inc(picked_set, 1)
                    these = bass.ds(k * CHUNK, CHUNK)
                    dve.tensor_tensor(gap[:, these], best[:, :], next_best[:, :], ALU.subtract).then_inc(gap_set, 1)
                    for to, one_hot in zip(all_picks, (first, second)):
                        dve.tensor_copy(to[:, these, :], one_hot[:, :, :])
                    dve.wait_ge(picked_set, k + 1)
                    dve.tensor_reduce(picked_sum[:, :], picked[:, :, :].rearrange("p t e -> p e t"), AX_X, ALU.add
                                      ).then_inc(sum_set, 1)

                def places(k):
                    dve.wait_ge(ranked, k + 1)
                    dve.wait_ge(sum_set, k + 1)
                    dve.tensor_tensor(picked_before[:, :], picked_before[:, :], picked_sum[:, :], ALU.add
                                      ).then_inc(counted, 1)
                    run(k, place_steps, len(pick_steps), in_chunk)
                    dve.tensor_copy(place[:, bass.ds(k * CHUNK, CHUNK), :], place_f[:, :, :]).then_inc(place_set, 1)

                for n in range(CHUNK):
                    normalise(0, n)
                dve.wait_ge(root_set, 2)
                for n in range(AHEAD):
                    normalise(1, n)
                with dve.Fori(1, NT // CHUNK - 1) as k:
                    for n in range(AHEAD, CHUNK):
                        normalise(k, n)
                    picks(k - 1)
                    for n in range(AHEAD):
                        normalise(k + 1, n)
                    places(k - 1)
                last = NT // CHUNK - 1
                for n in range(AHEAD, CHUNK):
                    normalise(last, n)
                picks(last - 1)
                places(last - 1)
                picks(last)
                places(last)

                def step(ins):
                    ins.then_inc(end_step, 1)
                    count["end"] += 1
                    dve.wait_ge(end_step, count["end"])

                dve.wait_ge(ranked, NT // CHUNK + 1)
                step(dve.tensor_copy(total[:, :], ps_total[:, 0:NEXP]))
                step(dve.tensor_scalar(pairs_i[:, :], total[:, :], 2.0 * P - 1, None, ALU.add))
                step(dve.tensor_single_scalar(pairs_j[:, :], pairs_i[:, :], 8, ALU.arith_shift_right))
                step(dve.tensor_copy(pairs[:, :], pairs_j[:, :]))
                step(dve.tensor_scalar(pairs[:, :], pairs[:, :], 1.0, None, ALU.max))
                ends, reach, k = pairs, 1, 0
                while reach < NEXP:
                    to = (ends_a, ends_b)[k % 2]
                    step(dve.tensor_copy(to[:, 0:reach], ends[:, 0:reach]))
                    step(dve.tensor_tensor(to[:, reach:NEXP], ends[:, reach:NEXP], ends[:, 0:NEXP - reach], ALU.add))
                    ends, reach, k = to, 2 * reach, k + 1
                step(dve.tensor_tensor(starts[:, :], ends[:, :], pairs[:, :], ALU.subtract))
                step(dve.tensor_copy(bounds[:, 0:NEXP], starts[0:1, :]))
                step(dve.tensor_copy(bounds[:, NEXP:NEXP + 1], ends[0:1, NEXP - 1:NEXP]))
                step(dve.tensor_scalar(rest_count[:, :], ends[0:1, NEXP - 1:NEXP], -16.0, 16.0 * (PAIRS + 1),
                                       ALU.mult, ALU.add))
                dve.tensor_tensor(zero_from[:, :], total[0:1, :], region[0:1, :], ALU.add).then_inc(zero_from_set, 1)
                step(dve.scalar_tensor_tensor(shift[:, :], starts[:, :], 2.0 * P, region[:, :], ALU.mult, ALU.subtract))
                wide_pairs = [1, PAIRS + 2, NEXP - 1]
                step(dve.tensor_scalar(last_pair[:, :], ends[0:1, NEXP - 1:NEXP], 1.0, None, ALU.subtract))
                step(dve.tensor_scalar(real_pair[:, :], pair_no[:, :], last_pair[:, 0:1], None, ALU.min))
                step(dve.tensor_tensor(shift_steps[:, :], shift[0:1, 1:NEXP], shift[0:1, 0:NEXP - 1], ALU.subtract))
                step(dve.tensor_tensor(reached[:, :, :], real_pair[:, :].rearrange("p (g a) -> p g a", a=1).broadcast_to(wide_pairs),
                                       ends[0:1, 0:NEXP - 1].rearrange("p (a e) -> p a e", a=1).broadcast_to(wide_pairs),
                                       ALU.is_ge))
                step(dve.tensor_tensor(reached_steps[:, :, :], reached[:, :, :], shift_steps[:, :].rearrange(
                    "p (a e) -> p a e", a=1).broadcast_to(wide_pairs), ALU.mult))
                step(dve.tensor_reduce(shifts[:, :], reached_steps[:, :, :], AX_X, ALU.add))
                step(dve.scalar_tensor_tensor(pair_start[:, :], real_pair[:, :], 2.0 * P, shifts[:, :],
                                              ALU.mult, ALU.subtract))
                step(dve.tensor_copy(pair_row[:, :], pair_start[:, :]))
                for n, one_hot in enumerate(all_picks):
                    step(dve.tensor_tensor(all_mark[:, :, :], one_hot[:, :, :], wide(shift[:, :], NT), ALU.mult))
                    step(dve.tensor_reduce(moved[:, :, n], all_mark[:, :, :], AX_X, ALU.add))
                step(dve.tensor_copy(old_place[:, :, :], place[:, :, :]))
                step(dve.tensor_tensor(new_place[:, :, :], old_place[:, :, :], moved[:, :, :], ALU.add))
                dve.wait_ge(squashed_set, 1)
                dve.tensor_scalar(top_w[:, 0, :], squashed[:, :], 0.5, 0.5, ALU.mult, ALU.add)
                dve.tensor_scalar(top_w[:, 1, :], squashed[:, :], -0.5, 0.5, ALU.mult, ALU.add)
                dve.wait_ge(scattered, 16 * 2 * NT)
                step(dve.tensor_copy(place[:, :, :], new_place[:, :, :]))
    return place, top_w, bounds, pair_row, rest_count, zeros, raw


def experts(nc, sb_in, ps_in, sem, turns, settle, ident, x2_rows, sorted_rows, expert_rows, place, top_w,
            bounds, pair_row, rest_count, zeros, raw, w1, w2, out):
    scope = ExitStack()
    with scope:
        sb, ps = sb_in(scope), ps_in(scope)
        FC = FF // P
        w1_t, w2_t = ([[sb(f"w{m}_{b}{part}", [P, k, n], F32R) for part in ("hi", "lo")] for b in (0, 1)]
                      for m, k, n in ((1, C, FF), (2, FC, D)))
        rows = sb("rows", [P, 2, D], F32)
        x_t = [sb(f"x_t{m}", [P, C, 2 * P], F32R) for m in ("hi", "lo")]
        s = sb("s", [P, FC, 2 * P], F32)
        s_t = [sb(f"s_t{m}", [P, FC, 2 * P], F32R) for m in ("hi", "lo")]
        y = sb("y", [P, 2, D], F32)
        place_now = [sb(f"place_now{b}", [P, 4, 2], I32) for b in (0, 1)]
        chosen = [sb(f"chosen{b}", [P, 2, D], F32) for b in range(4)]
        x2 = sb("x2_e", [P, NT, D], F32)
        ps_x = [ps(f"ps_x_e{n}", [P, 512]) for n in (0, 1)]
        ps_h = [ps(f"ps_h{f}", [P, 512]) for f in range(FC)]
        ps_mark = ps("ps_mark_e", [P, 512])
        ps_y = [ps(f"ps_y{n}", [P, 512]) for n in (0, 1)]

        raw_loaded = [sem(f"raw_loaded{b}") for b in (0, 1)]
        weights_split, weights_used, rows_loaded = sem("weights_split"), sem("weights_used"), sem("rows_loaded")
        x_turned, x_hi_set, x_lo_set = sem("x_turned_e"), sem("x_hi_set_e"), sem("x_lo_set_e")
        h_ready, s_set, s_hi_set, s_lo_set = (sem(n) for n in ("h_ready", "s_set", "s_hi_set", "s_lo_set"))
        y_ready, y_stored = sem("y_ready"), sem("y_stored")
        y_set = [sem(f"y_set{n}") for n in (0, 1)]
        rest_zeroed = sem("rest_zeroed")
        place_copied, combined = sem("place_copied"), sem("combined")
        chosen_loaded = [sem(f"chosen_loaded{b}") for b in range(4)]
        x2_loaded, part_set, out_stored = sem("x2_loaded_e"), sem("part_set"), sem("out_stored")

        def pairs_of(eng):
            return eng.value_load(bounds[0:1, NEXP:NEXP + 1], min_val=NT, max_val=PAIRS)

        with nc.Block() as block:

            @block.sync
            def _(sp):
                def load(pair):
                    row = sp.value_load(pair_row[0:1, bass.ds(pair, 1)], min_val=0, max_val=NEXP * REGION - 2 * P)
                    sp.dma_start(rows[:, :, :], sorted_rows[bass.ds(row, 2 * P), :]
                                 .rearrange("(t p) d -> p t d", p=P)).then_inc(rows_loaded, 16)

                load(0)
                count = pairs_of(sp)
                with sp.Fori(count, PAIRS + 1) as pair:
                    sp.dma_start(expert_rows[bass.ds(pair * 2 * P, 2 * P), :].rearrange("(t p) d -> p t d", p=P),
                                 zeros[:, :].rearrange("p (a d) -> p a d", a=1).broadcast_to([P, 2, D])
                                 ).then_inc(rest_zeroed, 16)
                sp.wait_ge(x_turned, 2)
                load(1)


                def load_and_store(g):
                    sp.wait_ge(x_turned, 2 * g + 4)
                    settle(sp)
                    load(g + 2)
                    for n in (0, 1):
                        sp.wait_ge(y_set[n], g + 2)
                    sp.dma_start(expert_rows[bass.ds(g * 2 * P, 2 * P), :].rearrange("(t p) d -> p t d", p=P),
                                 y[:, :, :]).then_inc(y_stored, 16)

                with sp.Fori(0, NT) as g:
                    load_and_store(g)
                    sp.dma_start(x2[:, g, :], x2_rows[bass.ds(g * P, P), :]).then_inc(x2_loaded, 16)
                with sp.Fori(NT, count) as g:
                    load_and_store(g)
                sp.wait_ge(rows_loaded, pairs_of(sp) * 16 + 32)
                settle(sp)

            @block.gpsimd
            def _(pool):
                pool.sem_inc(weights_used, 2)

                def load(e, b):
                    for to, w in zip(raw, (w1, w2)):
                        pool.dma_start(to[b][:, :, :], w[bass.ds(e, 1)].rearrange("e (c p) f -> p (e c) f", p=P)
                                       ).then_inc(raw_loaded[b], 16)

                def split(e, b):
                    if not isinstance(e, int) or e >= 2:
                        pool.wait_ge(raw_loaded[b], (e - b) * 16)
                    pool.wait_ge(weights_used, e + 1)
                    settle(pool)
                    for plain, parts in zip(raw, (w1_t, w2_t)):
                        pool.tensor_copy(parts[b][0][:, :, :], plain[b][:, :, :]).then_inc(weights_split, 1)
                    pool.wait_ge(weights_split, 4 * e + 2)
                    settle(pool)
                    for plain, parts in zip(raw, (w1_t, w2_t)):
                        pool.tensor_tensor(parts[b][1][:, :, :], plain[b][:, :, :], parts[b][0][:, :, :].bitcast(F32),
                                           ALU.subtract).then_inc(weights_split, 1)
                    pool.wait_ge(weights_split, 4 * e + 4)
                    settle(pool)

                pool.wait_ge(weights_split, 4)
                load(2, 0)
                split(1, 1)
                load(3, 1)
                with pool.Fori(1, NEXP // 2 - 1) as j:
                    for b in (0, 1):
                        split(2 * j + b, b)
                        load(2 * j + b + 2, b)
                split(NEXP - 2, 0)
                split(NEXP - 1, 1)
                pool.wait_ge(y_stored, 16 * pairs_of(pool) + 16)
                settle(pool)
                pool.wait_ge(rest_zeroed, pool.value_load(rest_count[0:1, 0:1], min_val=16, max_val=16 * PAIRS))
                settle(pool)

                def copy_places(t, b, tiles=4):
                    pool.wait_ge(combined, t + 1)
                    settle(pool)
                    pool.tensor_copy(place_now[b][:, 0:tiles, :], place[:, bass.ds(t, tiles), :]).then_inc(place_copied, 1)

                def choose(t, n):
                    pool.wait_ge(combined, t + 1)
                    settle(pool)
                    for k in (0, 1):
                        pool.indirect_dma_start(chosen[n % 4][:, k, :], None, expert_rows, bass.IndirectOffsetOnAxis(
                            place_now[n // 4][:, n % 4, k:k + 1], 0)).then_inc(chosen_loaded[n % 4], 16)

                with pool.Fori(0, NT // 8) as j:
                    for b in (0, 1):
                        copy_places(8 * j + 4 * b, b)
                        pool.wait_ge(place_copied, 2 * j + b + 1)
                        for n in range(4):
                            choose(8 * j + 4 * b + n, 4 * b + n)
                copy_places(NT - 1, 0, 1)
                pool.wait_ge(place_copied, NT // 8 * 2 + 1)
                choose(NT - 1, 0)

            @block.tensor
            def _(pe):
                def turn_rows(g):
                    pe.wait_ge(rows_loaded, 16 * g + 16)
                    for n in (0, 1):
                        turn(pe, ps_x[n], rows[:, n, :], ident[:, :]).then_inc(x_turned, 1)

                def pair(g, b):
                    pe.wait_ge(x_lo_set, 2 * g + 2)
                    for f in range(FC):
                        product(pe, ps_h[f][:, 0:2 * P], [w[:, :, f * P:(f + 1) * P] for w in w1_t[b]], x_t
                                ).then_inc(h_ready, 1)
                    turn_rows(g + 1)
                    for n in (0, 1):
                        pe.wait_ge(y_set[n], g + 1)
                        product(pe, ps_y[n][:, :], [part[:, :, n * P:(n + 1) * P] for part in s_t], w2_t[b], chunks=FC,
                                ready=lambda f: pe.wait_ge(s_lo_set, FC * g + f + 1)).then_inc(y_ready, 1)

                turn_rows(0)
                with pe.Fori(0, NEXP // 2) as j:
                    for b in (0, 1):
                        e = 2 * j + b
                        pe.wait_ge(weights_split, 4 * e + 4)
                        settle(pe)
                        first = pe.value_load(bounds[0:1, bass.ds(e, 1)], min_val=0, max_val=PAIRS - 1)
                        end = pe.value_load(bounds[0:1, bass.ds(e + 1, 1)], min_val=1, max_val=PAIRS)
                        with pe.Fori(first, end) as g:
                            pair(g, b)
                        pe.matmul(ps_mark[0:2, 0:2], ident[:, 0:2], ident[:, 0:2], start=True, stop=True
                                  ).then_inc(weights_used, 1)

            @block.scalar
            def _(act):
                act.sem_inc(y_stored, 16)
                for plain, parts in zip(raw, (w1_t, w2_t)):
                    act.copy(parts[0][0][:, :, :], plain[0][:, :, :]).then_inc(weights_split, 1)

                def high_x(g, n):
                    act.wait_ge(x_turned, 2 * g + n + 1)
                    act.copy(x_t[0][:, :, n * P:(n + 1) * P], ps_x[n][:, :].rearrange("p (c r) -> p c r", c=C)
                             ).then_inc(x_hi_set, 1)

                high_x(0, 0)
                high_x(0, 1)
                with act.Fori(0, pairs_of(act)) as g:
                    for f in range(FC):
                        act.wait_ge(h_ready, FC * g + f + 1)
                        act.activation(s[:, f, :], ps_h[f][:, 0:2 * P], ACT.Silu).then_inc(s_set, 1)
                        act.wait_ge(s_set, FC * g + f + 1)
                        act.copy(s_t[0][:, f, :], s[:, f, :]).then_inc(s_hi_set, 1)
                    for n in (0, 1):
                        high_x(g + 1, n)
                    act.wait_ge(y_ready, 2 * g + 1)
                    act.wait_ge(y_stored, 16 * g + 16)
                    act.copy(y[:, 0, :], ps_y[0][:, :]).then_inc(y_set[0], 1)

                def store(t, b, j):
                    act.wait_ge(combined, t + 5)
                    r = rows_of(t)
                    act.dma_start(out[bass.ds(t * P, r), :], x2[0:r, t, :]).then_inc(out_stored, 16)

                node_tiles(act, store)
                act.wait_ge(out_stored, 16 * NT)

            @block.vector
            def _(dve):
                dve.sem_inc(combined, 4)
                dve.sem_inc(y_set[0], 1)
                dve.sem_inc(y_set[1], 1)

                def low_x(g, n):
                    dve.wait_ge(x_hi_set, 2 * g + n + 1)
                    these = slice(n * P, (n + 1) * P)
                    dve.tensor_tensor(x_t[1][:, :, these], ps_x[n][:, :].rearrange("p (c r) -> p c r", c=C),
                                      x_t[0][:, :, these].bitcast(F32), ALU.subtract).then_inc(x_lo_set, 1)

                dve.wait_ge(weights_split, 2)
                for plain, parts in zip(raw, (w1_t, w2_t)):
                    dve.tensor_tensor(parts[0][1][:, :, :], plain[0][:, :, :], parts[0][0][:, :, :].bitcast(F32),
                                      ALU.subtract).then_inc(weights_split, 1)
                low_x(0, 0)
                low_x(0, 1)
                with dve.Fori(0, pairs_of(dve)) as g:
                    for f in range(FC):
                        dve.wait_ge(s_hi_set, FC * g + f + 1)
                        dve.tensor_tensor(s_t[1][:, f, :], s[:, f, :], s_t[0][:, f, :].bitcast(F32), ALU.subtract
                                          ).then_inc(s_lo_set, 1)
                    for n in (0, 1):
                        low_x(g + 1, n)
                    dve.wait_ge(y_ready, 2 * g + 2)
                    dve.wait_ge(y_stored, 16 * g + 16)
                    dve.tensor_scalar(y[:, 1, :], ps_y[1][:, :], 1.0, None, ALU.mult).then_inc(y_set[1], 1)

                def combine(t, b):
                    dve.wait_ge(chosen_loaded[b], (t - b) * 8 + 32)
                    for k, done in ((0, part_set), (1, combined)):
                        if k == 1:
                            dve.wait_ge(part_set, t + 1)
                        dve.scalar_tensor_tensor(x2[:, t, :], chosen[b][:, k, :], top_w[:, k, bass.ds(t, 1)], x2[:, t, :],
                                                 ALU.mult, ALU.add).then_inc(done, 1)

                dve.wait_ge(x2_loaded, 16 * NT)
                with dve.Fori(0, NT // 4) as j:
                    for b in range(4):
                        combine(4 * j + b, b)
                combine(NT - 1, 0)


def build(nc, x, src, dst, w_gnn, b_gnn, w_qkv, w_proj, b_proj, w_gate, w1, w2, out):
    table = nc.dram_tensor("gather_table", [NT * P, 2 * D], F16, kind="Internal").ap()
    q_rows = nc.dram_tensor("q_rows", [NT * P, D], F32, kind="Internal").ap()
    x2_rows = nc.dram_tensor("x2_rows", [NT * P, D], F32, kind="Internal").ap()
    sorted_rows = nc.dram_tensor("sorted_rows", [NEXP * REGION, D], F32, kind="Internal").ap()
    expert_rows = nc.dram_tensor("expert_rows", [(PAIRS + 1) * 2 * P, D], F32, kind="Internal").ap()
    window_rows = nc.dram_tensor("window_rows", [2 * NG], I32, kind="Internal").ap()
    everything = ExitStack()
    with everything:
        def sem(name):
            return everything.enter_context(nc.semaphore(name))

        def sb_in(scope):
            return lambda name, shape, dt: scope.enter_context(nc.sbuf_tensor(name, shape, dt))

        def ps_in(scope):
            return lambda name, shape: scope.enter_context(nc.psum_tensor(name, shape, F32))

        keep = sb_in(everything)
        ident = keep("ident", [P, P], F32)
        ones = keep("ones", [P, P], F32)
        mean = keep("mean", [P, NT], F32)
        rstd = keep("rstd", [P, NT], F32)
        dinv_down = keep("dinv_down", [P, NT], F32)
        real_row = keep("real_row", [P, 1], F32)

        acc_scope = everything.enter_context(ExitStack())
        acc = sb_in(acc_scope)("acc", [P, NT, D], F32)
        x2_stats = sb_in(acc_scope)("x2_stats", [P, NT, 6], F32)
        kv_scope = ExitStack()
        k_sum = sb_in(kv_scope)("k_sum", [P, D], F32)
        v = sb_in(kv_scope)("v", [P, D], F32)
        edge_scope = ExitStack()
        sb = sb_in(edge_scope)
        src_col = sb("src_col", [P, ET], I32)
        dst_col = sb("dst_col", [P, ET], F32)
        windows = sb("windows", [1, 2, NG], I32)
        tile_start = sb("tile_start", [P, NT], F32)
        iota = sb("iota", [P, P], BF16)
        w_t = [sb(f"w_qkv_t{n}", [P, C, 3 * D], F32R) for n in ("hi", "lo")]

        scope = ExitStack()
        with scope:
            sb, ps = sb_in(scope), ps_in(scope)
            edge_rows = [sb(f"{n}_rows", [P, ROWT * P], I32) for n in ("src", "dst")]
            edge_rows_f = [sb(f"{n}_rows_f", [P, ROWT * P], F32) for n in ("src", "dst")]
            w_ends = sb("window_ends", [P, 2, 2], F32)
            w_ends_i = sb("window_ends_i", [P, 2, 2], I32)
            w_tile_i = sb("window_tiles_i", [P, 2, 2], I32)
            w_clamped = sb("window_tiles", [P, 2, 2], I32)
            dst_i = sb("dst_i", [P, ET], I32)
            hi_i = sb("dst_tile_i", [P, ET], I32)
            dst_tile = sb("dst_tile", [P, ET], BF16)
            dst_in_tile = sb("dst_in_tile", [P, ET], BF16)
            number = sb("number", [P, P, BATCH], BF16)
            one_hot_lo = [r[:, :].bitcast(BF16).rearrange("p (n e) -> p n e", e=BATCH) for r in edge_rows]
            one_hot_hi = [sb(f"one_hot_hi{b}", [P, NT, BATCH], BF16) for b in (0, 1)]
            zeros = sb("zeros_b", [P, P], BF16)
            degree = sb("degree", [P, NT], F32)
            dinv_up = sb("dinv_up", [P, NT], F32)
            w_plain = [sb(f"w_plain{b}", [P, C, P], F32) for b in (0, 1)]
            per = NT // XPARTS
            unread = sb("unread", [P, per, D], BF16)
            sums, minus_mean, squares = (sb(n, [P, NT], F32) for n in ("sums", "minus_mean", "squares"))
            others = slice(ACT_PARTS * per, NT)
            stats = sb("stats", [P, NT - ACT_PARTS * per, 6], F32)
            mean_sum, mean_gap, square_sum, gap_square, square_mean = (
                sb(n, [P, NT - ACT_PARTS * per], F32) for n in ("mean_sum", "mean_gap", "square_sum", "gap_square",
                                                                "square_mean"))
            dinv, row_scale, var_eps, minus_half = (
                sb(n, [P, NT], F32) for n in ("dinv", "row_scale", "var_eps", "minus_half"))
            parts = [r[:, :].bitcast(F16).rearrange("p (t a d) -> p t a d", t=2, a=2)
                     for r in edge_rows_f + edge_rows]
            w_rows = [k_sum, v]
            turned = [ps(f"turned{b}", [P, 512]) for b in (0, 1)]
            ps_deg = ps("ps_deg", [P, 512])

            edges_loaded = [sem("src_loaded"), sem("dst_loaded")]
            windows_stored, windows_loaded = sem("windows_stored"), sem("windows_loaded")
            w_loaded = [sem(f"w_loaded{b}") for b in (0, 1)]
            x_loaded = [sem(f"x_loaded{n}") for n in range(ACT_PARTS + 1)]
            tail_zeroed, number_set = sem("tail_zeroed"), sem("number_set")
            edges_padded, consts_set = sem("edges_padded"), sem("consts_set")
            edge_step = sem("edge_step")
            edges_turned = sem("edges_turned")
            edges_copied = sem("edges_copied")
            w_turned, w_copied, w_hi_set, w_lo_set = (sem(n) for n in ("w_turned", "w_copied", "w_hi_set", "w_lo_set"))
            one_hots_built = [sem(f"one_hots_built{b}") for b in (0, 1)]
            one_hots_used = sem("one_hots_used")
            degrees_summed, degree_set, roots_set = sem("degrees_summed"), sem("degree_set"), sem("roots_set")
            moment_step, var_set = sem("moment_step"), sem("var_set")
            stats_set = sem("stats_set")
            summed, means_set, squares_summed = sem("summed"), sem("means_set"), sem("squares_summed")
            acc_set, hi_part_set, lo_part_set = sem("acc_set"), sem("hi_part_set"), sem("lo_part_set")
            parts_stored = [sem(f"parts_stored{b}") for b in range(4)]
            turns = sem("turns")

            def settle(eng):
                eng.sem_inc(turns, 1)

            with nc.Block() as block:

                @block.sync
                def _(sp):
                    sp.wait_ge(edges_padded, 2)
                    for rows, col, loaded in zip(edge_rows, (src, dst), edges_loaded):
                        full = EFULL * ROWT * P
                        sp.dma_start(rows[0:EFULL, :], col[0:full].rearrange("(r e) -> r e", e=ROWT * P)
                                     ).then_inc(loaded, 16)
                        sp.dma_start(rows[EFULL:EFULL + 1, 0:EREST],
                                     col[full:E].rearrange("(r e) -> r e", r=1)).then_inc(loaded, 16)
                    with sp.Fori(0, NWB // 2) as j:
                        for b in (0, 1):
                            sp.wait_ge(w_turned, 2 * j + b + 1)
                            sp.dma_start(w_rows[b][:, :], w_qkv[bass.ds((2 * j + b) * P, P), :]
                                         ).then_inc(w_loaded[b], 16)
                    sp.wait_ge(edge_step, 8)
                    for side in (0, 1):
                        sp.dma_start(window_rows[side * NG:(side + 1) * NG].rearrange("(r g) -> r g", g=2),
                                     w_clamped[0:ER, side, :]).then_inc(windows_stored, 16)
                    sp.wait_ge(windows_stored, 32)
                    sp.dma_start(windows[:, :, :], window_rows.rearrange("(a s g) -> a s g", a=1, s=2)
                                 ).then_inc(windows_loaded, 16)


                    def store_parts(u, tiles, b):
                        sp.wait_ge(lo_part_set, u + 1)
                        sp.dma_start(table[bass.ds(2 * u * P, tiles * P), :].rearrange("(t p) d -> p t d", p=P),
                                     parts[b][:, 0:tiles, :, :].rearrange("p t a d -> p t (a d)")
                                     ).then_inc(parts_stored[b], 16)

                    tile_pairs(sp, store_parts)
                    sp.wait_ge(windows_loaded, 16)
                    for b in range(4):
                        sp.wait_ge(parts_stored[b], 16 * (NT // 8 + 1 + (b == 0)))

                @block.gpsimd
                def _(pool):
                    pool.sem_inc(w_lo_set, 2)
                    pool.memset(edge_rows[0][:, :], 0).then_inc(edges_padded, 1)
                    pool.memset(edge_rows[1][:, :], PAD_DST).then_inc(edges_padded, 1)
                    pool.memset(ones[:, :], 1.0).then_inc(consts_set, 1)
                    pool.memset(zeros[:, :], 0.0).then_inc(consts_set, 1)
                    pool.iota(iota[:, :], [[1, P]], base=0, channel_multiplier=0,
                              allow_small_or_imprecise_dtypes=True).then_inc(consts_set, 1)
                    pool.iota(number[:, :, :], [[1, P], [0, BATCH]], base=0, channel_multiplier=0,
                              allow_small_or_imprecise_dtypes=True).then_inc(number_set, 1)
                    pool.iota(tile_start[:, :], [[P, NT]], base=0, channel_multiplier=0,
                              allow_small_or_imprecise_dtypes=True).then_inc(consts_set, 1)
                    pool.wait_ge(consts_set, 4)
                    pool.affine_select(out=ident[:, :], in_=ones[:, :], compare_op=ALU.is_equal, fill=0.0,
                                       base=0, pattern=[[-1, P]], channel_multiplier=1).then_inc(consts_set, 1)
                    pool.affine_select(out=real_row[:, :], in_=ones[:, 0:1], compare_op=ALU.is_gt, fill=0.0,
                                       base=LAST, pattern=[[0, 1]], channel_multiplier=-1).then_inc(consts_set, 1)
                    pool.memset(minus_half[:, :], -0.5).then_inc(consts_set, 1)
                    pool.wait_ge(consts_set, 7)
                    with pool.Fori(0, NWB // 2) as j:
                        for b in (0, 1):
                            cols = bass.ds((2 * j + b) * P, P)
                            pool.wait_ge(w_hi_set, 2 * j + b + 1)
                            settle(pool)
                            pool.tensor_tensor(w_t[1][:, :, cols], w_plain[b][:, :, :],
                                               w_t[0][:, :, cols].bitcast(F32), ALU.subtract).then_inc(w_lo_set, 1)
                    pool.wait_ge(var_set, 2)
                    pool.tensor_tensor(rstd[:, :], var_eps[:, :], minus_half[:, :], ALU.pow).then_inc(roots_set, 1)
                    pool.wait_ge(degree_set, 1)
                    for these in (slice(0, FIRST), slice(FIRST, NT)):
                        pool.tensor_tensor(dinv[:, these], degree[:, these], minus_half[:, these], ALU.pow
                                           ).then_inc(roots_set, 1)


                @block.tensor
                def _(pe):
                    pe.sem_inc(w_turned, 2)
                    pe.sem_inc(one_hots_used, 2)
                    pe.wait_ge(consts_set, 6)
                    n = 0
                    for k in (0, 1):
                        pe.wait_ge(edge_step, k + 1)
                        for b in range(ROWT):
                            pe.wait_ge(edges_copied, n + 1)
                            pe.transpose(turned[n % 2][:, 0:ER], edge_rows_f[k][0:ER, b * P:(b + 1) * P],
                                         ident[0:ER, 0:ER]).then_inc(edges_turned, 1)
                            n += 1
                    pe.wait_ge(edges_copied, n + 2)
                    pe.matmul(ps_deg[:, 0:NT], zeros[:, :], zeros[:, 0:NT], start=True, stop=False,
                              skip_group_check=True)

                    def count(t, b, j):
                        pe.wait_ge(one_hots_built[b], j + 1)
                        for e in range(BATCH):
                            last = pe.matmul(ps_deg[:, 0:NT], one_hot_lo[b][:, :, e], one_hot_hi[b][:, :, e],
                                             start=False, stop=False, skip_group_check=True)
                        last.then_inc(one_hots_used, 1)

                    some_node_tiles(pe, count, 0, ALONE)
                    with pe.Fori(0, NWB // 2) as j:
                        for b in (0, 1):
                            pe.wait_ge(w_loaded[b], 16 * j + 16)
                            pe.wait_ge(w_copied, 2 * j + b + 1)
                            turn(pe, turned[b], w_rows[b], ident[:, :]).then_inc(w_turned, 1)
                            count(2 * (j + ALONE) + b, b, j + ALONE)
                    some_node_tiles(pe, count, NWB // 2 + ALONE, NT // 2)
                    count(NT - 1, 0, NT // 2)
                    pe.matmul(ps_deg[:, 0:NT], zeros[:, :], zeros[:, 0:NT], start=False, stop=True,
                              skip_group_check=True).then_inc(degrees_summed, 1)

                @block.scalar
                def _(act):
                    for b in range(4):
                        act.sem_inc(parts_stored[b], 16)
                    act.sem_inc(w_copied, 2)
                    act.wait_ge(edges_loaded[1], 32)
                    act.wait_ge(tail_zeroed, 1)
                    for n in range(XPARTS):
                        full = per - (n == XPARTS - 1)
                        act.dma_start(acc[:, n * per:n * per + full, :],
                                     x[n * per * P:(n * per + full) * P, :].rearrange("(t p) d -> p t d", p=P)
                                     ).then_inc(x_loaded[min(n, ACT_PARTS)], 16)
                    act.dma_start(acc[0:LAST, NT - 1, :], x[(NT - 1) * P:N, :]).then_inc(x_loaded[ACT_PARTS], 16)

                    def sum_part(n):
                        these = slice(n * per, (n + 1) * per)
                        act.wait_ge(x_loaded[n], 16)
                        if n:
                            act.wait_ge(squares_summed, n * per)
                        settle(act)
                        with act.Fori(n * per, (n + 1) * per) as t:
                            act.activation(unread[:, t - n * per, :], acc[:, t, :], ACT.Copy, accum_out=sums[:, bass.ds(t, 1)]
                                           ).then_inc(summed, 1)
                        act.wait_ge(summed, (n + 1) * per)
                        act.activation(minus_mean[:, these], sums[:, these], ACT.Copy, scale=-1.0 / D).then_inc(means_set, 1)
                        act.wait_ge(means_set, n + 1)
                        settle(act)
                        with act.Fori(n * per, (n + 1) * per) as t:
                            act.activation(unread[:, t - n * per, :], acc[:, t, :], ACT.Square, bias=minus_mean[:, bass.ds(t, 1)],
                                           accum_out=squares[:, bass.ds(t, 1)]).then_inc(squares_summed, 1)

                    for n in range(BEFORE):
                        sum_part(n)
                    with act.Fori(0, NWB // 2) as j:
                        for b in (0, 1):
                            act.wait_ge(w_turned, 2 * j + b + 3)
                            act.wait_ge(w_lo_set, 2 * j + b + 1)
                            act.copy(w_plain[b][:, :, :].rearrange("p c o -> p (c o)"), turned[b][:, :]
                                     ).then_inc(w_copied, 1)
                            act.wait_ge(w_copied, 2 * j + b + 3)
                            settle(act)
                            act.copy(w_t[0][:, :, bass.ds((2 * j + b) * P, P)], w_plain[b][:, :, :]).then_inc(w_hi_set, 1)
                    for n in range(BEFORE, ACT_PARTS):
                        sum_part(n)

                    def high_part(u, tiles, b):
                        act.wait_ge(acc_set, 2 * u + tiles)
                        act.wait_ge(parts_stored[b], (u - b) * 4 + 16)
                        settle(act)
                        act.copy(parts[b][:, 0:tiles, 0, :], acc[:, bass.ds(2 * u, tiles), :]).then_inc(hi_part_set, 1)

                    tile_pairs(act, high_part)

                @block.vector
                def _(dve):
                    dve.memset(acc[P - DH:P, NT - 1, :], 0.0).then_inc(tail_zeroed, 1)
                    dve.sem_inc(edges_copied, 2)
                    steps = 0

                    def step(ins):
                        nonlocal steps
                        ins.then_inc(edge_step, 1)
                        steps += 1

                    def after_steps():
                        dve.wait_ge(edge_step, steps)

                    for k in (0, 1):
                        dve.wait_ge(edges_loaded[k], 32)
                        step(dve.tensor_copy(edge_rows_f[k][0:ER, :], edge_rows[k][0:ER, :]))
                    after_steps()
                    dst_groups = edge_rows_f[1][0:ER, :].rearrange("r (g e) -> r g e", g=2)
                    step(dve.tensor_reduce(w_ends[0:ER, 0, :], dst_groups, AX_X, ALU.min))
                    step(dve.tensor_reduce(w_ends[0:ER, 1, :], dst_groups, AX_X, ALU.max))
                    after_steps()
                    step(dve.tensor_copy(w_ends_i[0:ER], w_ends[0:ER]))
                    after_steps()
                    step(dve.tensor_single_scalar(w_tile_i[0:ER], w_ends_i[0:ER], 7, ALU.arith_shift_right))
                    after_steps()
                    step(dve.tensor_scalar(w_clamped[0:ER, 0, :], w_tile_i[0:ER, 0, :], NT - 1, None, ALU.min))
                    step(dve.tensor_scalar(w_clamped[0:ER, 1, :], w_tile_i[0:ER, 1, :], NT - 1, 1,
                                           ALU.min, ALU.add))
                    assert steps == 8
                    n = 0
                    for k in (0, 1):
                        col = (src_col, dst_col)[k]
                        for b in range(ROWT):
                            dve.wait_ge(edges_turned, n + 1)
                            dve.tensor_copy(col[:, b:ET:ROWT], turned[n % 2][:, 0:ER]).then_inc(edges_copied, 1)
                            n += 1
                    dve.wait_ge(edges_copied, n + 2)
                    step(dve.tensor_copy(dst_i[:, :], dst_col[:, :]))
                    after_steps()
                    step(dve.tensor_single_scalar(hi_i[:, :], dst_i[:, :], 7, ALU.arith_shift_right))
                    after_steps()
                    step(dve.tensor_copy(dst_tile[:, :], hi_i[:, :]))
                    after_steps()
                    step(dve.scalar_tensor_tensor(dst_in_tile[:, :], dst_tile[:, :], -float(P), dst_col[:, :],
                                                  ALU.mult, ALU.add))
                    after_steps()

                    dve.wait_ge(number_set, 1)

                    def one_hots(t, b, j):
                        dve.wait_ge(one_hots_used, t + 1)
                        for to, table_, n in ((one_hot_lo[b], dst_in_tile, P), (one_hot_hi[b][:, :, :], dst_tile, NT)):
                            these = table_[:, bass.ds(t * BATCH, BATCH)].rearrange("p (a e) -> p a e", a=1)
                            last = dve.tensor_tensor(to, number[:, 0:n, :], these.broadcast_to([P, n, BATCH]),
                                                     ALU.is_equal)
                        last.then_inc(one_hots_built[b], 1)

                    some_node_tiles(dve, one_hots, 0, EARLY)

                    moments = 0

                    def moment(ins):
                        nonlocal moments
                        ins.then_inc(moment_step, 1)
                        moments += 1

                    def after():
                        dve.wait_ge(moment_step, moments)

                    dve.wait_ge(x_loaded[ACT_PARTS], 16 * (XPARTS - ACT_PARTS + 1))
                    settle(dve)
                    with dve.Fori(0, NT - ACT_PARTS * per) as t:
                        dve.bn_stats(stats[:, t, :], acc[:, t + ACT_PARTS * per, :]).then_inc(stats_set, 1)
                    dve.wait_ge(stats_set, NT - ACT_PARTS * per)
                    even, odd = stats[:, :, 1], stats[:, :, 4]
                    moment(dve.tensor_tensor(mean_sum[:, :], even, odd, ALU.add))
                    moment(dve.tensor_tensor(mean_gap[:, :], even, odd, ALU.subtract))
                    moment(dve.tensor_tensor(square_sum[:, :], stats[:, :, 2], stats[:, :, 5], ALU.add))
                    after()
                    moment(dve.tensor_scalar(mean[:, others], mean_sum[:, :], 0.5, None, ALU.mult))
                    moment(dve.scalar_tensor_tensor(gap_square[:, :], mean_gap[:, :], 0.25, mean_gap[:, :],
                                                    ALU.mult, ALU.mult))
                    moment(dve.tensor_scalar(square_mean[:, :], square_sum[:, :], 1.0 / D, LN_EPS, ALU.mult, ALU.add))
                    after()
                    dve.tensor_tensor(var_eps[:, others], square_mean[:, :], gap_square[:, :], ALU.add).then_inc(var_set, 1)
                    dve.wait_ge(squares_summed, ACT_PARTS * per)
                    these = slice(0, ACT_PARTS * per)
                    moment(dve.tensor_scalar(mean[:, these], minus_mean[:, these], -1.0, None, ALU.mult))
                    dve.tensor_scalar(var_eps[:, these], squares[:, these], 1.0 / D, LN_EPS, ALU.mult, ALU.add
                                      ).then_inc(var_set, 1)

                    some_node_tiles(dve, one_hots, EARLY, NT // 2)
                    one_hots(NT - 1, 0, NT // 2)

                    dve.wait_ge(degrees_summed, 1)
                    dve.tensor_scalar(degree[:, :], ps_deg[:, 0:NT], 1.0, None, ALU.add).then_inc(degree_set, 1)
                    dve.wait_ge(roots_set, 1)
                    moment(dve.tensor_tensor(rstd[:, NT - 1:NT], rstd[:, NT - 1:NT], real_row[:, :], ALU.mult))

                    def scales(these, roots):
                        dve.wait_ge(roots_set, roots)
                        moment(dve.tensor_scalar(dinv_up[:, these], dinv[:, these], TABLE_SCALE, None, ALU.mult))
                        moment(dve.tensor_scalar(dinv_down[:, these], dinv[:, these], 1.0 / TABLE_SCALE, None, ALU.mult))
                        after()
                        moment(dve.tensor_tensor(row_scale[:, these], rstd[:, these], dinv_up[:, these], ALU.mult))
                        after()

                    def scaled_rows(u, tiles, b):
                        for n in range(tiles):
                            t = 2 * u + n
                            dve.tensor_scalar(acc[:, t, :], acc[:, t, :], mean[:, bass.ds(t, 1)],
                                              row_scale[:, bass.ds(t, 1)], ALU.subtract, ALU.mult).then_inc(acc_set, 1)

                    def low_part(u, tiles, b):
                        dve.wait_ge(hi_part_set, u + 1)
                        dve.tensor_tensor(parts[b][:, 0:tiles, 1, :], acc[:, bass.ds(2 * u, tiles), :],
                                          parts[b][:, 0:tiles, 0, :], ALU.subtract).then_inc(lo_part_set, 1)

                    scales(slice(0, FIRST), 2)
                    scaled_rows(0, 2, 0)
                    alone = FIRST // 2 - 1
                    for u in range(alone):
                        scaled_rows(u + 1, 2, u + 1)
                        low_part(u, 2, u)
                    scales(slice(FIRST, NT), 3)
                    turns_of_4 = (NT // 2 - 1 - alone) // 4
                    with dve.Fori(0, turns_of_4) as j:
                        for u in range(alone, alone + 4):
                            scaled_rows(4 * j + u + 1, 2, (u + 1) % 4)
                            low_part(4 * j + u, 2, u % 4)
                    for u in range(alone + 4 * turns_of_4, NT // 2):
                        scaled_rows(u + 1, 2 if u + 1 < NT // 2 else 1, (u + 1) % 4)
                        low_part(u, 2, u % 4)
                    low_part(NT // 2, 1, 0)

        scope = ExitStack()
        with scope:
            sb, ps = sb_in(scope), ps_in(scope)
            ring = sb("gathered", [P, GPT, GE, 2, D], F16)
            src_now = [sb(f"src_now{b}", [P, GPT * GE], I32) for b in (0, 1)]
            one_hot = sb("one_hot", [P, 2, GE, P], F16)
            x_rows = [sb(f"x_rows_b{b}", [P, D], F32) for b in (0, 1)]
            xn_t = [sb(f"xn_t{n}", [P, C, P], F32R) for n in ("hi", "lo")]
            q = sb("q", [P, D], F32)
            k = sb("k", [P, D], F32)
            zeros = sb("zeros_b2", [P, P], BF16)
            ps_turn = ps("ps_turn", [P, 512])
            ps_qv, ps_k, ps_kv = ps("ps_qv", [P, 512]), ps("ps_k", [P, 512]), ps("ps_kv", [P, 512])
            ps_sum = ps("ps_sum", [P, 2, 512])
            ps_mark = ps("ps_mark", [P, 512])

            landed = [sem(f"group_landed{g}") for g in range(GPT)]
            src_copied, group_summed = sem("src_copied"), sem("group_summed")
            one_hot_built, pair_summed, pair_added = sem("one_hot_built"), sem("pair_summed"), sem("pair_added")
            x_loaded = [sem(f"x_loaded_b{b}") for b in (0, 1)]
            xn_set, xn_turned, xn_hi_set, xn_lo_set = sem("xn_set"), sem("xn_turned"), sem("xn_hi_set"), sem("xn_lo_set")
            q_ready, k_ready, v_ready = sem("q_ready"), sem("k_ready"), sem("v_ready")
            q_set, k_set, v_set, q_stored = sem("q_set"), sem("k_set"), sem("v_set"), sem("q_stored")
            k_added, kv_summed, zeros_set = sem("k_added"), sem("kv_summed"), sem("zeros_set")

            with nc.Block() as block:

                @block.sync
                def _(sp):
                    def load_x(t, b, j):
                        sp.wait_ge(xn_turned, t + 1)
                        r = rows_of(t)
                        sp.dma_start(x_rows[b][0:r, :], x[bass.ds(t * P, r), :]).then_inc(x_loaded[b], 16)

                    node_tiles(sp, load_x)

                @block.gpsimd
                def _(pool):
                    def gather(t, b, j):
                        pool.wait_ge(group_summed, GPT * t + 1)
                        settle(pool)
                        pool.tensor_copy(src_now[b][:, :], src_col[:, bass.ds(GPT * GE * t, GPT * GE)]
                                         ).then_inc(src_copied, 1)
                        pool.wait_ge(src_copied, t + 1)
                        for g in range(GPT):
                            pool.wait_ge(group_summed, GPT * t + g + 1)
                            settle(pool)
                            for e in range(GE):
                                pool.indirect_dma_start(
                                    ring[:, g, e, :, :].rearrange("p a d -> p (a d)"), None, table,
                                    bass.IndirectOffsetOnAxis(src_now[b][:, g * GE + e:g * GE + e + 1], 0)
                                ).then_inc(landed[g], 16)

                    node_tiles(pool, gather)

                @block.tensor
                def _(pe):
                    pe.sem_inc(group_summed, GPT)
                    pe.sem_inc(xn_turned, 2)
                    pe.wait_ge(zeros_set, 2)
                    pe.matmul(ps_kv[:, :], zeros[:, :], one_hot[:, 0, :, :].bitcast(BF16).rearrange("p e n -> p (e n)"),
                              start=True, stop=False, skip_group_check=True)
                    pe.matmul(ps_sum[:, 0, :], zeros[:, :], one_hot[:, 0, :, :].bitcast(BF16).rearrange("p e n -> p (e n)"),
                              start=True, stop=True).then_inc(pair_summed, 1)
                    pair = pe.alloc_register("pair")
                    pe.reg_mov(pair, 1)

                    def sum_group(t, g):
                        at = GPT * t + g
                        first = pe.value_load(windows[0:1, 0, bass.ds(at, 1)], min_val=0, max_val=NT - 1)
                        end = pe.value_load(windows[0:1, 1, bass.ds(at, 1)], min_val=1, max_val=NT)
                        pe.wait_ge(landed[g], 16 * GE * t + 16 * GE)
                        settle(pe)
                        with pe.Fori(first, end):
                            now = pe.snap(pair, min_val=1, max_val=NG * NT)
                            half = pe.snap(now % 2)
                            pe.wait_ge(one_hot_built, now)
                            settle(pe)
                            for e in range(GE):
                                for part in (0, 1):
                                    last = pe.matmul(ps_sum[:, half, :], one_hot[:, half, e, :], ring[:, g, e, part, :],
                                                     start=e == 0 and part == 0, stop=e == GE - 1 and part == 1)
                            last.then_inc(pair_summed, 1)
                            pe.reg_add(pair, now, 1)
                        pe.matmul(ps_mark[0:2, 0:2], zeros[:, 0:2], zeros[:, 0:2], start=True, stop=True
                                  ).then_inc(group_summed, 1)

                    def tile(t, b, j):
                        pe.wait_ge(xn_set, t + 1)
                        turn(pe, ps_turn, x_rows[b], ident[:, :]).then_inc(xn_turned, 1)
                        sum_group(t, 0)
                        pe.wait_ge(xn_lo_set, t + 1)
                        product(pe, ps_qv[:, :], xn_t, [w[:, :, 0:D] for w in w_t]).then_inc(q_ready, 1)
                        sum_group(t, 1)
                        product(pe, ps_k[:, :], xn_t, [w[:, :, D:2 * D] for w in w_t]).then_inc(k_ready, 1)
                        sum_group(t, 2)
                        pe.wait_ge(q_set, t + 1)
                        product(pe, ps_qv[:, :], xn_t, [w[:, :, 2 * D:3 * D] for w in w_t]).then_inc(v_ready, 1)
                        sum_group(t, 3)
                        pe.wait_ge(k_set, t + 1)
                        pe.wait_ge(v_set, t + 1)
                        for c in range(C):
                            cols = slice(c * P, (c + 1) * P)
                            last = pe.matmul(ps_kv[:, cols], v[:, cols], k[:, cols], start=False, stop=False,
                                             skip_group_check=True)
                        last.then_inc(kv_summed, 1)

                    node_tiles(pe, tile)
                    pe.matmul(ps_kv[:, :], zeros[:, :], one_hot[:, 0, :, :].bitcast(BF16).rearrange("p e n -> p (e n)"),
                              start=False, stop=True, skip_group_check=True).then_inc(kv_summed, 1)

                @block.scalar
                def _(act):
                    act.sem_inc(q_stored, 16)

                    def tile(t, b, j):
                        act.wait_ge(xn_turned, t + 3)
                        act.copy(xn_t[0][:, :, :].rearrange("p c n -> p (c n)"), ps_turn[:, :]).then_inc(xn_hi_set, 1)
                        act.wait_ge(q_ready, t + 1)
                        act.wait_ge(q_stored, 16 * t + 16)
                        act.activation(q[:, :], ps_qv[:, :], ACT.Relu).then_inc(q_set, 1)
                        act.wait_ge(q_set, t + 1)
                        act.dma_start(q_rows[bass.ds(t * P, P), :], q[:, :]).then_inc(q_stored, 16)
                        act.wait_ge(k_ready, t + 1)
                        act.wait_ge(k_added, t + 1)
                        act.activation(k[:, :], ps_k[:, :], ACT.Relu).then_inc(k_set, 1)
                        act.wait_ge(v_ready, t + 1)
                        act.copy(v[:, :], ps_qv[:, :]).then_inc(v_set, 1)

                    node_tiles(act, tile)
                    act.wait_ge(q_stored, 16 * NT + 16)

                @block.vector
                def _(dve):
                    dve.memset(zeros[:, :], 0.0).then_inc(zeros_set, 1)
                    dve.memset(one_hot[:, 0, :, :], 0.0).then_inc(zeros_set, 1)
                    dve.memset(k_sum[:, :], 0.0).then_inc(k_added, 1)
                    dve.sem_inc(pair_added, 1)
                    pair, window_before = dve.alloc_register("pair"), dve.alloc_register("window_before")
                    dve.reg_mov(pair, 1)
                    dve.reg_mov(window_before, 0)

                    def add_pair(before, window):
                        dve.wait_ge(pair_summed, before + 1)
                        dve.wait_ge(pair_added, before + 1)
                        dve.tensor_tensor(acc[:, window, :], acc[:, window, :], ps_sum[:, before % 2, :], ALU.add
                                          ).then_inc(pair_added, 1)

                    def sum_group(t, g):
                        at = GPT * t + g
                        first = dve.value_load(windows[0:1, 0, bass.ds(at, 1)], min_val=0, max_val=NT - 1)
                        end = dve.value_load(windows[0:1, 1, bass.ds(at, 1)], min_val=1, max_val=NT)
                        with dve.Fori(first, end) as window:
                            now = dve.snap(pair, min_val=1, max_val=NG * NT)
                            half = dve.snap(now % 2)
                            start = tile_start[:, bass.ds(window, 1)]
                            for e in range(GE):
                                last = dve.tensor_scalar(one_hot[:, half, e, :], iota[:, :], start,
                                                         dst_col[:, bass.ds(at * GE + e, 1)], ALU.add, ALU.is_equal)
                            last.then_inc(one_hot_built, 1)
                            add_pair(now - 1, dve.snap(window_before, min_val=0, max_val=NT - 1))
                            dve.reg_add(pair, now, 1)
                            dve.reg_mov(window_before, window)

                    def normalise(t, b):
                        dve.wait_ge(x_loaded[b], (t - b) * 8 + 16)
                        dve.tensor_scalar(x_rows[b][:, :], x_rows[b][:, :], mean[:, bass.ds(t, 1)],
                                          rstd[:, bass.ds(t, 1)], ALU.subtract, ALU.mult).then_inc(xn_set, 1)

                    def tile(t, b, j):
                        sum_group(t, 0)
                        dve.wait_ge(xn_hi_set, t + 1)
                        dve.tensor_tensor(xn_t[1][:, :, :], ps_turn[:, :].rearrange("p (c n) -> p c n", c=C),
                                          xn_t[0][:, :, :].bitcast(F32), ALU.subtract).then_inc(xn_lo_set, 1)
                        for g in range(1, GPT):
                            sum_group(t, g)
                        dve.wait_ge(k_set, t + 1)
                        dve.wait_ge(k_added, t + 1)
                        dve.tensor_tensor(k_sum[:, :], k_sum[:, :], k[:, :], ALU.add).then_inc(k_added, 1)
                        if rows_of(t) == P:
                            normalise(t + 1, 1 - b)

                    normalise(0, 0)
                    node_tiles(dve, tile)
                    dve.drain()
                    now = dve.snap(pair, min_val=1, max_val=NG * NT + 1)
                    add_pair(now - 1, dve.snap(window_before, min_val=0, max_val=NT - 1))
                    dve.wait_ge(kv_summed, NT + 1)
                    dve.tensor_copy(v[:, :], ps_kv[:, :])

        edge_scope.close()
        mix(nc, sb_in, ps_in, sem, turns, settle, acc, x2_stats, k_sum, v, ident, ones, dinv_down, x, q_rows, x2_rows,
            w_gnn, b_gnn, w_proj, b_proj)
        kv_scope.close()
        def right(name, shape, dt):
            return everything.enter_context(nc.sbuf_tensor(name, shape, dt, side="right"))

        routing = route(nc, sb_in, right, ps_in, sem, turns, settle, acc, x2_stats, ident, w_gate, w1, w2,
                        sorted_rows)
        acc_scope.close()
        experts(nc, sb_in, ps_in, sem, turns, settle, ident, x2_rows, sorted_rows, expert_rows, *routing, w1, w2, out)


_INS = ['x', 'src', 'dst', 'L0_gnn_W', 'L0_gnn_b', 'L0_mix_qkv_weight', 'L0_mix_proj_weight',
        'L0_mix_proj_bias', 'L0_ffn_Wg', 'L0_ffn_W1', 'L0_ffn_W2']


def kernel(**inputs):
    import numpy as _np
    import concourse.bacc as _bacc
    from concourse import mybir as _mybir
    from concourse.bass_utils import run_bass_kernel_spmd as _run

    nc = _bacc.Bacc("TRN2", target_bir_lowering=False, num_devices=1)
    arrays, args = {}, []
    for name in _INS:
        a = _np.ascontiguousarray(inputs[name])
        arrays[f"in_{name}"] = a
        args.append(nc.dram_tensor(f"in_{name}", a.shape, _mybir.dt.from_np(a.dtype), kind="ExternalInput").ap())
    args.append(nc.dram_tensor("out_0", (N, D), _mybir.dt.float32, kind="ExternalOutput").ap())
    build(nc, *args)
    r = _run(nc, [arrays], core_ids=[0])
    return r.results[0]["out_0"]
```
